# Optimizing a Trainium2 kernel written in Bass

```python
import numpy as np
import jax
import jax.numpy as jnp

def _softmax(x, axis=-1):
    return jax.nn.softmax(x, axis=axis)

def _gelu(x):
    return jax.nn.gelu(x, approximate=True)

def _silu(x):
    return jax.nn.silu(x)

def _sigmoid(x):
    return jax.nn.sigmoid(x)

def _layernorm(x, axis=-1, eps=1e-05):
    m = jnp.mean(x, axis=axis, keepdims=True)
    v = jnp.var(x, axis=axis, keepdims=True)
    return (x - m) / jnp.sqrt(v + eps)

def _scatter_add(tgt, idx, src, axis=0):
    return tgt.at[idx].add(src)

def _segment_sum(src, seg, n):
    return jax.ops.segment_sum(src, seg, n)
kernel_name = 'mk_flamingo_gated_d4_seqx_r4_a9864a'

def setup_inputs(seed: int=0):
    np.random.seed(seed)
    _w = jnp.asarray

    def _rec_inputs():
        import jax
        import jax.numpy as jnp
        _rk = jax.random.key(seed)
        x = -9.806e-05 + 1 * jax.random.normal(jax.random.fold_in(_rk, 1), (2, 1024, 256), jnp.float32)
        _lenS = 1024 - jax.random.randint(jax.random.fold_in(_rk, 7), (2,), 0, max(1, 1024 // 4) + 1, jnp.int32)
        _lenS2 = 154 - jax.random.randint(jax.random.fold_in(_rk, 8), (2,), 0, max(1, 154 // 4) + 1, jnp.int32)
        _ctx_1024P = jax.random.normal(jax.random.fold_in(_rk, 11), (2, 16, 256), jnp.float32)
        _ctx_1024c = jax.random.dirichlet(jax.random.fold_in(_rk, 511), 0.3 * jnp.ones((16,), jnp.float32), (2, 154))
        _ctx_1024t = jnp.einsum('bsk,bkd->bsd', _ctx_1024c, _ctx_1024P)
        _ctx_1024t = _ctx_1024t * jax.lax.rsqrt(jnp.mean(jnp.square(_ctx_1024t)) + 1e-12) * 0.953939
        ctx_1024 = -1.52775e-05 + 0.999936 * (_ctx_1024t + 0.3 * jax.random.normal(jax.random.fold_in(_rk, 611), (2, 154, 256), jnp.float32))
        _g = jax.random.normal(jax.random.fold_in(_rk, 9001), (2, 4), jnp.float32)
        _g = jnp.sign(_g) * jnp.maximum(jnp.abs(_g), 1.0) + (_g == 0) * 1.0
        g_xattn = _g[0]
        g_ffn = _g[1]
        return (x, ctx_1024, g_xattn, g_ffn)
    x, ctx_1024, g_xattn, g_ffn = _rec_inputs()

    def _L0_xattn_setup():
        import jax, jax.numpy as jnp
        import numpy as np
        D = 256
        NUM_ITERS = 3
        EPS = 1e-06
        SCALE = D ** (-0.5)

        def rmsnorm(x, w, eps=EPS):
            return x * jax.lax.rsqrt(jnp.mean(x * x, axis=-1, keepdims=True) + eps) * w

        def gru_cell(x, h, wih, whh, bih, bhh):
            gx = x @ wih.T + bih
            gh = h @ whh.T + bhh
            xr, xz, xn = jnp.split(gx, 3, axis=-1)
            hr, hz, hn = jnp.split(gh, 3, axis=-1)
            r = jax.nn.sigmoid(xr + hr)
            z = jax.nn.sigmoid(xz + hz)
            n = jnp.tanh(xn + r * hn)
            return (1.0 - z) * n + z * h
        key = jax.random.key(seed)
        ks = jax.random.split(key, 8)
        B, K, M, d = (8, 64, 1024, D)
        w_std = d ** (-0.5)
        return {'slots': jax.random.normal(ks[0], (B, K, d), jnp.float32), 'P': jax.random.normal(ks[1], (B, M, d), jnp.float32), 'Wq': jax.random.normal(ks[2], (d, d), jnp.float32) * w_std, 'Wk': jax.random.normal(ks[3], (d, d), jnp.float32) * w_std, 'Wv': jax.random.normal(ks[4], (d, d), jnp.float32) * w_std, 'gru_wih': jax.random.normal(ks[5], (3 * d, d), jnp.float32) * w_std, 'gru_whh': jax.random.normal(ks[6], (3 * d, d), jnp.float32) * w_std, 'gru_bih': jnp.zeros((3 * d,), jnp.float32), 'gru_bhh': jnp.zeros((3 * d,), jnp.float32), 'slot_norm_w': jnp.ones((d,), jnp.float32), 'input_norm_w': jnp.ones((d,), jnp.float32)}
    _L0_xattn_all = _L0_xattn_setup()
    _L0_xattn_in = {k: v for k, v in _L0_xattn_all.items() if k in ('Wq', 'Wk', 'Wv', 'gru_wih', 'gru_whh', 'gru_bih', 'gru_bhh', 'slot_norm_w', 'input_norm_w')}
    del _L0_xattn_all

    def _L0_ffn_setup():
        import jax, jax.numpy as jnp
        import numpy as np
        IN_F = 256
        OUT_F = 256
        B, S = (8, 1024)

        def _pack_ternary(tern):
            enc = (tern + 1.0).astype(jnp.int32).reshape(-1)
            return (enc[0::4] | enc[1::4] << 2 | enc[2::4] << 4 | enc[3::4] << 6).astype(jnp.int32)
        key = jax.random.key(seed)
        kx, kw = jax.random.split(key)
        x = jax.random.normal(kx, (B, S, IN_F), dtype=jnp.float32)
        w = jax.random.normal(kw, (OUT_F, IN_F), dtype=jnp.float32) * 0.02
        scale = jnp.maximum(jnp.mean(jnp.abs(w)), 1e-05)
        wn = w / scale
        tern = jnp.sign(wn) * (jnp.abs(wn) > 0.5).astype(jnp.float32)
        packed = _pack_ternary(tern)
        bias = jnp.zeros((OUT_F,), dtype=jnp.float32)
        return {'x': x, 'packed_weight': packed, 'weight_scale': scale.reshape(1), 'bias': bias}
    _L0_ffn_all = _L0_ffn_setup()
    _L0_ffn_in = {k: v for k, v in _L0_ffn_all.items() if k in ('packed_weight', 'weight_scale', 'bias')}
    del _L0_ffn_all

    def _L1_xattn_setup():
        import jax, jax.numpy as jnp
        import numpy as np
        D_MODEL = 256
        NUM_HEADS = 16
        HEAD_DIM = D_MODEL // NUM_HEADS

        def _split_heads(x, B):
            return x.reshape(B, -1, NUM_HEADS, HEAD_DIM).transpose(0, 2, 1, 3)
        key = jax.random.key(seed)
        ks = jax.random.split(key, 11)
        B, S = (2, 512)
        s = 1.0 / np.sqrt(D_MODEL)
        inp = {'q': jax.random.normal(ks[0], (B, S, D_MODEL), jnp.float32), 'k': jax.random.normal(ks[1], (B, S, D_MODEL), jnp.float32), 'v': jax.random.normal(ks[2], (B, S, D_MODEL), jnp.float32), 'wq': jax.random.normal(ks[3], (D_MODEL, D_MODEL), jnp.float32) * s, 'bq': jnp.zeros((D_MODEL,), jnp.float32), 'wk': jax.random.normal(ks[4], (D_MODEL, D_MODEL), jnp.float32) * s, 'bk': jnp.zeros((D_MODEL,), jnp.float32), 'wv': jax.random.normal(ks[5], (D_MODEL, D_MODEL), jnp.float32) * s, 'bv': jnp.zeros((D_MODEL,), jnp.float32), 'wo': jax.random.normal(ks[6], (D_MODEL, D_MODEL), jnp.float32) * s, 'bo': jnp.zeros((D_MODEL,), jnp.float32)}
        return inp
    _L1_xattn_all = _L1_xattn_setup()
    _L1_xattn_in = {k: v for k, v in _L1_xattn_all.items() if k in ('wq', 'bq', 'wk', 'bk', 'wv', 'bv', 'wo', 'bo')}
    del _L1_xattn_all

    def _L1_ffn_setup():
        import jax, jax.numpy as jnp
        import numpy as np
        D_MODEL = 256
        key = jax.random.key(seed)
        k_x, k_w, k_a1, k_a2 = jax.random.split(key, 4)
        x = jax.random.normal(k_x, (4, 512, D_MODEL), dtype=jnp.float32)
        weight = jax.random.normal(k_w, (D_MODEL, D_MODEL), dtype=jnp.float32) * 0.02
        aux_weight1 = jax.random.normal(k_a1, (D_MODEL, D_MODEL), dtype=jnp.float32) * 0.02
        aux_weight2 = jax.random.normal(k_a2, (D_MODEL, D_MODEL), dtype=jnp.float32) * 0.02
        bias = jnp.zeros((D_MODEL,), dtype=jnp.float32)
        return {'x': x, 'weight': weight, 'aux_weight1': aux_weight1, 'aux_weight2': aux_weight2, 'bias': bias}
    _L1_ffn_all = _L1_ffn_setup()
    _L1_ffn_in = {k: v for k, v in _L1_ffn_all.items() if k in ('weight', 'aux_weight1', 'aux_weight2', 'bias')}
    del _L1_ffn_all

    def _L2_xattn_setup():
        import jax, jax.numpy as jnp
        import numpy as np
        DIM = 256
        N_HEADS = 16
        HEAD_DIM = DIM // N_HEADS
        B, N, M = (2, 512, 512)
        key = jax.random.key(seed)
        ks = jax.random.split(key, 10)
        s = 1.0 / np.sqrt(DIM)
        return {'x1': jax.random.normal(ks[0], (B, N, DIM), dtype=jnp.float32), 'x2': jax.random.normal(ks[1], (B, M, DIM), dtype=jnp.float32), 'Wq': jax.random.normal(ks[2], (DIM, DIM), dtype=jnp.float32) * s, 'bq': jnp.zeros((DIM,), dtype=jnp.float32), 'Wk': jax.random.normal(ks[3], (DIM, DIM), dtype=jnp.float32) * s, 'bk': jnp.zeros((DIM,), dtype=jnp.float32), 'Wv': jax.random.normal(ks[4], (DIM, DIM), dtype=jnp.float32) * s, 'bv': jnp.zeros((DIM,), dtype=jnp.float32), 'Wo': jax.random.normal(ks[5], (DIM, DIM), dtype=jnp.float32) * s, 'bo': jnp.zeros((DIM,), dtype=jnp.float32)}
    _L2_xattn_all = _L2_xattn_setup()
    _L2_xattn_in = {k: v for k, v in _L2_xattn_all.items() if k in ('Wq', 'bq', 'Wk', 'bk', 'Wv', 'bv', 'Wo', 'bo')}
    del _L2_xattn_all

    def _L2_ffn_setup():
        import jax, jax.numpy as jnp
        import numpy as np
        D_MODEL, D_FF, N_EXP = (256, 1024, 8)
        key = jax.random.key(seed)
        ks = jax.random.split(key, 8)
        s = lambda fan_in: 1.0 / np.sqrt(fan_in)
        x = jax.random.normal(ks[0], (4, 512, D_MODEL), dtype=jnp.float32)
        Wr = jax.random.uniform(ks[1], (N_EXP, D_MODEL), jnp.float32, -s(D_MODEL), s(D_MODEL))
        br = jax.random.uniform(ks[2], (N_EXP,), jnp.float32, -s(D_MODEL), s(D_MODEL))
        W1 = jax.random.uniform(ks[3], (N_EXP, D_FF, D_MODEL), jnp.float32, -s(D_MODEL), s(D_MODEL))
        b1 = jax.random.uniform(ks[4], (N_EXP, D_FF), jnp.float32, -s(D_MODEL), s(D_MODEL))
        W2 = jax.random.uniform(ks[5], (N_EXP, D_MODEL, D_FF), jnp.float32, -s(D_FF), s(D_FF))
        b2 = jax.random.uniform(ks[6], (N_EXP, D_MODEL), jnp.float32, -s(D_FF), s(D_FF))
        return {'x': x, 'Wr': Wr, 'br': br, 'W1': W1, 'b1': b1, 'W2': W2, 'b2': b2}
    _L2_ffn_all = _L2_ffn_setup()
    _L2_ffn_in = {k: v for k, v in _L2_ffn_all.items() if k in ('Wr', 'br', 'W1', 'b1', 'W2', 'b2')}
    del _L2_ffn_all

    def _L3_xattn_setup():
        import jax, jax.numpy as jnp
        import numpy as np
        MAX_BITS = 256.0

        def _quantize_kernel(kern):
            qmin = jnp.minimum(jnp.float32(10000000000.0), jnp.min(kern))
            qmax = jnp.maximum(jnp.float32(-10000000000.0), jnp.max(kern))
            s = 2.0 * jnp.maximum(jnp.abs(qmin), jnp.abs(qmax)) / MAX_BITS
            return jnp.round(kern / s) * s
        key = jax.random.key(seed)
        ks = jax.random.split(key, 9)
        B, S, D_IN, D_MODEL = (4, 512, 256, 256)
        sc = 0.02
        return {'q': jax.random.normal(ks[0], (B, S, D_IN), jnp.float32), 'k': jax.random.normal(ks[1], (B, S, D_IN), jnp.float32), 'v': jax.random.normal(ks[2], (B, S, D_IN), jnp.float32), 'Wq': jax.random.normal(ks[3], (D_IN, D_MODEL), jnp.float32) * sc, 'bq': jax.random.normal(ks[4], (D_MODEL,), jnp.float32) * sc, 'Wk': jax.random.normal(ks[5], (D_IN, D_MODEL), jnp.float32) * sc, 'bk': jax.random.normal(ks[6], (D_MODEL,), jnp.float32) * sc, 'Wv': jax.random.normal(ks[7], (D_IN, D_MODEL), jnp.float32) * sc, 'bv': jax.random.normal(ks[8], (D_MODEL,), jnp.float32) * sc}
    _L3_xattn_all = _L3_xattn_setup()
    _L3_xattn_in = {k: v for k, v in _L3_xattn_all.items() if k in ('Wq', 'bq', 'Wk', 'bk', 'Wv', 'bv')}
    del _L3_xattn_all

    def _L3_ffn_setup():
        import jax, jax.numpy as jnp
        import numpy as np
        TOPK = 4
        key = jax.random.key(seed)
        ks = jax.random.split(key, 9)
        B, T, D = (4, 512, 256)
        E, H = (32, 128)
        HS = H * TOPK
        s = lambda k, shape, fan: jax.random.normal(k, shape, dtype=jnp.float32) / np.sqrt(fan)
        return {'x': jax.random.normal(ks[0], (B, T, D), dtype=jnp.float32), 'router_w': s(ks[1], (E, D), D), 'router_bias': jnp.zeros((E,), dtype=jnp.float32), 'gate_w': s(ks[2], (E, H, D), D), 'up_w': s(ks[3], (E, H, D), D), 'down_w': s(ks[4], (E, D, H), H), 'sgate_w': s(ks[5], (HS, D), D), 'sup_w': s(ks[6], (HS, D), D), 'sdown_w': s(ks[7], (D, HS), HS)}
    _L3_ffn_all = _L3_ffn_setup()
    _L3_ffn_in = {k: v for k, v in _L3_ffn_all.items() if k in ('router_w', 'router_bias', 'gate_w', 'up_w', 'down_w', 'sgate_w', 'sup_w', 'sdown_w')}
    del _L3_ffn_all
    return {'x': x, 'ctx_1024': ctx_1024, 'g_xattn': g_xattn, 'g_ffn': g_ffn, 'L0_xattn_Wq': _L0_xattn_in['Wq'], 'L0_xattn_Wk': _L0_xattn_in['Wk'], 'L0_xattn_Wv': _L0_xattn_in['Wv'], 'L0_xattn_gru_wih': _L0_xattn_in['gru_wih'], 'L0_xattn_gru_whh': _L0_xattn_in['gru_whh'], 'L0_xattn_gru_bih': _L0_xattn_in['gru_bih'], 'L0_xattn_gru_bhh': _L0_xattn_in['gru_bhh'], 'L0_xattn_slot_norm_w': _L0_xattn_in['slot_norm_w'], 'L0_xattn_input_norm_w': _L0_xattn_in['input_norm_w'], 'L0_ffn_packed_weight': _L0_ffn_in['packed_weight'], 'L0_ffn_weight_scale': _L0_ffn_in['weight_scale'], 'L0_ffn_bias': _L0_ffn_in['bias'], 'L1_xattn_wq': _L1_xattn_in['wq'], 'L1_xattn_bq': _L1_xattn_in['bq'], 'L1_xattn_wk': _L1_xattn_in['wk'], 'L1_xattn_bk': _L1_xattn_in['bk'], 'L1_xattn_wv': _L1_xattn_in['wv'], 'L1_xattn_bv': _L1_xattn_in['bv'], 'L1_xattn_wo': _L1_xattn_in['wo'], 'L1_xattn_bo': _L1_xattn_in['bo'], 'L1_ffn_weight': _L1_ffn_in['weight'], 'L1_ffn_aux_weight1': _L1_ffn_in['aux_weight1'], 'L1_ffn_aux_weight2': _L1_ffn_in['aux_weight2'], 'L1_ffn_bias': _L1_ffn_in['bias'], 'L2_xattn_Wq': _L2_xattn_in['Wq'], 'L2_xattn_bq': _L2_xattn_in['bq'], 'L2_xattn_Wk': _L2_xattn_in['Wk'], 'L2_xattn_bk': _L2_xattn_in['bk'], 'L2_xattn_Wv': _L2_xattn_in['Wv'], 'L2_xattn_bv': _L2_xattn_in['bv'], 'L2_xattn_Wo': _L2_xattn_in['Wo'], 'L2_xattn_bo': _L2_xattn_in['bo'], 'L2_ffn_Wr': _L2_ffn_in['Wr'], 'L2_ffn_br': _L2_ffn_in['br'], 'L2_ffn_W1': _L2_ffn_in['W1'], 'L2_ffn_b1': _L2_ffn_in['b1'], 'L2_ffn_W2': _L2_ffn_in['W2'], 'L2_ffn_b2': _L2_ffn_in['b2'], 'L3_xattn_Wq': _L3_xattn_in['Wq'], 'L3_xattn_bq': _L3_xattn_in['bq'], 'L3_xattn_Wk': _L3_xattn_in['Wk'], 'L3_xattn_bk': _L3_xattn_in['bk'], 'L3_xattn_Wv': _L3_xattn_in['Wv'], 'L3_xattn_bv': _L3_xattn_in['bv'], 'L3_ffn_router_w': _L3_ffn_in['router_w'], 'L3_ffn_router_bias': _L3_ffn_in['router_bias'], 'L3_ffn_gate_w': _L3_ffn_in['gate_w'], 'L3_ffn_up_w': _L3_ffn_in['up_w'], 'L3_ffn_down_w': _L3_ffn_in['down_w'], 'L3_ffn_sgate_w': _L3_ffn_in['sgate_w'], 'L3_ffn_sup_w': _L3_ffn_in['sup_w'], 'L3_ffn_sdown_w': _L3_ffn_in['sdown_w']}

def reference(x, ctx_1024, g_xattn, g_ffn, L0_xattn_Wq, L0_xattn_Wk, L0_xattn_Wv, L0_xattn_gru_wih, L0_xattn_gru_whh, L0_xattn_gru_bih, L0_xattn_gru_bhh, L0_xattn_slot_norm_w, L0_xattn_input_norm_w, L0_ffn_packed_weight, L0_ffn_weight_scale, L0_ffn_bias, L1_xattn_wq, L1_xattn_bq, L1_xattn_wk, L1_xattn_bk, L1_xattn_wv, L1_xattn_bv, L1_xattn_wo, L1_xattn_bo, L1_ffn_weight, L1_ffn_aux_weight1, L1_ffn_aux_weight2, L1_ffn_bias, L2_xattn_Wq, L2_xattn_bq, L2_xattn_Wk, L2_xattn_bk, L2_xattn_Wv, L2_xattn_bv, L2_xattn_Wo, L2_xattn_bo, L2_ffn_Wr, L2_ffn_br, L2_ffn_W1, L2_ffn_b1, L2_ffn_W2, L2_ffn_b2, L3_xattn_Wq, L3_xattn_bq, L3_xattn_Wk, L3_xattn_bk, L3_xattn_Wv, L3_xattn_bv, L3_ffn_router_w, L3_ffn_router_bias, L3_ffn_gate_w, L3_ffn_up_w, L3_ffn_down_w, L3_ffn_sgate_w, L3_ffn_sup_w, L3_ffn_sdown_w):
    import jax
    import jax.numpy as jnp

    def _L0_xattn_ref(slots, P, Wq, Wk, Wv, gru_wih, gru_whh, gru_bih, gru_bhh, slot_norm_w, input_norm_w):
        import jax, jax.numpy as jnp
        import numpy as np
        D = 256
        NUM_ITERS = 3
        EPS = 1e-06
        SCALE = D ** (-0.5)

        def rmsnorm(x, w, eps=EPS):
            return x * jax.lax.rsqrt(jnp.mean(x * x, axis=-1, keepdims=True) + eps) * w

        def gru_cell(x, h, wih, whh, bih, bhh):
            gx = x @ wih.T + bih
            gh = h @ whh.T + bhh
            xr, xz, xn = jnp.split(gx, 3, axis=-1)
            hr, hz, hn = jnp.split(gh, 3, axis=-1)
            r = jax.nn.sigmoid(xr + hr)
            z = jax.nn.sigmoid(xz + hz)
            n = jnp.tanh(xn + r * hn)
            return (1.0 - z) * n + z * h
        Pn = rmsnorm(P, input_norm_w)
        k_proj = Pn @ Wk.T
        v_proj = Pn @ Wv.T
        for _ in range(NUM_ITERS):
            sn = rmsnorm(slots, slot_norm_w)
            q_proj = sn @ Wq.T
            scores = jnp.einsum('bkd,bmd->bkm', q_proj, k_proj) * SCALE
            attn = jax.nn.softmax(scores, axis=-2)
            attn = attn / (jnp.sum(attn, axis=-1, keepdims=True) + EPS)
            updates = jnp.einsum('bkm,bmd->bkd', attn, v_proj)
            slots = gru_cell(updates, slots, gru_wih, gru_whh, gru_bih, gru_bhh)
        return slots

    def _L0_ffn_ref(x, packed_weight, weight_scale, bias):
        import jax, jax.numpy as jnp
        import numpy as np
        IN_F = 256
        OUT_F = 256
        B, S = (8, 1024)

        def _pack_ternary(tern):
            enc = (tern + 1.0).astype(jnp.int32).reshape(-1)
            return (enc[0::4] | enc[1::4] << 2 | enc[2::4] << 4 | enc[3::4] << 6).astype(jnp.int32)
        n = OUT_F * IN_F
        shifts = jnp.array([0, 2, 4, 6], dtype=jnp.int32)
        enc = (packed_weight[None, :] >> shifts[:, None] & 3).reshape(-1)[:n]
        w = (enc.astype(jnp.float32) - 1.0).reshape(OUT_F, IN_F) * weight_scale
        act_scale = 127.0 / jnp.maximum(jnp.max(jnp.abs(x), axis=-1, keepdims=True), 1e-05)
        x_dq = jnp.clip(jnp.round(x * act_scale), -128.0, 127.0) / act_scale
        return jnp.einsum('bsi,oi->bso', x_dq, w) + bias

    def _L1_xattn_ref(q, k, v, wq, bq, wk, bk, wv, bv, wo, bo):
        import jax, jax.numpy as jnp
        import numpy as np
        D_MODEL = 256
        NUM_HEADS = 16
        HEAD_DIM = D_MODEL // NUM_HEADS

        def _split_heads(x, B):
            return x.reshape(B, -1, NUM_HEADS, HEAD_DIM).transpose(0, 2, 1, 3)
        B = q.shape[0]
        qh = _split_heads(q @ wq + bq, B)
        kh = _split_heads(k @ wk + bk, B)
        vh = _split_heads(v @ wv + bv, B)
        scale = 1.0 / np.sqrt(HEAD_DIM).astype(np.float32)
        scores = jnp.einsum('bhqd,bhkd->bhqk', qh, kh) * scale
        probs = jax.nn.softmax(scores, axis=-1)
        out = jnp.einsum('bhqk,bhkd->bhqd', probs, vh)
        out = out.transpose(0, 2, 1, 3).reshape(B, -1, D_MODEL)
        return out @ wo + bo

    def _L1_ffn_ref(x, weight, aux_weight1, aux_weight2, bias):
        import jax, jax.numpy as jnp
        import numpy as np
        D_MODEL = 256
        h = jnp.einsum('btc,cd->btd', x, weight)
        h = jnp.einsum('btc,cd->btd', h, aux_weight1)
        h = jnp.einsum('btc,cd->btd', h, aux_weight2)
        return jnp.tanh(h + bias)

    def _L2_xattn_ref(x1, x2, Wq, bq, Wk, bk, Wv, bv, Wo, bo):
        import jax, jax.numpy as jnp
        import numpy as np
        DIM = 256
        N_HEADS = 16
        HEAD_DIM = DIM // N_HEADS
        B, N, M = (2, 512, 512)
        b, n, _ = x1.shape
        m = x2.shape[1]
        q = x1 @ Wq.T + bq
        k = x2 @ Wk.T + bk
        v = x2 @ Wv.T + bv
        q = q.reshape(b, n, N_HEADS, HEAD_DIM).transpose(0, 2, 1, 3)
        k = k.reshape(b, m, N_HEADS, HEAD_DIM).transpose(0, 2, 1, 3)
        v = v.reshape(b, m, N_HEADS, HEAD_DIM).transpose(0, 2, 1, 3)
        scale = 1.0 / jnp.sqrt(jnp.asarray(HEAD_DIM, dtype=q.dtype))
        scores = jnp.einsum('bhnd,bhmd->bhnm', q, k) * scale
        attn = jax.nn.softmax(scores, axis=-1)
        o = jnp.einsum('bhnm,bhmd->bhnd', attn, v)
        o = o.transpose(0, 2, 1, 3).reshape(b, n, DIM)
        return o @ Wo.T + bo

    def _L2_ffn_ref(x, Wr, br, W1, b1, W2, b2):
        import jax, jax.numpy as jnp
        import numpy as np
        D_MODEL, D_FF, N_EXP = (256, 1024, 8)
        B, S, D = x.shape
        xf = x.reshape(-1, D)
        logits = xf @ Wr.T + br
        expert_idx = jnp.argmax(logits, axis=-1)
        h = jax.nn.relu(jnp.einsum('td,efd->etf', xf, W1) + b1[:, None, :])
        y = jnp.einsum('etf,edf->etd', h, W2) + b2[:, None, :]
        out = y[expert_idx, jnp.arange(xf.shape[0])]
        return out.reshape(B, S, D)

    def _L3_xattn_ref(q, k, v, Wq, bq, Wk, bk, Wv, bv):
        import jax, jax.numpy as jnp
        import numpy as np
        MAX_BITS = 256.0

        def _quantize_kernel(kern):
            qmin = jnp.minimum(jnp.float32(10000000000.0), jnp.min(kern))
            qmax = jnp.maximum(jnp.float32(-10000000000.0), jnp.max(kern))
            s = 2.0 * jnp.maximum(jnp.abs(qmin), jnp.abs(qmax)) / MAX_BITS
            return jnp.round(kern / s) * s
        qp = jnp.einsum('bsi,id->bsd', q, _quantize_kernel(Wq)) + bq
        kp = jnp.einsum('bsi,id->bsd', k, _quantize_kernel(Wk)) + bk
        vp = jnp.einsum('bsi,id->bsd', v, _quantize_kernel(Wv)) + bv
        dk = jnp.float32(kp.shape[-1])
        logits = jnp.einsum('bqd,bkd->bqk', qp, kp) / jnp.sqrt(dk)
        attn = jax.nn.softmax(logits, axis=-1)
        return jnp.einsum('bqk,bkd->bqd', attn, vp)

    def _L3_ffn_ref(x, router_w, router_bias, gate_w, up_w, down_w, sgate_w, sup_w, sdown_w):
        import jax, jax.numpy as jnp
        import numpy as np
        TOPK = 4
        B, T, D = x.shape
        flat = x.reshape(B * T, D)
        logits = flat.astype(jnp.float32) @ router_w.T + router_bias
        scores = jax.nn.softmax(logits, axis=-1)
        topk_scores, topk_idx = jax.lax.top_k(scores, TOPK)
        topk_scores = topk_scores / jnp.clip(topk_scores.sum(axis=-1, keepdims=True), 1e-12, None)
        h = jax.nn.silu(jnp.einsum('nd,ehd->neh', flat, gate_w)) * jnp.einsum('nd,ehd->neh', flat, up_w)
        expert_out = jnp.einsum('neh,edh->ned', h, down_w)
        sel = jnp.take_along_axis(expert_out, topk_idx[:, :, None], axis=1)
        out = (sel * topk_scores.astype(flat.dtype)[:, :, None]).sum(axis=1)
        out = out + jax.nn.silu(flat @ sgate_w.T) * (flat @ sup_w.T) @ sdown_w.T
        return out.reshape(B, T, D)
    x = x + jnp.tanh(g_xattn[0]) * _L0_xattn_ref(_layernorm(x, axis=-1), ctx_1024, L0_xattn_Wq, L0_xattn_Wk, L0_xattn_Wv, L0_xattn_gru_wih, L0_xattn_gru_whh, L0_xattn_gru_bih, L0_xattn_gru_bhh, L0_xattn_slot_norm_w, L0_xattn_input_norm_w)
    x = x + jnp.tanh(g_ffn[0]) * _L0_ffn_ref(_layernorm(x, axis=-1), L0_ffn_packed_weight, L0_ffn_weight_scale, L0_ffn_bias)
    x = x + jnp.tanh(g_xattn[1]) * _L1_xattn_ref(_layernorm(x, axis=-1), ctx_1024, ctx_1024, L1_xattn_wq, L1_xattn_bq, L1_xattn_wk, L1_xattn_bk, L1_xattn_wv, L1_xattn_bv, L1_xattn_wo, L1_xattn_bo)
    x = x + jnp.tanh(g_ffn[1]) * _L1_ffn_ref(_layernorm(x, axis=-1), L1_ffn_weight, L1_ffn_aux_weight1, L1_ffn_aux_weight2, L1_ffn_bias)
    x = x + jnp.tanh(g_xattn[2]) * _L2_xattn_ref(_layernorm(x, axis=-1), ctx_1024, L2_xattn_Wq, L2_xattn_bq, L2_xattn_Wk, L2_xattn_bk, L2_xattn_Wv, L2_xattn_bv, L2_xattn_Wo, L2_xattn_bo)
    x = x + jnp.tanh(g_ffn[2]) * _L2_ffn_ref(_layernorm(x, axis=-1), L2_ffn_Wr, L2_ffn_br, L2_ffn_W1, L2_ffn_b1, L2_ffn_W2, L2_ffn_b2)
    x = x + jnp.tanh(g_xattn[3]) * _L3_xattn_ref(_layernorm(x, axis=-1), ctx_1024, ctx_1024, L3_xattn_Wq, L3_xattn_bq, L3_xattn_Wk, L3_xattn_bk, L3_xattn_Wv, L3_xattn_bv)
    x = x + jnp.tanh(g_ffn[3]) * _L3_ffn_ref(_layernorm(x, axis=-1), L3_ffn_router_w, L3_ffn_router_bias, L3_ffn_gate_w, L3_ffn_up_w, L3_ffn_down_w, L3_ffn_sgate_w, L3_ffn_sup_w, L3_ffn_sdown_w)
    return x

_drawn_inputs = setup_inputs


def setup_inputs(seed=0):
    import zlib

    import numpy as np

    out = dict(_drawn_inputs(seed))
    spreads = {'L0_xattn_gru_bih': (0.0, 0.1),
     'L0_xattn_gru_bhh': (0.0, 0.1),
     'L0_xattn_slot_norm_w': (1.0, 0.2),
     'L0_xattn_input_norm_w': (1.0, 0.2),
     'L0_ffn_bias': (0.0, 0.1),
     'L1_xattn_bq': (0.0, 0.268),
     'L1_xattn_bk': (0.0, 2.0),
     'L1_xattn_bv': (0.0, 0.1),
     'L1_xattn_bo': (0.0, 0.1),
     'L1_ffn_bias': (0.0, 0.1),
     'L2_xattn_bq': (0.0, 0.273),
     'L2_xattn_bk': (0.0, 2.0),
     'L2_xattn_bv': (0.0, 0.1),
     'L2_xattn_bo': (0.0, 0.1),
     'L3_ffn_router_bias': (0.0, 0.1)}
    factors = {'g_ffn': 23.408,
     'L2_ffn_b1': 4.011,
     'L2_ffn_b2': 3.25,
     'L3_xattn_Wq': 7.289,
     'L3_xattn_bq': 22.502,
     'L3_xattn_Wk': 7.499,
     'L3_xattn_bk': 64.0,
     'L3_xattn_bv': 3.423}
    for name, (base, spread) in spreads.items():
        noise = np.random.default_rng([zlib.crc32(name.encode()), seed]).standard_normal(out[name].shape)
        drawn = base * np.exp(spread * noise) if base else spread * noise
        out[name] = jnp.asarray(drawn.astype(out[name].dtype))
    for name, factor in factors.items():
        out[name] = (out[name] * factor).astype(out[name].dtype)
    return out
```

```python
from contextlib import ExitStack

import concourse.bass as bass
from concourse import mybir

F32 = mybir.dt.float32
BF16 = mybir.dt.bfloat16
I32 = mybir.dt.int32
U32 = mybir.dt.uint32
ALU = mybir.AluOpType
ACT = mybir.ActivationFunctionType
AX = mybir.AxisListType

P = 128
B, S, D, M = 2, 1024, 256, 154
C = D // P
T = B * S // P
GT = 4
GN = GT * P
G = T // GT
GB = G // B
MR = M - P
BM = B * M
ITERS = 3
H, HD = 16, 16
E4, K4, F4 = 32, 4, 128
NT4 = K4 * T + E4
NQ = NT4 // 4
FS = K4 * F4
E2, F2 = 8, 1024
NT2 = T + E2
ROUND = 1.5 * 2 ** 23
LN_EPS, RMS_EPS = 1e-5, 1e-6
RSQRT_MAGIC = 0x5F3759DF
NEWTON = 3


class Chain:

    def __init__(self, eng, sem, per_turn=0, turn=0):
        self.eng, self.sem, self.n = eng, sem, 0
        self.base, self.per_turn = turn * per_turn, per_turn

    def step(self, ins):
        ins.then_inc(self.sem, 1)
        self.n += 1

    def settle(self):
        self.eng.wait_ge(self.sem, self.base + self.n)

    def close(self):
        assert self.n == self.per_turn, (self.n, self.per_turn)


class Series:

    def __init__(self, sem, totals):
        self.sem, self.base, n = sem, {}, 0
        for stage, total in totals.items():
            self.base[stage] = n
            n += total

    def at(self, stage, n):
        return self.sem, self.base[stage] + n


def weight(ap):
    return ap.rearrange("(c p) n -> p c n", p=P)


def build(nc, d, out, last_stage):
    ctx = ExitStack()
    with ctx:
        def sb(name, shape, dt=F32):
            return ctx.enter_context(nc.sbuf_tensor(name, shape, dt))

        def sem(name):
            return ctx.enter_context(nc.semaphore(name))

        def series(name, totals):
            return Series(sem(name), totals)

        psum = ctx.enter_context(nc.psum_tensor("psum", [P, 8, 512], F32))
        bank = [psum[:, i] for i in range(8)]
        x_tok = sb("x_tok", [P, T, D])
        ident = sb("ident", [P, P])
        ones = sb("ones", [P, P])
        ctxT = sb("ctxT", [P, C, BM])
        tanh_g = sb("tanh_g", [P, 8])
        arena = sb("arena", [P, 32768])
        used = [0]

        def carve(cols, *shape, at=None):
            if at is None:
                at = used[0]
                used[0] += cols
            assert at + cols <= 32768
            return arena[:, at:at + cols]

        xn = sb("xn", [P, G, GT, D])
        xq = sb("xq", [P, 2, GT * D], BF16)
        xnT = sb("xnT", [P, 2, C, GN])
        stats = sb("stats", [P, 2, GT, 6])
        meanvar = sb("meanvar", [P, 2, GT, 2])
        add_row = sb("add_row", [P, 5, D])
        ident_bf = sb("ident_bf", [P, P], BF16)
        scrap = sb("scrap", [P, 64])
        scraps = iter(range(64))

        def take_wait(dve):
            k = next(scraps)
            dve.memset(scrap[:, k:k + 1], 0.0)

        nwt = sb("nwt", [P, 2, 3, T])

        hT = carve(C * T * P).rearrange("p (c n) -> p c n", c=C)
        wqkv0 = carve(3 * C * D).rearrange("p (w c n) -> p w c n", w=3, c=C)
        wih = carve(C * 3 * D).rearrange("p (c n) -> p c n", c=C)
        whh = carve(C * 3 * D).rearrange("p (c n) -> p c n", c=C)
        vec0 = carve(16 * C).rearrange("p (v c) -> p v c", c=C)
        sq = carve(2 * C * GN).rearrange("p (q c n) -> p q c n", q=2, c=C)
        PnT = carve(C * BM).rearrange("p (c n) -> p c n", c=C)
        kvT = carve(2 * C * BM).rearrange("p (w c n) -> p w c n", w=2, c=C)
        kqT = carve(C * BM).rearrange("p (c n) -> p c n", c=C)
        vW = carve(B * 3 * D).rearrange("p (b n) -> p b n", b=B)
        vWr = carve(B * 3 * D).rearrange("p (b n) -> p b n", b=B)
        vWs = carve(B * 3 * D).rearrange("p (b n) -> p b n", b=B)
        vWsr = carve(B * 3 * D).rearrange("p (b n) -> p b n", b=B)
        diag = carve(2 * GN).rearrange("p (q n) -> p q n", q=2)
        spread = carve(G * GN).rearrange("p (q n) -> p q n", q=G)
        e_main = carve(B * S).rearrange("p (b n) -> p b n", b=B)
        e_rem = carve(B * S).rearrange("p (b n) -> p b n", b=B)
        gate_r = carve(2 * GN).rearrange("p (q n) -> p q n", q=2)
        gate_z = carve(2 * GN).rearrange("p (q n) -> p q n", q=2)
        gate_u = carve(2 * GN).rearrange("p (q n) -> p q n", q=2)
        cand = carve(2 * GN).rearrange("p (q n) -> p q n", q=2)
        small = carve(256)
        rms16 = small[:, 0:T]
        mx = small[:, 16:32].rearrange("p (k b q) -> p k b q", k=2, b=B)[:, :, :, 0:2]
        mneg = small[:, 32:36].rearrange("p (k b) -> p k b", k=2)
        ssum = small[:, 36:40].rearrange("p (k b) -> p k b", k=2)
        sinv = small[:, 40:44].rearrange("p (k b) -> p k b", k=2)
        rinv = small[:, 48:64]
        bsum = small[:, 64:64 + 8 * C].rearrange("p (v c) -> p v c", c=C)
        BIH, BHH, SLOTW, INW = 0, 3, 6, 7

        packed = sb("packed", [P, C, D // 4], I32)
        unpacked = sb("unpacked", [P, C, D // 4], I32)
        tern = sb("tern", [P, C, D], BF16)
        qT = xnT[:].bitcast(BF16)
        wscale = sb("wscale", [P, 1])
        amax = sb("amax", [P, G, 3, GT])

        used[0] = 0
        wmha = carve(2 * 4 * C * D).rearrange("p (l w c n) -> p l w c n", l=2, w=4, c=C)
        vmha = carve(2 * 4 * C).rearrange("p (l v c) -> p l v c", l=2, v=4)
        qhT = carve(2 * C * GN).rearrange("p (u c n) -> p u c n", u=2, c=C)
        keys = carve(C * B * 2 * M).rearrange("p (c b h m) -> p c b h m", c=C, b=B, h=2)
        ctxR = carve(C * B * P).rearrange("p (c b n) -> p c b n", c=C, b=B)
        vals = carve(B * H * P + P)
        valsR = carve(B * 4 * P + P)
        probs = carve(2 * H * M).rearrange("p (u h m) -> p u h m", u=2, h=H)
        probsR = carve(2 * H * 32).rearrange("p (u h m) -> p u h m", u=2, h=H)
        probsT = carve(2 * 20 * P).rearrange("p (u h m) -> p u h m", u=2, h=20)
        headsT = carve(2 * C * GN).rearrange("p (u c n) -> p u c n", u=2, c=C)
        smax = carve(2 * H).rearrange("p (u h) -> p u h", u=2)
        nmax = carve(2 * H).rearrange("p (u h) -> p u h", u=2)
        hsum = carve(2 * H).rearrange("p (u h) -> p u h", u=2)
        rsum = carve(2 * H).rearrange("p (u h) -> p u h", u=2)
        bvrow = carve(C * P).rearrange("p (c n) -> p c n", c=C)
        mask16 = sb("mask16", [P, 2])
        mask32 = sb("mask32", [P, 4])
        pidx = sb("pidx", [P, 2], I32)

        side = sb("side", [P, 4608])
        wtri = side[:, 0:3 * C * D].rearrange("p (w c n) -> p w c n", w=3, c=C)
        wtri12 = side[:, 1536:2560].rearrange("p (w c n) -> p w c n", w=2, c=C)
        tri_out = side[:, 2560:4608].rearrange("p (u n) -> p u n", u=2)

        W1 = arena[:, 0:E2 * C * F2].rearrange("p (e n) -> p e n", e=E2)
        W2 = arena[:, E2 * C * F2:].rearrange("p (e n) -> p e n", e=E2)
        b2row = side[:, 0:E2 * D]
        xin = side[:, 2560:3072].rearrange("p (u n) -> p u n", u=2)
        xinT = side[:, 3072:3584].rearrange("p (u n) -> p u n", u=2)
        yout = side[:, 3584:4096].rearrange("p (u n) -> p u n", u=2)
        b1col = side[:, 4096:4096 + E2 * F2 // P]
        wr5 = side[:, 4160:4160 + C * E2].rearrange("p (c n) -> p c n", c=C)
        br5 = side[:, 4176:4176 + E2]
        hpre = xn[:].rearrange("p g t d -> p (g t d)")[:, 0:2048].rearrange("p (u n) -> p u n", u=2)
        hact = xn[:].rearrange("p g t d -> p (g t d)")[:, 2048:4096].rearrange("p (u n) -> p u n", u=2)
        gathered5 = side[:, 0:T * D].rearrange("p (k d) -> p k d", d=D)

        used[0] = 24576
        w6 = carve(3 * C * D).rearrange("p (w c n) -> p w c n", w=3, c=C)
        vec6 = carve(2 * C).rearrange("p (v c) -> p v c", c=C)
        max6 = carve(16)
        kpT6 = carve(C * BM).rearrange("p (c n) -> p c n", c=C)
        kq6 = carve(C * BM).rearrange("p (c n) -> p c n", c=C)
        bias6 = carve(BM)
        bq6 = carve(C * P).rearrange("p (c n) -> p c n", c=C)
        vals6 = carve(B * D).rearrange("p (b n) -> p b n", b=B)
        vals6R = carve(B * D).rearrange("p (b n) -> p b n", b=B)
        sc6 = carve(2 * GT * M).rearrange("p (u t m) -> p u t m", u=2, t=GT)
        probs6T = carve(2 * GN).rearrange("p (u n) -> p u n", u=2)
        probs6R = carve(2 * GN).rearrange("p (u n) -> p u n", u=2)
        col6 = carve(2 * 4 * GT).rearrange("p (u k t) -> p u k t", u=2, k=4)

        GU = arena[:, 0:E4 * C * 2 * F4].rearrange("p (e c n) -> p e c n", e=E4, c=C)
        DOWN0 = E4 * C * 2 * F4
        DW = arena[:, DOWN0:DOWN0 + E4 * D].rearrange("p (e n) -> p e n", e=E4)
        TAIL = DOWN0 + E4 * D
        sgate = side[:, 0:C * FS].rearrange("p (c n) -> p c n", c=C)
        sup = side[:, C * FS:2 * C * FS].rearrange("p (c n) -> p c n", c=C)
        sdown = side[:, 2 * C * FS:2 * C * FS + FS // P * D].rearrange("p (h n) -> p h n", n=D)
        wr7 = side[:, 3072:3072 + C * E4].rearrange("p (c n) -> p c n", c=C)
        br7 = side[:, 3136:3136 + E4]
        tanh_s = xq[:].rearrange("p u n -> p (u n)").bitcast(F32).rearrange("p (u n) -> p u n", u=2)
        xnT_more = arena[:, 28672:28672 + 2048].rearrange("p (u c n) -> p u c n", u=2, c=C)
        hshared = arena[:, 30720:30720 + 2048].rearrange("p (h n) -> p h n", n=GN)
        xn_flat = xn[:].rearrange("p g t d -> p (g t d)")
        qin = xn_flat[:, 0:2048].rearrange("p (u t d) -> p u t d", u=2, t=4)
        qinT = xn_flat[:, 2048:4096].rearrange("p (u c n) -> p u c n", u=2, c=C)
        qout = xnT[:].rearrange("p u c n -> p (u c n)").rearrange("p (u n) -> p u n", u=2)
        qtanh = arena[:, 28672:29696].rearrange("p (u t n) -> p u t n", u=2, t=4)
        qhid = arena[:, 29696:30720].rearrange("p (u t n) -> p u t n", u=2, t=4)
        qhidT = arena[:, 30720:31744].rearrange("p (u n) -> p u n", u=2)
        gathered7 = arena[:, 0:T * K4 * D].rearrange("p (t k d) -> p t k d", t=T, k=K4)

        before = sb("before", [P, P], BF16)
        upto = sb("upto", [P, 2, 32], BF16)
        ones_bf = sb("ones_bf", [P, P], BF16)
        iota_e = sb("iota_e", [P, 32])
        iota_n = sb("iota_n", [P, 96])
        zeros = sb("zeros", [P, D])
        route = {}
        for s_, E_, K_, NT_, region in ((5, E2, 1, NT2, xq[:].rearrange("p u n -> p (u n)").bitcast(F32)),
                                      (7, E4, K4, NT4, arena[:, TAIL:28672])):
            at = [0]

            def part(cols, dt=F32):
                r = region[:, at[0]:at[0] + cols]
                at[0] += cols
                return r if dt is F32 else r.bitcast(dt)

            route[s_] = dict(
                E=E_, K=K_, NT=NT_,
                logits=part(T * E_).rearrange("p (t e) -> p t e", t=T),
                top=part(T * 8).rearrange("p (t k) -> p t k", k=8),
                index=part(T * 8, U32).rearrange("p (t k) -> p t k", k=8),
                index_f=part(T * K_).rearrange("p (t k) -> p t k", k=K_),
                hot=part(T * K_ * E_ // 2, BF16).rearrange("p (t k e) -> p t k e", t=T, k=K_),
                any_hot=part(T * E_ // 2, BF16).rearrange("p (t e) -> p t e", t=T),
                earlier=part((T + 1) * E_ // 2, BF16).rearrange("p (t e) -> p t e", t=T + 1),
                place=part(T * E_).rearrange("p (t e) -> p t e", t=T),
                picked=part(T * E_).rearrange("p (t e) -> p t e", t=T),
                slot=part(T * K_).rearrange("p (t k) -> p t k", k=K_),
                slot_i=part(T * K_, I32).rearrange("p (t k) -> p t k", k=K_),
                start=part(2 * E_),
                share=part(T * K_).rearrange("p (t k) -> p t k", k=K_) if K_ > 1 else None,
                total=part(2 * T) if K_ > 1 else None,
                count=part(4),
                count_i=part(2, I32),
                tiles_b=part(P // 2, BF16),
                passed=part(NT_ // 2, BF16),
                expert=part(NT_, I32) if s_ == 7 else sb(f"expert{s_}", [1, NT_], I32)[:],
                expert_f=part(NT_) if s_ == 7 else sb(f"expert_f{s_}", [1, NT_])[:])
            assert at[0] <= region.shape[1], at[0]

        def head_steps():
            for n in range(-1, T + 1):
                g, t = n // GT, n % GT
                ops = []
                if n == -1:
                    ops += [("turn", 0), ("query", 0)]
                score = [("score", n + 1, k) for k in range(4)] if n + 1 < T else []
                turn = [("weights", n, k) for k in range(5)] if 0 <= n < T else []
                weigh = [("values", n - 1, c) for c in range(C)] if n >= 1 else []
                ops += score[0:2] + turn[0:2] + score[2:3] + weigh[0:1] + turn[2:3] + score[3:4] + weigh[1:2] + turn[3:5]
                if n >= 0 and t == 1 and g + 1 < G:
                    ops.append(("turn", g + 1))
                if n >= 0 and t == 2 and g + 1 < G:
                    ops.append(("query", g + 1))
                if n >= GT and t == 0:
                    ops.append(("project", g - 1))
                yield n, ops

        ring = {}
        for n, ops in head_steps():
            for op in ops:
                if op[0] == "weights":
                    ring[op] = len(ring)
                elif op[0] in ("turn", "query"):
                    for c in range(C):
                        ring[op + (c,)] = len(ring)
        RING = len(ring)
        assert RING % 2 == 0

        x_loaded = sem("x_loaded")
        ctx_loaded = sem("ctx_loaded")
        gains_loaded = sem("gains_loaded")
        w0_loaded = sem("w0_loaded")
        unpacked_ready = sem("unpacked_ready")
        out_stored = sem("out_stored")
        w1_loaded = sem("w1_loaded")
        rows_loaded = sem("rows_loaded")
        w3_loaded = sem("w3_loaded")
        wmha_loaded = [sem(f"wmha_loaded{l}") for l in range(2)]
        rows_ready = sem("rows_ready")
        row_added = series("row_added", {s: G for s in (1, 2, 4, 6)})
        tern_ready = sem("tern_ready")
        xq_ready = sem("xq_ready")
        masks_made = sem("masks_made")
        project_ready = series("project_ready", {1: G, 3: G})
        tri_folded = sem("tri_folded")
        tri_copied = sem("tri_copied")
        tri_summed = sem("tri_summed")
        tri_tanh = sem("tri_tanh")
        ctxR_made = sem("ctxR_made")
        bv_ready = series("bv_ready", {l: C for l in range(2)})
        context_done = series("context_done", {l: 7 for l in range(2)})
        keys_ready = series("keys_ready", {l: C for l in range(2)})
        vals_ready = series("vals_ready", {l: B for l in range(2)})
        cvec_ready = series("cvec_ready", {l: 1 for l in range(2)})
        q_ready, half_projected = (series(k, {s: 2 * G for s in (2, 4)}) for k in ("q_ready", "half_projected"))
        half_added = series("half_added", {s: G for s in (2, 4)})
        headsT_ready = [series(f"headsT_ready{c}", {s: G for s in (2, 4)}) for c in range(C)]
        pair_scored, pair_max, pair_exp = (series(k, {s: 4 * T for s in (2, 4)}) for k in ("pair_scored", "pair_max", "pair_exp"))
        half_sums, half_scaled = (series(k, {s: 2 * T for s in (2, 4)}) for k in ("half_sums", "half_scaled"))
        pv_done = series("pv_done", {s: 2 * T for s in (2, 4)})
        ring_filled = series("ring_filled", {s: RING for s in (2, 4)})
        ring_read = [series(f"ring_read{k}", {s: RING // 2 for s in (2, 4)}) for k in range(2)]
        route_consts = sem("route_consts")
        zeroed = sem("zeroed")
        w5_loaded = sem("w5_loaded")
        expert5_loaded = sem("expert5_loaded")
        logits_done, logits_read, hot_ready = (series(k, {s: G for s in (5, 7)}) for k in ("logits_done", "logits_read", "hot_ready"))
        earlier_ready = series("earlier_ready", {s: T for s in (5, 7)})
        ranks_done, count_done, tiles_ready, start_done, slots_ready, passed_ready, expert_done, expert_ready = (
            series(k, {s: 1 for s in (5, 7)}) for k in (
                "ranks_done", "count_done", "tiles_ready", "start_done", "slots_ready", "passed_ready", "expert_done", "expert_ready"))
        scattered = series("scattered", {5: 16 * T, 7: 16 * T * 4})
        in_loaded, stored = ([series(f"{k}{u}", {5: 8 * NT2, 7: 8 * NQ}) for u in range(2)] for k in ("in_loaded", "stored"))
        in_turned, inT_ready = (series(k, {5: NT2, 7: 2 * NQ}) for k in ("in_turned", "inT_ready"))
        hidden_done, out_done, out_ready = (series(k, {5: NT2, 7: NQ}) for k in ("hidden_done", "out_done", "out_ready"))
        hidden_turned = series("hidden_turned", {5: 2 * NT2, 7: NQ})
        hpre_copied, h_act = sem("hpre_copied"), sem("h_act")
        gathered5_in = [sem(f"gathered5_in{g}") for g in range(G)]
        (shares_shifted, shares_exp, shared_hid, shared_done, shared_added, shared_down, shared_tanh, qtanh_ready,
         qgate_ready, qhid_ready, qhidT_ready, w7_loaded) = (
            sem(k) for k in ("shares_shifted", "shares_exp", "shared_hid", "shared_done", "shared_added", "shared_down",
                             "shared_tanh", "qtanh_ready", "qgate_ready", "qhid_ready", "qhidT_ready", "w7_loaded"))
        ws_loaded = sem("ws_loaded")
        gathered7_in = [sem(f"gathered7_in{g}") for g in range(G)]
        w6_loaded, max_found, max_turned, max_diag, max_spread, w6_rounded, kp_done, kp_ready, ctx6_done, ctx6_ready = (
            sem(k) for k in ("w6_loaded", "max_found", "max_turned", "max_diag", "max_spread", "w6_rounded", "kp_done",
                             "kp_ready", "ctx6_done", "ctx6_ready"))
        scored6, scores_read6, max_ready6, exp_ready6, turned6, main_copied6, rest_copied6, pv_done6 = (
            sem(k) for k in ("scored6", "scores_read6", "max_ready6", "exp_ready6", "turned6", "main_copied6",
                             "rest_copied6", "pv_done6"))
        consts_made = sem("consts_made")
        gains_ready = sem("gains_ready")
        dve_step = sem("dve_step")
        xn_ready = series("xn_ready", {s: G for s in range(8)})
        turned = series("turned", {s: G * C for s in (0, 1, 3, 5, 6, 7)})
        xnT_ready = series("xnT_ready", {s: G * C for s in (0, 1, 3, 5, 6, 7)})
        h_ready = sem("h_ready")
        c_sq = sem("c_sq")
        c_ms = sem("c_ms")
        c_rms = sem("c_rms")
        c_pn = sem("c_pn")
        c_kv = sem("c_kv")
        c_kv_copied = sem("c_kv_copied")
        c_kq = sem("c_kq")
        c_kq_copied = sem("c_kq_copied")
        c_vw = sem("c_vw")
        c_vw_copied = sem("c_vw_copied")
        sq_ready = sem("sq_ready")
        ms_ready = sem("ms_ready")
        diag_ready = sem("diag_ready")
        spread_ready = sem("spread_ready")
        spread_copied = sem("spread_copied")
        scores_ready = sem("scores_ready")
        scores_scaled = sem("scores_scaled")
        max_ready = sem("max_ready")
        rinv_ready = sem("rinv_ready")
        exp_ready = sem("exp_ready")
        sinv_ready = sem("sinv_ready")
        vws_ready = sem("vws_ready")
        rowsum_ready = sem("rowsum_ready")
        attn_ready = sem("attn_ready")
        gate_done = {k: sem(f"gate_{k}_done") for k in ("hn", "r", "z", "xn")}
        gate_read = {k: sem(f"gate_{k}_read") for k in ("hn", "r", "z", "xn")}
        cand_ready = sem("cand_ready")
        slotsT_ready = sem("slotsT_ready")
        x_done = series("x_done", {s: G for s in range(8)})

        xs5 = nc.dram_tensor("xs5", (NT2 * P, D), F32, kind="Internal").ap()
        ys5 = nc.dram_tensor("ys5", (NT2 * P, D), F32, kind="Internal").ap()
        xs7 = nc.dram_tensor("xs7", (NT4 * P, D), F32, kind="Internal").ap()
        ys7 = nc.dram_tensor("ys7", (NT4 * P, D), F32, kind="Internal").ap()
        block = ctx.enter_context(nc.Block())


        def route_constants_gpsimd(pool):
            pool.memset(zeros[:], 0.0).then_inc(route_consts, 1)
            pool.memset(ones_bf[:], 1.0).then_inc(route_consts, 1)
            pool.iota(iota_e[:], [[1, 32]], base=0, channel_multiplier=0,
                      allow_small_or_imprecise_dtypes=True).then_inc(route_consts, 1)
            pool.iota(iota_n[:], [[1, 96]], base=0, channel_multiplier=0,
                      allow_small_or_imprecise_dtypes=True).then_inc(route_consts, 1)
            pool.wait_ge(route_consts, 2)
            pool.affine_select(before[:], ones_bf[:], [[1, P]], ALU.is_gt, 0.0, base=0,
                               channel_multiplier=-1).then_inc(route_consts, 1)
            pool.affine_select(upto[:, 0], ones_bf[:, 0:32], [[1, 32]], ALU.is_gt, 0.0, base=0,
                               channel_multiplier=-1).then_inc(route_consts, 1)
            pool.affine_select(upto[:, 1], ones_bf[:, 0:32], [[1, 32]], ALU.is_ge, 0.0, base=0,
                               channel_multiplier=-1).then_inc(route_consts, 1)

        def place(s, g):
            return xnT_more[:, g - 2] if s == 7 and g >= 2 else xnT[:, g % 2]

        def route_tensor(pe, s, wr, wr_loaded, free):
            r = route[s]
            E = r["E"]
            pe.wait_ge(*wr_loaded)
            pe.wait_ge(route_consts, 7)
            free()
            for g in range(G):
                turn_group(pe, s, g)
                pe.wait_ge(*xnT_ready.at(s, (g + 1) * C))
                if g >= 2:
                    pe.wait_ge(*logits_read.at(s, g - 1))
                for t in range(GT):
                    for c in range(C):
                        ins = pe.matmul(bank[2 + g % 2][:, t * E:(t + 1) * E], place(s, g)[:, c, t * P:(t + 1) * P], wr[:, c],
                                        start=(c == 0), stop=(c == C - 1))
                ins.then_inc(logits_done.sem, 1)
            pe.wait_ge(*earlier_ready.at(s, T))
            pe.wait_ge(*hot_ready.at(s, G))
            for n in range(T):
                dst = bank[4][:, n * E:(n + 1) * E]
                ins = pe.matmul(dst, before[:], r["any_hot"][:, n], start=True, stop=(n == 0))
                if n:
                    ins = pe.matmul(dst, ones_bf[:], r["earlier"][:, n], start=False, stop=True)
            ins.then_inc(ranks_done.sem, 1)
            pe.matmul(bank[5][0:E, 0:1], r["earlier"][:, T], ones_bf[:, 0:1], start=True, stop=True).then_inc(count_done.sem, 1)
            pe.wait_ge(*tiles_ready.at(s, 1))
            pe.matmul(bank[6][:, 0:E], r["tiles_b"][0:E], upto[0:E, 0, 0:E], start=True, stop=True)
            pe.matmul(bank[6][0:E, E:E + 1], upto[0:E, 1, 0:E], r["tiles_b"][0:E, 0:1], start=True,
                      stop=True).then_inc(start_done.sem, 1)
            pe.wait_ge(*passed_ready.at(s, 1))
            pe.matmul(bank[7][0:1, 0:r["NT"]], ones_bf[0:E, 0:1], r["passed"][0:E], start=True,
                      stop=True).then_inc(expert_done.sem, 1)

        def route_scalar(act, s):
            for g in range(G):
                if g >= 2 and s == 5:
                    act.wait_ge(*logits_done.at(s, g - 1))
                elif g >= 2:
                    act.wait_ge(*x_done.at(6, G))
                copy_turned(act, s, g, place(s, g))

        def route_vector(dve, ch, s, br):
            r = route[s]
            E, K, NT = r["E"], r["K"], r["NT"]
            dve.wait_ge(route_consts, 7)
            for g in range(G):
                ts_ = slice(g * GT, (g + 1) * GT)
                dve.wait_ge(*logits_done.at(s, g + 1))
                dve.tensor_tensor(r["logits"][:, ts_], bank[2 + g % 2][:, 0:GT * E].rearrange("p (t e) -> p t e", t=GT),
                                  br.unsqueeze(1).broadcast_to([P, GT, E]), ALU.add).then_inc(logits_read.sem, 1)
                dve.wait_ge(*logits_read.at(s, g + 1))
                for n in range(g * GT, (g + 1) * GT):
                    ch.step(dve.max(r["top"][:, n], r["logits"][:, n]))
                ch.settle()
                for n in range(g * GT, (g + 1) * GT):
                    ch.step(dve.max_index(r["index"][:, n], r["top"][:, n], r["logits"][:, n]))
                ch.settle()
                ch.step(dve.tensor_copy(r["index_f"][:, ts_], r["index"][:, ts_, 0:K]))
                ch.settle()
                ins = dve.tensor_tensor(r["hot"][:, ts_].rearrange("p t k e -> p (t k) e"),
                                        iota_e[:, 0:E].unsqueeze(1).broadcast_to([P, GT * K, E]),
                                        r["index_f"][:, ts_].rearrange("p t k -> p (t k)").unsqueeze(2).broadcast_to([P, GT * K, E]),
                                        ALU.is_equal)
                ch.step(ins)
                ch.settle()
                with nc.allow_low_precision(reason="sums of zeros and ones"):
                    dve.tensor_reduce(r["any_hot"][:, ts_], r["hot"][:, ts_].rearrange("p t k e -> p t e k"), AX.X,
                                      ALU.add).then_inc(hot_ready.sem, 1)
            for n in range(T):
                dve.wait_ge(*hot_ready.at(s, n // GT + 1))
                if n:
                    dve.wait_ge(*earlier_ready.at(s, n))
                    ins = dve.tensor_tensor(r["earlier"][:, n + 1], r["earlier"][:, n], r["any_hot"][:, n], ALU.add)
                else:
                    ins = dve.tensor_copy(r["earlier"][:, 1], r["any_hot"][:, 0])
                ins.then_inc(earlier_ready.sem, 1)
            dve.wait_ge(*count_done.at(s, 1))
            ch.step(dve.tensor_scalar(r["count_i"][0:E, 0:1], bank[5][0:E, 0:1], P - 1.0, None, ALU.add))
            ch.settle()
            ch.step(dve.tensor_scalar(r["count_i"][0:E, 1:2], r["count_i"][0:E, 0:1], 7, None, ALU.arith_shift_right))
            ch.settle()
            ch.step(dve.tensor_copy(r["count"][0:E, 0:1], r["count_i"][0:E, 1:2]))
            ch.settle()
            dve.tensor_scalar(r["tiles_b"][0:E], ones[0:E], r["count"][0:E, 0:1], None, ALU.mult).then_inc(tiles_ready.sem, 1)
            dve.wait_ge(*start_done.at(s, 1))
            ch.step(dve.tensor_copy(r["start"][:, 0:E], bank[6][:, 0:E]))
            ch.step(dve.tensor_copy(r["count"][0:E, 1:2], bank[6][0:E, E:E + 1]))
            ch.settle()
            dve.tensor_scalar(r["passed"][0:E], iota_n[0:E, 0:NT], r["count"][0:E, 1:2], None,
                              ALU.is_ge).then_inc(passed_ready.sem, 1)
            dve.wait_ge(*ranks_done.at(s, 1))
            ch.step(dve.scalar_tensor_tensor(r["place"], r["start"][:, 0:E].unsqueeze(1).broadcast_to([P, T, E]), float(P),
                                             bank[4][:, 0:T * E].rearrange("p (t e) -> p t e", t=T), ALU.mult, ALU.add))
            ch.settle()
            for k in range(K):
                ch.step(dve.tensor_tensor(r["picked"], r["hot"][:, :, k], r["place"], ALU.mult))
                ch.settle()
                ch.step(dve.tensor_reduce(r["slot"][:, :, k], r["picked"], AX.X, ALU.add))
                ch.settle()
            dve.tensor_copy(r["slot_i"], r["slot"]).then_inc(slots_ready.sem, 1)
            dve.wait_ge(*expert_done.at(s, 1))
            ch.step(dve.tensor_scalar(r["expert_f"][0:1], bank[7][0:1, 0:NT], float(E - 1), None, ALU.min))
            ch.settle()
            dve.tensor_copy(r["expert"][0:1], r["expert_f"][0:1]).then_inc(expert_ready.sem, 1)

        def scatter_gpsimd(pool, s, xs):
            r = route[s]
            pool.wait_ge(*slots_ready.at(s, 1))
            pool.wait_ge(zeroed, 2 * 16)
            for n in range(T):
                for k in range(r["K"]):
                    pool.indirect_dma_start(xs, bass.IndirectOffsetOnAxis(r["slot_i"][:, n, k:k + 1].bitcast(U32), 0),
                                            xn[:, n // GT, n % GT], None).then_inc(scattered.sem, 16)

        def shares_vector(dve, ch):
            r = route[7]
            top, share, total = r["top"][:, :, 0:K4], r["share"], r["total"]
            ch.step(dve.tensor_tensor(share, top, top[:, :, 0:1].broadcast_to([P, T, K4]), ALU.subtract))
            ch.settle()
            dve.tensor_copy(total[:, T:T + 1], gain(7)).then_inc(shares_shifted, 1)
            dve.wait_ge(shares_exp, 1)
            ch.step(dve.tensor_reduce(total[:, 0:T], share, AX.X, ALU.add))
            ch.settle()
            ch.step(dve.reciprocal(total[:, 0:T], total[:, 0:T]))
            ch.settle()
            ch.step(dve.tensor_scalar(total[:, 0:T], total[:, 0:T], gain(7), None, ALU.mult))
            ch.settle()
            ch.step(dve.tensor_tensor(share, share, total[:, 0:T].unsqueeze(2).broadcast_to([P, T, K4]), ALU.mult))

        def shared_tensor(pe):
            def hidden(k):
                g, h = k // 4, k % 4
                if k >= 2:
                    pe.wait_ge(shared_hid, k - 1)
                for j, w in enumerate((sgate, sup)):
                    for c in range(C):
                        ins = pe.matmul(bank[2 * (k % 2) + j], w[:, c, h * P:(h + 1) * P], place(7, g)[:, c],
                                        start=(c == 0), stop=(c == C - 1))
                ins.then_inc(shared_done, 1)

            def down(g):
                pe.wait_ge(shared_hid, 4 * (g + 1))
                for t in range(GT):
                    if g and t % 2 == 0:
                        pe.wait_ge(shared_added, 2 * (g - 1) + t // 2 + 1)
                    for h in range(4):
                        ins = pe.matmul(bank[6 + t // 2][:, (t % 2) * D:(t % 2 + 1) * D], hshared[:, h, t * P:(t + 1) * P],
                                        sdown[:, h], start=(h == 0), stop=(h == 3))
                    if t % 2:
                        ins.then_inc(shared_down, 1)

            pe.wait_ge(*slots_ready.at(7, 1))
            pe.wait_ge(*expert_ready.at(7, 1))
            pe.wait_ge(*logits_read.at(7, G))
            for k in range(4 * G):
                hidden(k)
                if k and k % 4 == 0:
                    down(k // 4 - 1)
            down(G - 1)

        def shared_scalar(act):
            act.wait_ge(shares_shifted, 1)
            act.activation(route[7]["share"], route[7]["share"], ACT.Exp).then_inc(shares_exp, 1)
            for k in range(4 * G):
                act.wait_ge(shared_done, k + 1)
                act.activation(tanh_s[:, k % 2], bank[2 * (k % 2)], ACT.Tanh, scale=0.5).then_inc(shared_tanh, 1)

        def shared_vector(dve, ch):
            def add(g):
                for half in range(2):
                    dve.wait_ge(shared_down, 2 * g + half + 1)
                    t0 = g * GT + 2 * half
                    xs = x_tok[:, t0:t0 + 2].rearrange("p t d -> p (t d)")
                    dve.scalar_tensor_tensor(xs, bank[6 + half], gain(7), xs, ALU.mult, ALU.add).then_inc(shared_added, 1)

            for k in range(4 * G):
                g, h = k // 4, k % 4
                dve.wait_ge(shared_tanh, k + 1)
                ch.step(dve.scalar_tensor_tensor(tanh_s[:, k % 2], tanh_s[:, k % 2], 1.0, bank[2 * (k % 2)], ALU.add, ALU.mult))
                if h == 0 and g:
                    dve.wait_ge(shared_down, 2 * g)
                ch.settle()
                dve.scalar_tensor_tensor(hshared[:, h], tanh_s[:, k % 2], 0.5, bank[2 * (k % 2) + 1], ALU.mult,
                                         ALU.mult).then_inc(shared_hid, 1)
                if h == 0 and g:
                    add(g - 1)
            add(G - 1)

        def quads_sync(sp):
            def load(q, u):
                sp.dma_start(qin[:, u], xs7[bass.ds(q * 4 * P, 4 * P), :].rearrange("(t p) d -> p t d", p=P)
                             ).then_inc(in_loaded[u].sem, 16)

            def store(q, u):
                sp.dma_start(ys7[bass.ds(q * 4 * P, 4 * P), :].rearrange("(t p) d -> p t d", p=P),
                             qout[:, u].rearrange("p (t d) -> p t d", d=D)).then_inc(stored[u].sem, 16)

            sp.wait_ge(*scattered.at(7, T * K4 * 16))
            load(0, 0)
            load(1, 1)
            with sp.Fori(0, NQ // 2 - 1) as j:
                for u in range(2):
                    sp.wait_ge(*in_turned.at(7, 4 * j + 2 * u + 2))
                    load(2 * j + u + 2, u)
                    sp.wait_ge(*out_ready.at(7, 2 * j + u + 1))
                    store(2 * j + u, u)
            for u in range(2):
                sp.wait_ge(*out_ready.at(7, NQ - 1 + u))
                store(NQ - 2 + u, u)

        def quads_tensor(pe):
            ex = route[7]["expert"]

            def expert_of(i):
                return pe.value_load(ex[0:1, bass.ds(i, 1)], min_val=0, max_val=E4 - 1)

            def turn_in(u, turn):
                pe.wait_ge(*in_loaded[u].at(7, 16 * turn + 16))
                for c in range(C):
                    for t in range(4):
                        ins = pe.transpose(bank[c][:, t * P:(t + 1) * P], qin[:, u, t, c * P:(c + 1) * P], ident[:])
                    ins.then_inc(in_turned.sem, 1)

            def hidden(q, u):
                experts = [expert_of(4 * q + t) for t in range(4)]
                pe.wait_ge(*inT_ready.at(7, 2 * q + 2))
                for t, e in enumerate(experts):
                    for c in range(C):
                        ins = pe.matmul(bank[2 + t // 2][:, (t % 2) * 2 * F4:(t % 2 + 1) * 2 * F4],
                                        qinT[:, u, c, t * P:(t + 1) * P],
                                        arena[:, bass.ds(e * (C * 2 * F4) + c * 2 * F4, 2 * F4)],
                                        start=(c == 0), stop=(c == C - 1))
                ins.then_inc(hidden_done.sem, 1)

            def turn_hidden(q, u):
                pe.wait_ge(qhid_ready, q + 1)
                for t in range(4):
                    ins = pe.transpose(bank[4][:, t * P:(t + 1) * P], qhid[:, u, t], ident[:])
                ins.then_inc(hidden_turned.sem, 1)

            def output(q, u, first=False):
                experts = [expert_of(4 * q + t) for t in range(4)]
                if not first:
                    pe.wait_ge(*out_ready.at(7, q))
                pe.wait_ge(qhidT_ready, q + 1)
                for t, e in enumerate(experts):
                    ins = pe.matmul(bank[6 + t // 2][:, (t % 2) * D:(t % 2 + 1) * D], qhidT[:, u, t * P:(t + 1) * P],
                                    arena[:, bass.ds(e * D + DOWN0, D)], start=True, stop=True)
                ins.then_inc(out_done.sem, 1)

            def step(q, u, turn, first=False):
                turn_in(1 - u, turn)
                turn_hidden(q, u)
                hidden(q + 1, 1 - u)
                output(q, u, first)

            pe.wait_ge(w7_loaded, 8 * 16)
            turn_in(0, 0)
            pe.wait_ge(shared_hid, 4 * G)
            hidden(0, 0)
            pe.wait_ge(shared_added, 2 * G)
            step(0, 0, 0, first=True)
            with pe.Fori(0, NQ // 2 - 1) as j:
                step(2 * j + 1, 1, j + 1)
                step(2 * j + 2, 0, j + 1)
            turn_hidden(NQ - 1, 1)
            output(NQ - 1, 1)

        def quads_scalar(act):
            def copy_in(q, u):
                for c in range(C):
                    act.wait_ge(*in_turned.at(7, 2 * q + c + 1))
                    act.activation(qinT[:, u, c], bank[c], ACT.Copy).then_inc(inT_ready.sem, 1)

            def tanh_gate(q, u):
                act.wait_ge(*hidden_done.at(7, q + 1))
                gate = psum[:, 2:4].rearrange("p b (t w n) -> p (b t) w n", t=2, w=2)[:, :, 0]
                act.activation(qtanh[:, u], gate, ACT.Tanh, scale=0.5).then_inc(qtanh_ready, 1)

            def copy_hidden(q, u):
                act.wait_ge(*hidden_turned.at(7, q + 1))
                act.activation(qhidT[:, u], bank[4], ACT.Copy).then_inc(qhidT_ready, 1)

            copy_in(0, 0)
            tanh_gate(0, 0)
            with act.Fori(0, NQ // 2 - 1) as j:
                for u in range(2):
                    copy_in(2 * j + u + 1, 1 - u)
                    copy_hidden(2 * j + u, u)
                    tanh_gate(2 * j + u + 1, 1 - u)
            copy_in(NQ - 1, 1)
            copy_hidden(NQ - 2, 0)
            tanh_gate(NQ - 1, 1)
            copy_hidden(NQ - 1, 1)

        def quads_vector(dve):
            up = psum[:, 2:4].rearrange("p b (t w n) -> p (b t) w n", t=2, w=2)[:, :, 1]
            gate = psum[:, 2:4].rearrange("p b (t w n) -> p (b t) w n", t=2, w=2)[:, :, 0]

            def hidden(q, u):
                dve.wait_ge(qtanh_ready, q + 1)
                dve.scalar_tensor_tensor(qtanh[:, u], qtanh[:, u], 1.0, gate, ALU.add, ALU.mult).then_inc(qgate_ready, 1)
                dve.wait_ge(qgate_ready, q + 1)
                dve.scalar_tensor_tensor(qhid[:, u], qtanh[:, u], 0.5, up, ALU.mult, ALU.mult).then_inc(qhid_ready, 1)

            def copy_out(q, u):
                dve.wait_ge(*out_done.at(7, q + 1))
                dve.tensor_copy(qout[:, u], psum[:, 6:8].rearrange("p b n -> p (b n)")).then_inc(out_ready.sem, 1)

            hidden(0, 0)
            hidden(1, 1)
            copy_out(0, 0)
            hidden(2, 0)
            copy_out(1, 1)
            with dve.Fori(1, NQ // 2 - 1) as j:
                hidden(2 * j + 1, 1)
                dve.wait_ge(*stored[0].at(7, 16 * j))
                copy_out(2 * j, 0)
                hidden(2 * j + 2, 0)
                dve.wait_ge(*stored[1].at(7, 16 * j))
                copy_out(2 * j + 1, 1)
            hidden(NQ - 1, 1)
            for u in range(2):
                dve.wait_ge(*stored[u].at(7, 16 * (NQ // 2 - 1)))
                copy_out(NQ - 2 + u, u)

        def gather7_gpsimd(pool):
            for u in range(2):
                pool.wait_ge(*stored[u].at(7, NQ // 2 * 16))
            for n in range(T):
                for k in range(K4):
                    pool.indirect_dma_start(gathered7[:, n, k], None, ys7,
                                            bass.IndirectOffsetOnAxis(route[7]["slot_i"][:, n, k:k + 1].bitcast(U32), 0)
                                            ).then_inc(gathered7_in[n // GT], 16)

        def combine7_vector(dve, ch):
            dve.wait_ge(shared_added, 2 * G)
            ch.settle()
            for g in range(G):
                dve.wait_ge(gathered7_in[g], 16 * GT * K4)
                for k in range(K4):
                    for n in range(g * GT, (g + 1) * GT):
                        ins = dve.scalar_tensor_tensor(x_tok[:, n], gathered7[:, n, k], route[7]["share"][:, n, k:k + 1],
                                                       x_tok[:, n], ALU.mult, ALU.add)
                        if k < K4 - 1:
                            ch.step(ins)
                    ch.settle()
                ins.then_inc(x_done.sem, 1)

        def expert_tiles_sync(sp):
            def load(i, u, turn):
                sp.dma_start(xin[:, u], xs5[bass.ds(i * P, P), :]).then_inc(in_loaded[u].sem, 16)

            def store(i, u):
                sp.dma_start(ys5[bass.ds(i * P, P), :], yout[:, u]).then_inc(stored[u].sem, 16)

            sp.wait_ge(*scattered.at(5, T * 16))
            load(0, 0, 0)
            load(1, 1, 0)
            with sp.Fori(0, NT2 // 2 - 1) as j:
                for u in range(2):
                    sp.wait_ge(*in_turned.at(5, 2 * j + u + 1))
                    load(2 * j + u + 2, u, j)
                    sp.wait_ge(*out_ready.at(5, 2 * j + u + 1))
                    store(2 * j + u, u)
            for u in range(2):
                sp.wait_ge(*out_ready.at(5, NT2 - 1 + u))
                store(NT2 - 2 + u, u)

        def expert_tiles_tensor(pe):
            ex = route[5]["expert"]

            def turn_in(i, u, j):
                pe.wait_ge(*in_loaded[u].at(5, 16 * j + 16))
                for c in range(C):
                    ins = pe.transpose(bank[0][:, c * P:(c + 1) * P], xin[:, u, c * P:(c + 1) * P], ident[:])
                ins.then_inc(in_turned.sem, 1)

            def hidden(i, u, e):
                pe.wait_ge(*inT_ready.at(5, i + 1))
                for h in range(2):
                    for c in range(C):
                        ins = pe.matmul(bank[2 + h], xinT[:, u, c * P:(c + 1) * P],
                                        W1[:, e, c * F2 + h * 512:c * F2 + h * 512 + 512] if isinstance(e, int) else
                                        arena[:, bass.ds(e * (C * F2) + (c * F2 + h * 512), 512)],
                                        start=(c == 0), stop=(c == C - 1))
                ins.then_inc(hidden_done.sem, 1)

            def turn_hidden(i, u):
                pe.wait_ge(hpre_copied, i + 1)
                for k in range(8):
                    ins = pe.transpose(bank[4 + k // 4][:, k % 4 * P:(k % 4 + 1) * P], hpre[:, u, k * P:(k + 1) * P], ident[:])
                    if k % 4 == 3:
                        ins.then_inc(hidden_turned.sem, 1)

            def output(i, u, e):
                pe.wait_ge(h_act, (i + 1) * 2)
                for k in range(8):
                    ins = pe.matmul(bank[6 + u][:, 0:D], hact[:, u, k * P:(k + 1) * P],
                                    arena[:, bass.ds(e * (8 * D) + (E2 * C * F2 + k * D), D)], start=(k == 0), stop=(k == 7))
                ins.then_inc(out_done.sem, 1)

            def expert_of(i):
                return pe.value_load(ex[0:1, bass.ds(i, 1)], min_val=0, max_val=E2 - 1)

            pe.wait_ge(*expert_ready.at(5, 1))
            pe.wait_ge(*logits_read.at(5, G))
            pe.wait_ge(*slots_ready.at(5, 1))
            pe.wait_ge(expert5_loaded, 2 * E2 * 16)
            turn_in(0, 0, 0)
            hidden(0, 0, expert_of(0))
            turn_hidden(0, 0)

            def step(i, u, j):
                turn_in(i, u, j)
                hidden(i, u, expert_of(i))
                output(i - 1, 1 - u, expert_of(i - 1))
                turn_hidden(i, u)

            with pe.Fori(0, NT2 // 2 - 1) as j:
                step(2 * j + 1, 1, j)
                step(2 * j + 2, 0, j + 1)
            step(NT2 - 1, 1, NT2 // 2 - 1)
            output(NT2 - 1, 1, expert_of(NT2 - 1))

        def expert_tiles_scalar(act):
            ex = route[5]["expert"]
            act.wait_ge(*expert_ready.at(5, 1))
            with act.Fori(0, NT2 // 2) as j:
                for u in range(2):
                    i = 2 * j + u
                    e = act.value_load(ex[0:1, bass.ds(i, 1)], min_val=0, max_val=E2 - 1)
                    act.wait_ge(*in_turned.at(5, i + 1))
                    act.activation(xinT[:, u], bank[0][:, 0:C * P], ACT.Copy).then_inc(inT_ready.sem, 1)
                    for k in range(8):
                        if k % 4 == 0:
                            act.wait_ge(*hidden_turned.at(5, 2 * i + k // 4 + 1))
                        ins = act.activation(hact[:, u, k * P:(k + 1) * P], bank[4 + k // 4][:, k % 4 * P:(k % 4 + 1) * P],
                                             ACT.Relu, bias=b1col[:, bass.ds(e * 8 + k, 1)])
                        if k % 4 == 3:
                            ins.then_inc(h_act, 1)

        def expert_tiles_vector(dve):
            ex = route[5]["expert"]

            def copy_hidden(i, u):
                dve.wait_ge(*hidden_done.at(5, i + 1))
                dve.tensor_copy(hpre[:, u], psum[:, 2:4].rearrange("p b n -> p (b n)")).then_inc(hpre_copied, 1)

            def copy_out(i, u):
                e = dve.value_load(ex[0:1, bass.ds(i, 1)], min_val=0, max_val=E2 - 1)
                dve.wait_ge(*out_done.at(5, i + 1))
                dve.tensor_tensor(yout[:, u], bank[6 + u][:, 0:D], b2row[:, bass.ds(e * D, D)], ALU.add).then_inc(out_ready.sem, 1)

            dve.wait_ge(w5_loaded, 4 * 16)
            dve.wait_ge(*expert_ready.at(5, 1))
            dve.wait_ge(*scattered.at(5, T * 16))
            def steps(j):
                copy_hidden(2 * j + 1, 1)
                dve.wait_ge(*stored[0].at(5, 16 * j))
                copy_out(2 * j, 0)
                copy_hidden(2 * j + 2, 0)
                dve.wait_ge(*stored[1].at(5, 16 * j))
                copy_out(2 * j + 1, 1)

            copy_hidden(0, 0)
            copy_hidden(1, 1)
            copy_out(0, 0)
            copy_hidden(2, 0)
            copy_out(1, 1)
            with dve.Fori(1, NT2 // 2 - 1) as j:
                steps(j)
            copy_hidden(NT2 - 1, 1)
            for u in range(2):
                dve.wait_ge(*stored[u].at(5, 16 * (NT2 // 2 - 1)))
                copy_out(NT2 - 2 + u, u)

        def gather_gpsimd(pool):
            for u in range(2):
                pool.wait_ge(*stored[u].at(5, NT2 // 2 * 16))
            for n in range(T):
                pool.indirect_dma_start(gathered5[:, n], None, ys5,
                                        bass.IndirectOffsetOnAxis(route[5]["slot_i"][:, n, 0:1].bitcast(U32), 0)
                                        ).then_inc(gathered5_in[n // GT], 16)

        def combine_vector(dve, ch):
            for n in range(T):
                if n % GT == 0:
                    dve.wait_ge(gathered5_in[n // GT], 16 * GT)
                ins = dve.scalar_tensor_tensor(x_tok[:, n], gathered5[:, n], gain(5), x_tok[:, n], ALU.mult,
                                         ALU.add)
                if n % GT == GT - 1:
                    ins.then_inc(x_done.sem, 1)
                    next_norm(dve, ch, 5, n // GT)

        def single_context_tensor(pe):
            pe.wait_ge(max_found, 3)
            pe.wait_ge(*inT_ready.at(5, NT2))
            pe.wait_ge(*out_ready.at(5, NT2))
            pe.transpose(bank[0][0:3, 0:P], max6[:, 0:3], ident[:]).then_inc(max_turned, 1)
            pe.wait_ge(max_diag, 1)
            pe.matmul(bank[1][:, 0:3], ones[0:3], max6[0:3, 4:7], start=True, stop=True).then_inc(max_spread, 1)
            pe.wait_ge(w6_rounded, 1)
            for o in range(C):
                for c in range(C):
                    ins = pe.matmul(bank[2 + o][:, 0:BM], w6[:, 0, c, o * P:(o + 1) * P], ctxT[:, c],
                                    start=(c == 0), stop=(c == C - 1))
                ins.then_inc(kp_done, 1)
            pe.wait_ge(w6_rounded, 2)
            for b in range(B):
                for c in range(C):
                    ins = pe.matmul(bank[7][:, b * D:(b + 1) * D], ctxT[:, c, b * M:b * M + P], w6[:, 1, c],
                                    start=(c == 0), stop=(c == C - 1))
            ins.then_inc(ctx6_done, 1)
            for b in range(B):
                for c in range(C):
                    ins = pe.matmul(bank[0][0:MR, b * D:(b + 1) * D], ctxT[:, c, b * M + P:(b + 1) * M], w6[:, 1, c],
                                    start=(c == 0), stop=(c == C - 1))
            ins.then_inc(ctx6_done, 1)
            pe.wait_ge(w6_rounded, 3)
            pe.wait_ge(kp_ready, C)
            for o in range(C):
                for c in range(C):
                    ins = pe.matmul(bank[4 + o][:, 0:BM], w6[:, 2, c, o * P:(o + 1) * P], kpT6[:, c],
                                    start=(c == 0), stop=(c == C - 1))
                ins.then_inc(ctx6_done, 1)
            for c in range(C):
                ins = pe.matmul(bank[6][:, 0:BM], bq6[:, c], kpT6[:, c], start=(c == 0), stop=(c == C - 1))
            ins.then_inc(ctx6_done, 1)

        def single_context_scalar(act):
            act.wait_ge(w6_loaded, 4 * 16)
            for o in range(C):
                act.wait_ge(kp_done, o + 1)
                act.activation(kpT6[:, o], bank[2 + o][:, 0:BM], ACT.Identity, bias=vec6[:, 1, o:o + 1]).then_inc(kp_ready, 1)

        def single_context_vector(dve, ch):
            dve.wait_ge(w6_loaded, 4 * 16)
            for k in range(3):
                dve.tensor_reduce(max6[:, k:k + 1], w6[:, k].rearrange("p c n -> p (c n)"), AX.X, ALU.max,
                                  apply_absolute_value=True).then_inc(max_found, 1)
            for c in range(C):
                ch.step(dve.tensor_scalar(bq6[:, c], ones[:], vec6[:, 0, c:c + 1], None, ALU.mult))
            dve.wait_ge(max_turned, 1)
            ch.step(dve.tensor_reduce(max6[0:3, 3:4], bank[0][0:3, 0:P], AX.X, ALU.max))
            ch.settle()
            dve.tensor_scalar(max6[0:3, 4:7], ident[0:3, 0:3], max6[0:3, 3:4], None, ALU.mult).then_inc(max_diag, 1)
            dve.wait_ge(max_spread, 1)
            ch.step(dve.tensor_scalar(max6[:, 8:11], bank[1][:, 0:3], 1.0 / 128, None, ALU.mult))
            ch.settle()
            ch.step(dve.reciprocal(max6[:, 12:15], max6[:, 8:11]))
            ch.settle()
            for k in range(3):
                w = w6[:, k].rearrange("p c n -> p (c n)")
                ch.step(dve.tensor_scalar(w, w, max6[:, 12 + k:13 + k], ROUND, ALU.mult, ALU.add))
                ch.settle()
                dve.tensor_scalar(w, w, -ROUND, max6[:, 8 + k:9 + k], ALU.add, ALU.mult).then_inc(w6_rounded, 1)
            dve.wait_ge(ctx6_done, 1)
            dve.tensor_copy(vals6.rearrange("p b n -> p (b n)"), bank[7]).then_inc(ctx6_ready, 1)
            dve.wait_ge(ctx6_done, 2)
            dve.tensor_copy(vals6R[0:MR].rearrange("p b n -> p (b n)"), bank[0][0:MR]).then_inc(ctx6_ready, 1)
            for o in range(C):
                dve.wait_ge(ctx6_done, 3 + o)
                dve.tensor_copy(kq6[:, o], bank[4 + o][:, 0:BM]).then_inc(ctx6_ready, 1)
            dve.wait_ge(ctx6_done, 5)
            dve.tensor_copy(bias6, bank[6][:, 0:BM]).then_inc(ctx6_ready, 1)

        def single_tensor(pe):
            def scores(g):
                b = g // GB
                turn_group(pe, 6, g)
                pe.wait_ge(*xnT_ready.at(6, (g + 1) * C))
                if g == 0:
                    pe.wait_ge(ctx6_ready, 5)
                else:
                    pe.wait_ge(scores_read6, 2 * g)
                for t in range(GT):
                    for c in range(C):
                        ins = pe.matmul(bank[2 + t // 2][:, (t % 2) * M:(t % 2 + 1) * M], xnT[:, g % 2, c, t * P:(t + 1) * P],
                                        kq6[:, c, b * M:(b + 1) * M], start=(c == 0), stop=(c == C - 1))
                    if t % 2:
                        ins.then_inc(scored6, 1)

            pe.wait_ge(ctx6_ready, 2)
            scores(0)
            for g in range(G):
                if g + 1 < G:
                    scores(g + 1)
                u, b = g % 2, g // GB
                pe.wait_ge(exp_ready6, g + 1)
                if g:
                    pe.wait_ge(main_copied6, g)
                for t in range(GT):
                    ins = pe.transpose(bank[4][:, t * P:(t + 1) * P], sc6[:, u, t, 0:P], ident[:])
                ins.then_inc(turned6, 1)
                if g:
                    pe.wait_ge(rest_copied6, g)
                for t in range(GT):
                    ins = pe.transpose(bank[5][0:MR, t * P:(t + 1) * P], sc6[:, u, t, P:M], ident[:])
                ins.then_inc(turned6, 1)
                pe.wait_ge(main_copied6, g + 1)
                pe.wait_ge(rest_copied6, g + 1)
                if g:
                    pe.wait_ge(*x_done.at(6, g))
                for t in range(GT):
                    dst = bank[6 + t // 2][:, (t % 2) * D:(t % 2 + 1) * D]
                    pe.matmul(dst, probs6T[:, u, t * P:(t + 1) * P], vals6[:, b], start=True, stop=False)
                    ins = pe.matmul(dst, probs6R[0:MR, u, t * P:(t + 1) * P], vals6R[0:MR, b], start=False, stop=True)
                    if t % 2:
                        ins.then_inc(pv_done6, 1)

        def single_scalar(act):
            def copy_group(g):
                if g >= 2:
                    act.wait_ge(scored6, 2 * (g - 1))
                copy_turned(act, 6, g, xnT[:, g % 2])

            copy_group(0)
            for g in range(G):
                if g + 1 < G:
                    copy_group(g + 1)
                u = g % 2
                act.wait_ge(max_ready6, g + 1)
                for t in range(GT):
                    ins = act.activation(sc6[:, u, t], sc6[:, u, t], ACT.Exp, bias=col6[:, u, 1, t:t + 1], scale=D ** -0.5,
                                         accum_out=col6[:, u, 2, t:t + 1])
                ins.then_inc(exp_ready6, 1)
                act.wait_ge(turned6, 2 * g + 1)
                if g >= 2:
                    act.wait_ge(pv_done6, 2 * (g - 1))
                act.activation(probs6T[:, u], bank[4], ACT.Copy).then_inc(main_copied6, 1)

        def single_vector(dve, ch):
            def scores(g):
                u, b = g % 2, g // GB
                if g >= 2:
                    dve.wait_ge(turned6, 2 * (g - 1))
                for half in range(2):
                    dve.wait_ge(scored6, 2 * g + half + 1)
                    dve.tensor_tensor(sc6[:, u, 2 * half:2 * half + 2],
                                      bank[2 + half][:, 0:2 * M].rearrange("p (t m) -> p t m", t=2),
                                      bias6[:, b * M:(b + 1) * M].unsqueeze(1).broadcast_to([P, 2, M]),
                                      ALU.add).then_inc(scores_read6, 1)
                dve.wait_ge(scores_read6, 2 * (g + 1))
                ch.step(dve.tensor_reduce(col6[:, u, 0], sc6[:, u], AX.X, ALU.max))
                ch.settle()
                dve.tensor_scalar(col6[:, u, 1], col6[:, u, 0], -D ** -0.5, None, ALU.mult).then_inc(max_ready6, 1)

            scores(0)
            for g in range(G):
                if g + 1 < G:
                    scores(g + 1)
                u = g % 2
                dve.wait_ge(exp_ready6, g + 1)
                ch.step(dve.reciprocal(col6[:, u, 3], col6[:, u, 2]))
                ch.settle()
                ch.step(dve.tensor_scalar(col6[:, u, 3], col6[:, u, 3], gain(6), None, ALU.mult))
                dve.wait_ge(turned6, 2 * g + 2)
                if g >= 2:
                    dve.wait_ge(pv_done6, 2 * (g - 1))
                dve.tensor_copy(probs6R[0:MR, u], bank[5][0:MR]).then_inc(rest_copied6, 1)
                dve.wait_ge(*row_added.at(6, g + 1))
                ch.settle()
                for t in range(GT):
                    dve.wait_ge(pv_done6, 2 * g + t // 2 + 1)
                    xs = x_tok[:, g * GT + t]
                    ins = dve.scalar_tensor_tensor(xs, bank[6 + t // 2][:, (t % 2) * D:(t % 2 + 1) * D], col6[:, u, 3, t:t + 1],
                                                   xs, ALU.mult, ALU.add)
                ins.then_inc(x_done.sem, 1)
                next_norm(dve, ch, 6, g)

        def rsqrt_newton(ch, v, y, t):
            dve = nc.vector
            ch.step(dve.tensor_scalar(y.bitcast(I32), v.bitcast(I32), -0.5, float(RSQRT_MAGIC), ALU.mult, ALU.add))
            for _ in range(NEWTON):
                ch.settle()
                ch.step(dve.tensor_tensor(t, y, y, ALU.mult))
                yield
                ch.settle()
                ch.step(dve.scalar_tensor_tensor(t, t, -0.5, v, ALU.mult, ALU.mult))
                yield
                ch.settle()
                ch.step(dve.scalar_tensor_tensor(y, t, 1.5, y, ALU.add, ALU.mult))
                yield
            ch.settle()

        def layer_norm_parts(dve, ch, s, g):
            u = g % 2
            for t in range(GT):
                ch.step(dve.bn_stats(stats[:, u, t], x_tok[:, g * GT + t]))
                yield
            ch.settle()
            for t in range(GT):
                ch.step(dve.bn_aggr(meanvar[:, u, t], stats[:, u, t]))
            yield
            ch.settle()
            v, y, t_ = (nwt[:, u, k, 0:GT] for k in range(3))
            ch.step(dve.tensor_scalar(v, meanvar[:, u, :, 1], LN_EPS, None, ALU.add))
            yield
            ch.settle()
            yield from rsqrt_newton(ch, v, y, t_)
            for t in range(GT):
                ins = dve.tensor_scalar(xn[:, g, t], x_tok[:, g * GT + t], meanvar[:, u, t, 0:1],
                                        nwt[:, u, 1, t:t + 1], ALU.subtract, ALU.mult)
                if t == GT - 1:
                    ins.then_inc(xn_ready.sem, 1)
                yield

        def layer_norm(dve, ch, s, g):
            for _ in layer_norm_parts(dve, ch, s, g):
                pass

        def turn_group(pe, s, g):
            pe.wait_ge(*xn_ready.at(s, g + 1))
            for c in range(C):
                if g >= 1:
                    pe.wait_ge(*xnT_ready.at(s, (g - 1) * C + c + 1))
                for t in range(GT):
                    ins = pe.transpose(bank[c][:, t * P:(t + 1) * P], xn[:, g, t, c * P:(c + 1) * P], ident[:])
                ins.then_inc(turned.sem, 1)

        def copy_turned(act, s, g, dst):
            for c in range(C):
                act.wait_ge(*turned.at(s, g * C + c + 1))
                act.activation(dst[:, c], bank[c][:], ACT.Copy).then_inc(xnT_ready.sem, 1)

        def gain(s):
            k = (4 if s % 2 else 0) + s // 2
            return tanh_g[:, k:k + 1]


        def slot_iterations_gpsimd(pool):
            pool.wait_ge(*xnT_ready.at(0, G * C))
            pool.sem_inc(h_ready, 8)
            with pool.Fori(0, ITERS) as it:
                for q in range(G):
                    pool.wait_ge(h_ready, it * 8 + 2 * q + 2)
                    if q >= 2:
                        pool.wait_ge(ms_ready, it * G + q - 1)
                    pool.tensor_tensor(sq[:, q % 2], hT[:, :, q * GN:(q + 1) * GN], hT[:, :, q * GN:(q + 1) * GN],
                                       ALU.mult).then_inc(sq_ready, 1)
                for b in range(B):
                    pool.wait_ge(sinv_ready, it * B + b + 1)
                    if b == 0:
                        pool.wait_ge(h_ready, it * 8 + 8)
                    pool.tensor_tensor(vWs[:, b], vW[:, b], sinv[:, 0, b:b + 1].broadcast_to([P, 3 * D]), ALU.mult)
                    pool.tensor_tensor(vWsr[0:MR, b], vWr[0:MR, b], sinv[0:MR, 1, b:b + 1].broadcast_to([MR, 3 * D]),
                                       ALU.mult).then_inc(vws_ready, 1)

        def mha_constants_gpsimd(pool):
            pool.wait_ge(*x_done.at(0, G))
            pool.memset(ctxR, 0.0).then_inc(ctxR_made, 1)
            pool.memset(vals, 0.0).then_inc(ctxR_made, 1)
            pool.memset(valsR, 0.0).then_inc(ctxR_made, 1)
            pool.memset(probsR, 0.0).then_inc(ctxR_made, 1)
            pool.wait_ge(ctxR_made, 1)
            for c in range(C):
                for b in range(B):
                    pool.tensor_copy(ctxR[:, c, b].rearrange("p (q m) -> p q m", q=4)[:, :, 0:MR],
                                     ctxT[:, c, b * M + P:(b + 1) * M].unsqueeze(1).broadcast_to([P, 4, MR])
                                     ).then_inc(ctxR_made, 1)

        def mha_gpsimd(pool, l, k):
            s = 2 + 2 * l
            for n in range(T):
                u = n % 2
                if n % GT == 0:
                    add_row_gpsimd(pool, s, k, n // GT)
                for half in range(2):
                    hs = slice(8 * half, 8 * half + 8)
                    pool.wait_ge(*half_sums.at(s, 2 * n + half + 1))
                    pool.tensor_tensor(probs[:, u, hs, 0:P], probs[:, u, hs, 0:P],
                                       rsum[:, u, hs].unsqueeze(2).broadcast_to([P, 8, P]), ALU.mult)
                    if half == 0 and n >= 2:
                        pool.wait_ge(*ring_filled.at(s, ring["weights", n - 2, 4] + 1))
                    pool.tensor_tensor(probsR[:, u, hs, 0:MR], probs[:, u, hs, P:M],
                                       rsum[:, u, hs].unsqueeze(2).broadcast_to([P, 8, MR]), ALU.mult).then_inc(half_scaled.sem, 1)

        def add_rows_gpsimd(pool, s, k):
            for g in range(G):
                add_row_gpsimd(pool, s, k, g)

        def add_row_gpsimd(pool, s, k, g):
            pool.wait_ge(*xn_ready.at(s, g + 1))
            xs = x_tok[:, g * GT:(g + 1) * GT]
            pool.tensor_tensor(xs, xs, add_row[:, k].unsqueeze(1).broadcast_to([P, GT, D]), ALU.add).then_inc(row_added.sem, 1)


        def start_slots_tensor(pe):
            for g in range(G):
                turn_group(pe, 0, g)

        def context_slots_tensor(pe):
            pe.wait_ge(*xnT_ready.at(0, G * C))
            pe.wait_ge(c_sq, 1)
            for c in range(C):
                ins = pe.matmul(bank[0][:, 0:BM], ones[:], sq[:, 0, c, 0:BM], start=(c == 0), stop=(c == C - 1))
            ins.then_inc(c_ms, 1)
            pe.wait_ge(w0_loaded, 6 * 16)
            pe.wait_ge(c_pn, C)
            for w in range(2):
                for o in range(C):
                    for c in range(C):
                        ins = pe.matmul(bank[1 + 2 * w + o][:, 0:BM], wqkv0[:, 1 + w, c, o * P:(o + 1) * P],
                                        PnT[:, c], start=(c == 0), stop=(c == C - 1))
                    ins.then_inc(c_kv, 1)
            pe.wait_ge(c_kv_copied, 4)
            for o in range(C):
                for c in range(C):
                    ins = pe.matmul(bank[1 + o][:, 0:BM], wqkv0[:, 0, c, o * P:(o + 1) * P], kvT[:, 0, c],
                                    start=(c == 0), stop=(c == C - 1))
                ins.then_inc(c_kq, 1)
            half = 3 * D // 2
            for b in range(B):
                for k, (lo, n) in enumerate(((0, P), (P, MR))):
                    j = b * 2 + k
                    if j >= 1:
                        pe.wait_ge(c_vw_copied, j)
                    for h in range(2):
                        for c in range(C):
                            ins = pe.matmul(bank[6 + h][0:n, 0:half], kvT[:, 1, c, b * M + lo:b * M + lo + n],
                                            wih[:, c, h * half:(h + 1) * half], start=(c == 0), stop=(c == C - 1))
                    ins.then_inc(c_vw, 1)

        def slot_iterations_tensor(pe):
            pe.wait_ge(c_kq_copied, C)
            pe.wait_ge(c_vw_copied, 4)
            with pe.Fori(0, ITERS) as it:
                def spread_group(q, j):
                    pe.wait_ge(diag_ready, it * 8 + j + 1)
                    if j >= 1:
                        pe.wait_ge(spread_copied, it * 8 + j)
                    pe.matmul(bank[1][:], ones[:], diag[:, q % 2], start=True, stop=True).then_inc(spread_ready, 1)

                for q in range(G):
                    pe.wait_ge(sq_ready, it * G + q + 1)
                    for t in range(GT):
                        for c in range(C):
                            ins = pe.matmul(bank[0][:, q * GT + t:q * GT + t + 1], sq[:, q % 2, c, t * P:(t + 1) * P],
                                            ones[:, 0:1], start=(c == 0), stop=(c == C - 1))
                    ins.then_inc(ms_ready, 1)
                for q in range(G):
                    if q == 3:
                        for k in range(G):
                            spread_group(k, k)
                    main, rem = (bank[2 + 2 * (q % 3)], bank[3 + 2 * (q % 3)])
                    if q == 3:
                        pe.wait_ge(scores_scaled, it * 8 + 2)
                    b = q // GB
                    for dst, lo, n in ((main, 0, P), (rem, P, MR)):
                        for c in range(C):
                            ins = pe.matmul(dst[0:n, :], kqT[:, c, b * M + lo:b * M + lo + n],
                                            hT[:, c, q * GN:(q + 1) * GN], start=(c == 0), stop=(c == C - 1))
                    ins.then_inc(scores_ready, 1)

                def gate_block(k, cols, w, rhs, start, stop):
                    ins = None
                    for n, (lhs, r) in enumerate(zip(w, rhs)):
                        ins = pe.matmul(bank[dict(hn=4, r=5, z=6, xn=7)[k]][:], lhs[:, cols], r,
                                        start=(start and n == 0), stop=(stop and n == len(w) - 1))
                    return ins

                def recurrent_part(q, o):
                    j = 2 * q + o
                    h = [hT[:, c, q * GN:(q + 1) * GN] for c in range(C)]
                    if j == 0:
                        pe.wait_ge(scores_scaled, it * 8 + 6)
                    for k, gate in (("hn", 2), ("r", 0), ("z", 1)):
                        if j >= 1:
                            pe.wait_ge(gate_read[k], it * 8 + j)
                        cols = slice(gate * D + o * P, gate * D + (o + 1) * P)
                        ins = gate_block(k, cols, [whh[:, c] for c in range(C)], h, True, k == "hn")
                        if k == "hn":
                            ins.then_inc(gate_done["hn"], 1)

                def input_part(q, o):
                    j, b = 2 * q + o, q // GB
                    n0 = (q % GB) * GN
                    e = [e_main[:, b, n0:n0 + GN], e_rem[0:MR, b, n0:n0 + GN]]
                    pe.wait_ge(attn_ready, it * G + q + 1)
                    for k, gate in (("r", 0), ("z", 1), ("xn", 2)):
                        if k == "xn" and j >= 1:
                            pe.wait_ge(gate_read["xn"], it * 8 + j)
                        cols = slice(gate * D + o * P, gate * D + (o + 1) * P)
                        gate_block(k, cols, [vWs[:, b], vWsr[0:MR, b]], e, k == "xn", True).then_inc(gate_done[k], 1)

                def row_sums(b):
                    pe.wait_ge(vws_ready, it * B + b + 1)
                    for t in range(S // P):
                        col = bank[0][:, T + b * 8 + t:T + b * 8 + t + 1]
                        pe.matmul(col, e_main[:, b, t * P:(t + 1) * P], sinv[:, 0, b:b + 1], start=True, stop=False)
                        ins = pe.matmul(col, e_rem[0:MR, b, t * P:(t + 1) * P], sinv[0:MR, 1, b:b + 1],
                                        start=False, stop=True)
                    ins.then_inc(rowsum_ready, 1)

                recurrent_part(0, 0)
                row_sums(0)
                spread_group(0, 4)
                spread_group(1, 5)
                input_part(0, 0)
                recurrent_part(0, 1)
                row_sums(1)
                input_part(0, 1)
                spread_group(2, 6)
                spread_group(3, 7)
                for q in range(1, G):
                    for o in range(C):
                        recurrent_part(q, o)
                        input_part(q, o)

        def finish_slots_tensor(pe):
            for q in range(G):
                pe.wait_ge(h_ready, 8 * ITERS + (2 * q + 2 if q < 2 else 8))
                for half in range(2):
                    k = 2 * q + half
                    for t in range(2):
                        for c in range(C):
                            n0 = q * GN + (half * 2 + t) * P
                            ins = pe.transpose(bank[k][:, t * D + c * P:t * D + (c + 1) * P],
                                               hT[:, c, n0:n0 + P], ident[:])
                    ins.then_inc(slotsT_ready, 1)

        def ternary_tensor(pe):
            pe.wait_ge(consts_made, 3)
            pe.wait_ge(tern_ready, 4)
            for g in range(G):
                u = g % 2
                pe.wait_ge(xq_ready, g + 1)
                if g == 0:
                    pe.wait_ge(*x_done.at(0, 1))
                for c in range(C):
                    if g >= 1:
                        pe.wait_ge(*xnT_ready.at(1, (g - 1) * C + c + 1))
                    for t in range(GT):
                        ins = pe.transpose(bank[c].bitcast(BF16)[:, t * P:(t + 1) * P],
                                           xq[:, u, t * D + c * P:t * D + (c + 1) * P], ident_bf[:])
                    ins.then_inc(turned.sem, 1)
                pe.wait_ge(*xnT_ready.at(1, (g + 1) * C))
                if g < 2:
                    pe.wait_ge(*x_done.at(0, G))
                else:
                    pe.wait_ge(*x_done.at(1, g - 1))
                for t in range(GT):
                    for c in range(C):
                        ins = pe.matmul(bank[4 + 2 * u + t // 2][:, (t % 2) * D:(t % 2 + 1) * D],
                                        qT[:, u, c, t * P:(t + 1) * P], tern[:, c], start=(c == 0), stop=(c == C - 1))
                ins.then_inc(project_ready.sem, 1)

        def mha_context_tensor(pe, l):
            s = 2 + 2 * l
            pe.wait_ge(wmha_loaded[l], 5 * 16)
            pe.wait_ge(*x_done.at(s - 1, G))
            for o in range(C):
                for c in range(C):
                    ins = pe.matmul(bank[2 + o][:, 0:BM], wmha[:, l, 1, c, o * P:(o + 1) * P], ctxT[:, c],
                                    start=(c == 0), stop=(c == C - 1))
                ins.then_inc(context_done.sem, 1)
            pe.wait_ge(ctxR_made, 4 + C * B)
            for b in range(B):
                for c in range(C):
                    ins = pe.matmul(bank[4 + b][:, 0:D], ctxT[:, c, b * M:b * M + P], wmha[:, l, 2, c],
                                    start=(c == 0), stop=(c == C - 1))
                ins.then_inc(context_done.sem, 1)
            for b in range(B):
                for c in range(C):
                    ins = pe.matmul(bank[6 + b][:, 0:D], ctxR[:, c, b], wmha[:, l, 2, c],
                                    start=(c == 0), stop=(c == C - 1))
                ins.then_inc(context_done.sem, 1)
            pe.wait_ge(*keys_ready.at(l, 1))
            pe.wait_ge(*bv_ready.at(l, C))
            for c in range(C):
                ins = pe.matmul(bank[2][:, 0:D], bvrow[:, c], wmha[:, l, 3, c], start=(c == 0), stop=(c == C - 1))
            ins.then_inc(context_done.sem, 1)

        def fill_ring(pe, s, op):
            r = ring[op]
            if r >= 2:
                pe.wait_ge(*ring_read[r % 2].at(s, r // 2))
            return bank[2 + r % 2]

        def mha_tensor(pe, l):
            s = 2 + 2 * l

            def turn(g):
                pe.wait_ge(*xn_ready.at(s, g + 1))
                for c in range(C):
                    dst = fill_ring(pe, s, ("turn", g, c))
                    for t in range(GT):
                        ins = pe.transpose(dst[:, t * P:(t + 1) * P], xn[:, g, t, c * P:(c + 1) * P], ident[:])
                    ins.then_inc(ring_filled.sem, 1)

            def query(g):
                for c in range(C):
                    r = ring["turn", g, c]
                    pe.wait_ge(*ring_read[r % 2].at(s, r // 2 + 1))
                for o in range(C):
                    dst = fill_ring(pe, s, ("query", g, o))
                    for c in range(C):
                        ins = pe.matmul(dst, wmha[:, l, 0, c, o * P:(o + 1) * P], xnT[:, g % 2, c],
                                        start=(c == 0), stop=(c == C - 1))
                    ins.then_inc(ring_filled.sem, 1)

            def score(n, k):
                g, t, b = n // GT, n % GT, n // (GT * GB)
                if t == 0 and k == 0:
                    for o in range(C):
                        r = ring["query", g, o]
                        pe.wait_ge(*ring_read[r % 2].at(s, r // 2 + 1))
                K = 4 * n + k
                if K >= 2:
                    pe.wait_ge(*pair_exp.at(s, K - 1))
                for j in range(2 * (k % 2), 2 * (k % 2) + 2):
                    rows = slice(32 * j, 32 * j + 32)
                    ins = pe.matmul(bank[4 + j][:, 0:2 * M], qhT[rows, g % 2, k // 2, t * P:(t + 1) * P],
                                    keys[rows, k // 2, b].rearrange("p h m -> p (h m)"), start=True, stop=True,
                                    tile_position=(32 * j, 0))
                ins.then_inc(pair_scored.sem, 1)

            def weights(n, k):
                u = n % 2
                if k in (0, 2, 4):
                    pe.wait_ge(*half_scaled.at(s, 2 * n + (1 if k == 0 else 2)))
                dst = fill_ring(pe, s, ("weights", n, k))
                for j in range(4):
                    src = probs[:, u, 4 * k + j, 0:P] if k < 4 else probsR[:, u, 4 * j:4 * j + 4].rearrange("p h m -> p (h m)")
                    ins = pe.transpose(dst[:, j * P:(j + 1) * P], src, ident[:])
                ins.then_inc(ring_filled.sem, 1)

            def values(n, c):
                g, t, b, u = n // GT, n % GT, n // (GT * GB), n % 2
                if t == 0 and g >= 1:
                    pe.wait_ge(*(x_done if c else half_added).at(s, g))
                if c == 0:
                    for k in (3, 4):
                        r = ring["weights", n, k]
                        pe.wait_ge(*ring_read[r % 2].at(s, r // 2 + 1))
                for h in range(8 * c, 8 * c + 8):
                    pe.matmul(bank[c][:, t * P:(t + 1) * P], vals[:, (b * H + h) * P:(b * H + h + 1) * P], probsT[:, u, h],
                              start=(h == 8 * c), stop=False)
                for q in range(2 * c, 2 * c + 2):
                    ins = pe.matmul(bank[c][:, t * P:(t + 1) * P], valsR[:, (b * 4 + q) * P:(b * 4 + q + 1) * P],
                                    probsT[:, u, 16 + q], start=False, stop=(q == 2 * c + 1))
                ins.then_inc(pv_done.sem, 1)

            def project(g):
                for c in range(C):
                    pe.wait_ge(*headsT_ready[c].at(s, g + 1))
                for t in range(GT):
                    for c in range(C):
                        ins = pe.matmul(bank[t // 2][:, (t % 2) * D:(t % 2 + 1) * D],
                                        headsT[:, g % 2, c, t * P:(t + 1) * P], wmha[:, l, 3, c],
                                        start=(c == 0), stop=(c == C - 1))
                    if t % 2:
                        ins.then_inc(half_projected.sem, 1)

            pe.wait_ge(*vals_ready.at(l, B))
            pe.wait_ge(*cvec_ready.at(l, 1))
            for n, ops in head_steps():
                for op in ops:
                    dict(turn=turn, query=query, score=score, weights=weights, values=values, project=project)[op[0]](*op[1:])

        def tri_fold_tensor(pe):
            pe.wait_ge(w3_loaded, 3 * 16)
            pe.wait_ge(*x_done.at(2, G))
            for k in range(2):
                if k:
                    pe.wait_ge(tri_copied, C)
                for o in range(C):
                    for c in range(C):
                        ins = pe.matmul(bank[2 + o][:, 0:D], wtri[:, 1 - k, c, o * P:(o + 1) * P],
                                        wtri[:, 2, c] if k == 0 else wtri12[:, 0, c], start=(c == 0), stop=(c == C - 1))
                    ins.then_inc(tri_folded, 1)
            pe.wait_ge(tri_copied, 2 * C)

        def tri_tensor(pe):
            for g in range(G):
                u = g % 2
                turn_group(pe, 3, g)
                pe.wait_ge(*xnT_ready.at(3, (g + 1) * C))
                if g >= 2:
                    pe.wait_ge(tri_summed, g - 1)
                for t in range(GT):
                    for c in range(C):
                        ins = pe.matmul(bank[4 + 2 * u + t // 2][:, (t % 2) * D:(t % 2 + 1) * D],
                                        xnT[:, u, c, t * P:(t + 1) * P], wtri12[:, 1, c], start=(c == 0), stop=(c == C - 1))
                ins.then_inc(project_ready.sem, 1)


        def context_slots_scalar(act):
            for k in range(4):
                act.wait_ge(c_kv, k + 1)
                act.activation(kvT[:, k // 2, k % 2], bank[1 + k][:, 0:BM], ACT.Copy).then_inc(c_kv_copied, 1)
            for o in range(C):
                act.wait_ge(c_kq, o + 1)
                act.activation(kqT[:, o], bank[1 + o][:, 0:BM], ACT.Copy, scale=vec0[:, SLOTW, o:o + 1]).then_inc(c_kq_copied, 1)
            half = 3 * D // 2
            for b in range(B):
                for k, (dst, n) in enumerate(((vW, P), (vWr, MR))):
                    act.wait_ge(c_vw, b * 2 + k + 1)
                    act.activation(dst[0:n, b, 0:half], bank[6][0:n, 0:half], ACT.Copy)
                    act.activation(dst[0:n, b, half:], bank[7][0:n, 0:half], ACT.Copy).then_inc(c_vw_copied, 1)

        def slot_iterations_scalar(act):
            act.wait_ge(c_rms, 2)
            with act.Fori(0, ITERS) as it:
                def copy_spread(j, q):
                    act.wait_ge(spread_ready, it * 8 + j + 1)
                    if j >= 4:
                        act.wait_ge(scores_scaled, it * 8 + 2 * q + 2)
                    act.activation(spread[:, q], bank[1][:], ACT.Copy).then_inc(spread_copied, 1)

                def exponentials(b):
                    act.wait_ge(max_ready, it * B + b + 1)
                    act.activation(e_main[:, b], e_main[:, b], ACT.Exp, bias=mneg[:, 0, b:b + 1], scale=D ** -0.5,
                                   accum_out=ssum[:, 0, b:b + 1]).then_inc(exp_ready, 1)
                    act.activation(e_rem[0:MR, b], e_rem[0:MR, b], ACT.Exp, bias=mneg[0:MR, 1, b:b + 1], scale=D ** -0.5,
                                   accum_out=ssum[0:MR, 1, b:b + 1]).then_inc(exp_ready, 1)

                def gates(q, o):
                    j = 2 * q + o
                    for k, dst, bias, fn in (("hn", gate_u, 5, ACT.Identity), ("r", gate_r, 0, ACT.Tanh),
                                             ("z", gate_z, 1, ACT.Tanh)):
                        act.wait_ge(gate_done[k], it * 8 + j + 1)
                        if k == "hn" and j >= 2:
                            act.wait_ge(h_ready, 8 + it * 8 + j - 1)
                        act.activation(dst[:, o], bank[dict(hn=4, r=5, z=6)[k]][:], fn, bias=bsum[:, bias, o:o + 1],
                                       scale=0.5).then_inc(gate_read[k], 1)

                def candidate(q, o):
                    j = 2 * q + o
                    act.wait_ge(gate_read["xn"], it * 8 + j + 1)
                    act.activation(cand[:, o], cand[:, o], ACT.Tanh, bias=vec0[:, BIH + 2, o:o + 1]).then_inc(cand_ready, 1)

                for q in range(GB):
                    copy_spread(q, q)
                for q in range(GB, G):
                    copy_spread(q, q)
                exponentials(0)
                exponentials(1)
                copy_spread(4, 0)
                copy_spread(5, 1)
                gates(0, 0)
                gates(0, 1)
                copy_spread(6, 2)
                copy_spread(7, 3)
                candidate(0, 0)
                candidate(0, 1)
                for q in range(1, G):
                    gates(q, 0)
                    gates(q, 1)
                    candidate(q, 0)
                    candidate(q, 1)

        def ternary_scalar(act):
            for g in range(G):
                if g >= 2:
                    act.wait_ge(*project_ready.at(1, g - 1))
                for c in range(C):
                    act.wait_ge(*turned.at(1, g * C + c + 1))
                    act.activation(qT[:, g % 2, c, 0:GN], bank[c].bitcast(BF16)[:, 0:GN], ACT.Copy).then_inc(xnT_ready.sem, 1)

        def empty_ring(eng, l, op, copy):
            s = 2 + 2 * l
            r = ring[op]
            if (eng is nc.scalar) != (r % 2 == 0):
                return
            src = bank[2 + r % 2]
            eng.wait_ge(*ring_filled.at(s, r + 1))
            if op[0] == "turn":
                g, c = op[1:]
                copy(xnT[:, g % 2, c], src, None).then_inc(ring_read[r % 2].sem, 1)
            elif op[0] == "query":
                g, o = op[1:]
                copy(qhT[:, g % 2, o], src, vmha[:, l, 0, o:o + 1]).then_inc(ring_read[r % 2].sem, 1)
            else:
                n, k = op[1:]
                if k < 2 and n >= 2:
                    eng.wait_ge(*pv_done.at(s, 2 * (n - 1)))
                copy(probsT[:, n % 2, 4 * k:4 * k + 4].rearrange("p h m -> p (h m)"), src, None).then_inc(ring_read[r % 2].sem, 1)

        def mha_scalar(act, l):
            s = 2 + 2 * l

            def copy(dst, src, bias):
                if bias is None:
                    return act.activation(dst, src, ACT.Copy)
                return act.activation(dst, src, ACT.Identity, bias=bias)

            def score(n, k):
                u = n % 2
                act.wait_ge(*pair_max.at(s, 4 * n + k + 1))
                if k == 0 and n >= 2:
                    r = ring["weights", n - 2, 4]
                    act.wait_ge(*ring_filled.at(s, r + 1))
                for j in range(4):
                    h = 4 * k + j
                    ins = act.activation(probs[:, u, h, 0:M], bank[4 + 2 * (k % 2) + j // 2][:, (j % 2) * M:(j % 2 + 1) * M],
                                         ACT.Exp, bias=nmax[:, u, h:h + 1], scale=HD ** -0.5, accum_out=hsum[:, u, h:h + 1])
                ins.then_inc(pair_exp.sem, 1)

            act.wait_ge(wmha_loaded[l], 5 * 16)
            act.wait_ge(ctxR_made, 4)
            if l:
                act.wait_ge(*x_done.at(s - 1, G))
            for n, ops in head_steps():
                for op in ops:
                    if op[0] == "score":
                        score(*op[1:])
                    elif op[0] == "weights":
                        empty_ring(act, l, op, copy)
                    elif op[0] in ("turn", "query"):
                        for c in range(C):
                            empty_ring(act, l, op + (c,), copy)
                    elif op[0] == "project":
                        act.wait_ge(*pv_done.at(s, 2 * GT * (op[1] + 1)))
                        act.activation(headsT[:, op[1] % 2, 0], bank[0], ACT.Copy).then_inc(headsT_ready[0].sem, 1)

        def tri_scalar(act):
            for k in range(2):
                for o in range(C):
                    act.wait_ge(tri_folded, k * C + o + 1)
                    act.activation(wtri12[:, k, o], bank[2 + o][:, 0:D], ACT.Copy).then_inc(tri_copied, 1)
            for g in range(G + 1):
                if g < G:
                    if g >= 2:
                        act.wait_ge(*project_ready.at(3, g - 1))
                    copy_turned(act, 3, g, xnT[:, g % 2])
                if g >= 1:
                    act.wait_ge(tri_summed, g)
                    r = tri_out[:, (g - 1) % 2]
                    act.activation(r, r, ACT.Tanh).then_inc(tri_tanh, 1)


        def context_slots_vector(dve):
            dve.wait_ge(w0_loaded, 6 * 16)
            ch = Chain(dve, sem("ctx_steps"))
            ch.step(dve.tensor_tensor(bsum[:, 0:2], vec0[:, BIH:BIH + 2], vec0[:, BHH:BHH + 2], ALU.add))
            ch.settle()
            dve.tensor_scalar(bsum[:, 0:2], bsum[:, 0:2], 0.5, None, ALU.mult).then_inc(c_rms, 1)
            dve.tensor_scalar(bsum[:, 5], vec0[:, BHH + 2], 0.5, None, ALU.mult).then_inc(c_rms, 1)
            dve.wait_ge(c_ms, 1)
            v, y, t_ = (spread[:, k, 0:BM] for k in range(3))
            ch.step(dve.tensor_scalar(v, bank[0][:, 0:BM], 1.0 / D, RMS_EPS, ALU.mult, ALU.add))
            ch.settle()
            for _ in rsqrt_newton(ch, v, y, t_):
                pass
            for c in range(C):
                dve.scalar_tensor_tensor(PnT[:, c], ctxT[:, c], vec0[:, INW, c:c + 1], y, ALU.mult,
                                         ALU.mult).then_inc(c_pn, 1)

        SLOT_STEPS = 2 + 3 * NEWTON + 2 * 2 + 2 * 1 + 2 * 1 + 8 * 3
        def slot_iterations_vector(dve):
            steps = sem("slot_steps")
            with dve.Fori(0, ITERS) as it:
                ch = Chain(dve, steps, SLOT_STEPS, it)

                def diagonal(q, col, j):
                    if j >= 2:
                        dve.wait_ge(spread_ready, it * 8 + j - 1)
                    dve.tensor_tensor(diag[:, q % 2].rearrange("p (t n) -> p t n", t=GT),
                                      ident[:].unsqueeze(1).broadcast_to([P, GT, P]),
                                      col.unsqueeze(2).broadcast_to([P, GT, P]), ALU.mult).then_inc(diag_ready, 1)

                dve.wait_ge(ms_ready, it * G + G)
                v, t_ = nwt[:, 0, 0], nwt[:, 0, 2]
                ch.step(dve.tensor_scalar(v, bank[0][:, 0:T], 1.0 / D, RMS_EPS, ALU.mult, ALU.add))
                ch.settle()
                for _ in rsqrt_newton(ch, v, rms16, t_):
                    pass
                for q in range(G):
                    diagonal(q, rms16[:, q * GT:(q + 1) * GT], q)

                def scale_scores(q):
                    b, n0 = q // GB, (q % GB) * GN
                    main, rem = (bank[2 + 2 * (q % 3)], bank[3 + 2 * (q % 3)])
                    dve.wait_ge(scores_ready, it * G + q + 1)
                    dve.wait_ge(spread_copied, it * 8 + q + 1)
                    take_wait(dve)
                    for k, (src, dst, n) in enumerate(((main, e_main, P), (rem, e_rem, MR))):
                        dve.tensor_tensor_reduce(dst[0:n, b, n0:n0 + GN], src[0:n, :], spread[0:n, q], 1.0, -3.0e38,
                                                 ALU.mult, ALU.max, mx[0:n, k, b, q % GB:q % GB + 1]).then_inc(scores_scaled, 1)

                def negated_max(b):
                    dve.wait_ge(scores_scaled, it * 8 + 4 * b + 4)
                    for k, n in enumerate((P, MR)):
                        ch.step(dve.tensor_reduce(mneg[0:n, k, b:b + 1], mx[0:n, k, b], AX.X, ALU.max, negate=True))
                    ch.settle()
                    dve.tensor_scalar(mneg[:, 0, b:b + 1], mneg[:, 0, b:b + 1], D ** -0.5, None, ALU.mult)
                    dve.tensor_scalar(mneg[0:MR, 1, b:b + 1], mneg[0:MR, 1, b:b + 1], D ** -0.5, None,
                                      ALU.mult).then_inc(max_ready, 1)

                def inverse_sums(b):
                    dve.wait_ge(exp_ready, it * 4 + 2 * b + 2)
                    ch.step(dve.reciprocal(sinv[:, 0, b:b + 1], ssum[:, 0, b:b + 1]))
                    dve.reciprocal(sinv[0:MR, 1, b:b + 1], ssum[0:MR, 1, b:b + 1]).then_inc(sinv_ready, 1)

                def inverse_row_sums(b):
                    dve.wait_ge(rowsum_ready, it * B + b + 1)
                    r = rinv[:, b * 8:b * 8 + 8]
                    ch.step(dve.tensor_scalar(r, bank[0][:, T + b * 8:T + b * 8 + 8], RMS_EPS, None, ALU.add))
                    ch.settle()
                    dve.reciprocal(r, r).then_inc(rinv_ready, 1)
                    dve.wait_ge(rinv_ready, it * B + b + 1)
                    for q in range(b * GB, (b + 1) * GB):
                        diagonal(q, rinv[:, q * GT:(q + 1) * GT], 4 + q)

                def attention(q):
                    b, n0 = q // GB, (q % GB) * GN
                    dve.wait_ge(spread_copied, it * 8 + 4 + q + 1)
                    dve.tensor_tensor(e_main[:, b, n0:n0 + GN], e_main[:, b, n0:n0 + GN], spread[:, q], ALU.mult)
                    dve.tensor_tensor(e_rem[0:MR, b, n0:n0 + GN], e_rem[0:MR, b, n0:n0 + GN], spread[0:MR, q],
                                      ALU.mult).then_inc(attn_ready, 1)

                def argument(q, o):
                    j = 2 * q + o
                    dve.wait_ge(gate_read["r"], it * 8 + j + 1)
                    ch.step(dve.scalar_tensor_tensor(gate_u[:, o], gate_r[:, o], 1.0, gate_u[:, o], ALU.add, ALU.mult))
                    ch.settle()
                    dve.wait_ge(gate_done["xn"], it * 8 + j + 1)
                    dve.tensor_tensor(cand[:, o], bank[7][:], gate_u[:, o], ALU.add).then_inc(gate_read["xn"], 1)

                def new_slots(q, o):
                    j = 2 * q + o
                    h = hT[:, o, q * GN:(q + 1) * GN]
                    dve.wait_ge(cand_ready, it * 8 + j + 1)
                    dve.wait_ge(gate_read["z"], it * 8 + j + 1)
                    dve.wait_ge(gate_done["xn"], it * 8 + 2 * q + 2)
                    ch.step(dve.tensor_tensor(gate_r[:, o], h, cand[:, o], ALU.subtract))
                    ch.settle()
                    ch.step(dve.scalar_tensor_tensor(gate_r[:, o], gate_z[:, o], 1.0, gate_r[:, o], ALU.add, ALU.mult))
                    ch.settle()
                    dve.scalar_tensor_tensor(h, gate_r[:, o], 0.5, cand[:, o], ALU.mult, ALU.add).then_inc(h_ready, 1)

                scale_scores(0)
                scale_scores(1)
                negated_max(0)
                scale_scores(2)
                scale_scores(3)
                negated_max(1)
                inverse_sums(0)
                inverse_sums(1)
                inverse_row_sums(0)
                attention(0)
                attention(1)
                argument(0, 0)
                inverse_row_sums(1)
                argument(0, 1)
                attention(2)
                attention(3)
                new_slots(0, 0)
                new_slots(0, 1)
                for q in range(1, G):
                    argument(q, 0)
                    argument(q, 1)
                    new_slots(q, 0)
                    new_slots(q, 1)
                ch.close()

        def unpack_ternary_vector(dve):
            dve.wait_ge(w1_loaded, 2 * 16)
            for k in range(4):
                if k:
                    dve.wait_ge(tern_ready, k)
                dve.tensor_scalar(unpacked[:], packed[:], 2 * k, 3, ALU.arith_shift_right,
                                  ALU.bitwise_and).then_inc(unpacked_ready, 1)
                dve.wait_ge(unpacked_ready, k + 1)
                dve.tensor_scalar(tern[:, :, k * 64:(k + 1) * 64], unpacked[:], -1.0, None, ALU.add).then_inc(tern_ready, 1)

        def quantise(dve, ch, g):
            top, scale, back = (amax[:, g, k] for k in range(3))
            dve.wait_ge(*xn_ready.at(1, g + 1))
            ch.step(dve.tensor_reduce(top, xn[:, g], AX.X, ALU.max, apply_absolute_value=True))
            ch.settle()
            ch.step(dve.tensor_scalar(top, top, 1e-5, None, ALU.max))
            ch.settle()
            ch.step(dve.reciprocal(scale, top))
            ch.settle()
            ch.step(dve.tensor_scalar(scale, scale, 127.0, None, ALU.mult))
            ch.step(dve.tensor_scalar(back, top, wscale[:], 1.0 / 127.0, ALU.mult, ALU.mult))
            ch.settle()
            ch.step(dve.tensor_scalar(back, back, gain(1), None, ALU.mult))
            for t in range(GT):
                ch.step(dve.tensor_scalar(xn[:, g, t], xn[:, g, t], scale[:, t:t + 1], ROUND, ALU.mult, ALU.add))
            ch.settle()
            flat = xn[:, g].rearrange("p t d -> p (t d)")
            ch.step(dve.tensor_scalar(flat, flat, -ROUND, 127.0, ALU.add, ALU.min))
            ch.settle()
            if g >= 2:
                dve.wait_ge(*turned.at(1, (g - 1) * C))
            dve.tensor_scalar(xq[:, g % 2], flat, -128.0, None, ALU.max).then_inc(xq_ready, 1)

        def finish_slots_vector(dve, ch):
            dve.wait_ge(gains_ready, 1)
            for g in range(G):
                for k in (2 * g, 2 * g + 1):
                    dve.wait_ge(slotsT_ready, k + 1)
                    xs = x_tok[:, 2 * k:2 * k + 2].rearrange("p t d -> p (t d)")
                    ins = dve.scalar_tensor_tensor(xs, bank[k], gain(0), xs, ALU.mult, ALU.add)
                    if k % 2:
                        ins.then_inc(x_done.sem, 1)
                    else:
                        ch.step(ins)
                next_norm(dve, ch, 0, g)
                if last_stage >= 1:
                    quantise(dve, ch, g)

        def next_norm(dve, ch, s, g):
            for _ in next_norm_parts(dve, ch, s, g):
                pass

        def next_norm_parts(dve, ch, s, g):
            if s < last_stage:
                dve.wait_ge(*x_done.at(s, g + 1))
                yield from layer_norm_parts(dve, ch, s + 1, g)

        def ternary_vector(dve, ch):
            for g in range(G):
                dve.wait_ge(*project_ready.at(1, g + 1))
                dve.wait_ge(*row_added.at(1, g + 1))
                for t in range(GT):
                    xs = x_tok[:, g * GT + t]
                    ins = dve.scalar_tensor_tensor(xs, bank[4 + 2 * (g % 2) + t // 2][:, (t % 2) * D:(t % 2 + 1) * D],
                                                   amax[:, g, 2, t:t + 1], xs, ALU.mult, ALU.add)
                    if t == GT - 1:
                        ins.then_inc(x_done.sem, 1)
                next_norm(dve, ch, 1, g)

        def mha_context_vector(dve, ch, l):
            s = 2 + 2 * l
            if l == 0:
                dve.wait_ge(masks_made, 1)
                ch.step(dve.tensor_scalar(pidx[:, 1:2], pidx[:, 0:1], 16, None, ALU.bitwise_and))
                ch.settle()
                for k in range(2):
                    ch.step(dve.tensor_scalar(mask16[:, k:k + 1], pidx[:, 1:2], 16.0 * k, None, ALU.is_equal))
                ch.settle()
                ch.step(dve.tensor_scalar(pidx[:, 1:2], pidx[:, 0:1], 5, None, ALU.arith_shift_right))
                ch.settle()
                for k in range(4):
                    ch.step(dve.tensor_scalar(mask32[:, k:k + 1], pidx[:, 1:2], 1.0 * k, None, ALU.is_equal))
                ch.settle()
            dve.wait_ge(wmha_loaded[l], 5 * 16)
            if l:
                dve.wait_ge(*context_done.at(0, 7))
            for c in range(C):
                dve.tensor_scalar(bvrow[:, c], ones[:], vmha[:, l, 2, c:c + 1], None, ALU.mult).then_inc(bv_ready.sem, 1)
            for o in range(C):
                dve.wait_ge(*context_done.at(l, o + 1))
                for b in range(B):
                    for h in range(2):
                        ins = dve.tensor_scalar(keys[:, o, b, h], bank[2 + o][:, b * M:(b + 1) * M], vmha[:, l, 1, o:o + 1],
                                                mask16[:, h:h + 1], ALU.add, ALU.mult)
                ins.then_inc(keys_ready.sem, 1)
            dve.wait_ge(ctxR_made, 4)
            for b in range(B):
                dve.wait_ge(*context_done.at(l, 3 + b))
                for c in range(C):
                    at = (b * C + c) * 8 * P
                    ch.step(dve.tensor_copy(vals[:, at:at + 8 * (P + HD)].rearrange("p (j n) -> p j n", j=8)[:, :, 0:HD],
                                            bank[4 + b][:, c * P:(c + 1) * P].rearrange("p (j n) -> p j n", j=8)))
                dve.wait_ge(*context_done.at(l, 5 + b))
                for h in range(4):
                    for c in range(C):
                        at = (b * C + c) * 2 * P
                        ins = dve.tensor_scalar(
                            valsR[:, at:at + 2 * (P + 64)].rearrange("p (q n) -> p q n", q=2)[:, :, h * HD:(h + 1) * HD],
                            bank[6 + b][:, c * P:(c + 1) * P].rearrange("p (q n) -> p q n", q=2)[:, :, h * HD:(h + 1) * HD],
                            mask32[:, h:h + 1], None, ALU.mult)
                        if h < 3 or c == 0:
                            ch.step(ins)
                ins.then_inc(vals_ready.sem, 1)
            dve.wait_ge(*context_done.at(l, 7))
            dve.wait_ge(rows_loaded, 5 * 16)
            row = add_row[:, 1 + l]
            ch.step(dve.tensor_tensor(row, bank[2][:, 0:D], row, ALU.add))
            ch.settle()
            dve.tensor_scalar(row, row, gain(s), None, ALU.mult).then_inc(cvec_ready.sem, 1)

        def mha_vector(dve, ch, l):
            s = 2 + 2 * l

            def copy(dst, src, bias):
                if bias is None:
                    return dve.tensor_copy(dst, src)
                return dve.tensor_scalar(dst, src, bias, None, ALU.add)

            def score(n, k):
                u = n % 2
                dve.wait_ge(*pair_scored.at(s, 4 * n + k + 1))
                m = smax[:, u, 4 * k:4 * k + 4]
                ch.step(dve.tensor_reduce(m.rearrange("p (b h) -> p b h", b=2),
                                          psum[:, 4 + 2 * (k % 2):6 + 2 * (k % 2), 0:2 * M].rearrange("p b (h m) -> p b h m", h=2),
                                          AX.X, ALU.max))
                ch.settle()
                dve.tensor_scalar(nmax[:, u, 4 * k:4 * k + 4], m, -HD ** -0.5, None, ALU.mult).then_inc(pair_max.sem, 1)

            def inverse_sums(n, half):
                dve.wait_ge(*pair_exp.at(s, 4 * n + 2 * half + 2))
                dve.reciprocal(rsum[:, n % 2, 8 * half:8 * half + 8], hsum[:, n % 2, 8 * half:8 * half + 8]).then_inc(half_sums.sem, 1)

            def finish(g):
                dve.wait_ge(*row_added.at(s, g + 1))
                for half in range(2):
                    dve.wait_ge(*half_projected.at(s, 2 * g + half + 1))
                    t0 = g * GT + 2 * half
                    xs = x_tok[:, t0:t0 + 2].rearrange("p t d -> p (t d)")
                    dve.scalar_tensor_tensor(xs, bank[half], gain(s), xs, ALU.mult,
                                             ALU.add).then_inc(x_done.sem if half else half_added.sem, 1)

            norm = iter(())
            for n, ops in head_steps():
                for op in ops:
                    next(norm, None)
                    next(norm, None)
                    if op[0] == "score":
                        score(*op[1:])
                        if op[2] == 2:
                            inverse_sums(op[1], 0)
                    elif op[0] == "weights":
                        empty_ring(dve, l, op, copy)
                    elif op[0] in ("turn", "query"):
                        for c in range(C):
                            empty_ring(dve, l, op + (c,), copy)
                    elif op[0] == "project":
                        g = op[1]
                        dve.wait_ge(*pv_done.at(s, 2 * GT * (g + 1)))
                        dve.tensor_copy(headsT[:, g % 2, 1], bank[1]).then_inc(headsT_ready[1].sem, 1)
                if n + 1 < T:
                    inverse_sums(n + 1, 1)
                for op in ops:
                    if op[0] == "project":
                        for _ in norm:
                            pass
                        finish(op[1])
                        norm = next_norm_parts(dve, ch, s, op[1])
            for _ in norm:
                pass

        def tri_vector(dve, ch):
            def finish(g):
                dve.wait_ge(tri_tanh, g + 1)
                xs = x_tok[:, g * GT:(g + 1) * GT].rearrange("p t d -> p (t d)")
                dve.scalar_tensor_tensor(xs, tri_out[:, g % 2], gain(3), xs, ALU.mult, ALU.add).then_inc(x_done.sem, 1)
                next_norm(dve, ch, 3, g)

            for g in range(G):
                u = g % 2
                dve.wait_ge(*project_ready.at(3, g + 1))
                dve.tensor_tensor(tri_out[:, u].rearrange("p (t d) -> p t d", d=D),
                                  psum[:, 4 + 2 * u:6 + 2 * u].rearrange("p b (t d) -> p (b t) d", d=D),
                                  add_row[:, 4].unsqueeze(1).broadcast_to([P, GT, D]), ALU.add).then_inc(tri_summed, 1)
                if g >= 1:
                    finish(g - 1)
            finish(G - 1)

        @block.sync
        def _(sp):
            sp.dma_start(x_tok[:], d["x"].rearrange("(t p) d -> p t d", p=P)).then_inc(x_loaded, 16)
            sp.dma_start(ctxT[:], d["ctxT"].rearrange("(c p) n -> p c n", p=P)).then_inc(ctx_loaded, 16)
            sp.dma_start(tanh_g[:], d["gains"].partition_broadcast(P)).then_inc(gains_loaded, 16)
            for k, name in enumerate(("wq0", "wk0", "wv0")):
                sp.dma_start(wqkv0[:, k], weight(d[name])).then_inc(w0_loaded, 16)
            sp.dma_start(wih, weight(d["wih"])).then_inc(w0_loaded, 16)
            sp.dma_start(whh, weight(d["whh"])).then_inc(w0_loaded, 16)
            sp.dma_start(vec0[:, 0:8], d["vec0"].rearrange("p (v c) -> p v c", c=C)).then_inc(w0_loaded, 16)
            sp.dma_start(packed[:], weight(d["packed"])).then_inc(w1_loaded, 16)
            sp.dma_start(wscale[:], d["wscale"].partition_broadcast(P)).then_inc(w1_loaded, 16)
            for k, name in enumerate(("row1", "row2", "row4", "row6", "row3")):
                sp.dma_start(add_row[:, k], d[name].partition_broadcast(P)).then_inc(rows_loaded, 16)
            for k, name in enumerate(("tri_wT", "tri_a1T", "tri_a2")):
                sp.dma_start(wtri[:, k], weight(d[name])).then_inc(w3_loaded, 16)
            if last_stage >= 5:
                sp.wait_ge(route_consts, 1)
                sp.dma_start(xs5.rearrange("(t p) d -> p t d", p=P),
                             zeros[:].unsqueeze(1).broadcast_to([P, NT2, D])).then_inc(zeroed, 16)
                sp.dma_start(xs7.rearrange("(t p) d -> p t d", p=P),
                             zeros[:].unsqueeze(1).broadcast_to([P, NT4, D])).then_inc(zeroed, 16)
            if last_stage >= 2:
                sp.wait_ge(*x_done.at(0, G))
                for l in range(2):
                    for k, name in enumerate(("wq", "wk", "wv", "wo")):
                        sp.dma_start(wmha[:, l, k], weight(d[f"{name}{l + 1}"])).then_inc(wmha_loaded[l], 16)
                    sp.dma_start(vmha[:, l], d[f"vec{l + 1}"].rearrange("p (v c) -> p v c", c=C)).then_inc(wmha_loaded[l], 16)
            if last_stage >= 5:
                sp.wait_ge(*x_done.at(3, G))
                sp.dma_start(b2row, d["b2"].partition_broadcast(P)).then_inc(w5_loaded, 16)
                sp.dma_start(br5, d["br5"].partition_broadcast(P)).then_inc(w5_loaded, 16)
                sp.dma_start(b1col, d["b1"]).then_inc(w5_loaded, 16)
                sp.dma_start(wr5, weight(d["wr5"])).then_inc(w5_loaded, 16)
                sp.wait_ge(*x_done.at(4, G))
                for e in range(E2):
                    sp.dma_start(W1[:, e].rearrange("p (c n) -> p c n", c=C), weight(d["W1"][e * D:(e + 1) * D])).then_inc(expert5_loaded, 16)
                    sp.dma_start(W2[:, e].rearrange("p (k n) -> p k n", n=D), weight(d["W2"][e * F2:(e + 1) * F2])).then_inc(expert5_loaded, 16)
                expert_tiles_sync(sp)
            if last_stage >= 6:
                sp.wait_ge(*out_done.at(5, NT2))
                for k, name in enumerate(("wk6", "wv6", "wq6")):
                    sp.dma_start(w6[:, k], weight(d[name])).then_inc(w6_loaded, 16)
                sp.dma_start(vec6, d["vec6"].rearrange("p (v c) -> p v c", c=C)).then_inc(w6_loaded, 16)
            if last_stage >= 7:
                for k in range(4):
                    sp.dma_start(GU[:, 8 * k:8 * k + 8].rearrange("p e c n -> p (e c) n"),
                                 d["gate_up"][8 * k * D:8 * (k + 1) * D].rearrange("(e p) n -> p e n", p=P)).then_inc(w7_loaded, 16)
                    sp.dma_start(DW[:, 8 * k:8 * k + 8],
                                 d["down"][8 * k * F4:8 * (k + 1) * F4].rearrange("(e p) n -> p e n", p=P)).then_inc(w7_loaded, 16)
                sp.wait_ge(*x_done.at(5, G))
                sp.dma_start(wr7, weight(d["wr7"])).then_inc(ws_loaded, 16)
                sp.dma_start(br7, d["br7"].partition_broadcast(P)).then_inc(ws_loaded, 16)
                sp.dma_start(sgate, weight(d["sgate"])).then_inc(ws_loaded, 16)
                sp.dma_start(sup, weight(d["sup"])).then_inc(ws_loaded, 16)
                sp.dma_start(sdown, weight(d["sdown"])).then_inc(ws_loaded, 16)
                quads_sync(sp)
            sp.wait_ge(*x_done.at(last_stage, G))
            sp.dma_start(out.rearrange("(t p) d -> p t d", p=P), x_tok[:]).then_inc(out_stored, 16)
            sp.wait_ge(out_stored, 16)

        @block.gpsimd
        def _(pool):
            pool.memset(ones[:], 1.0).then_inc(consts_made, 1)
            pool.wait_ge(consts_made, 1)
            pool.affine_select(ident[:], ones[:], [[-1, P]], ALU.is_equal, 0.0, base=0,
                               channel_multiplier=1).then_inc(consts_made, 1)
            if last_stage >= 5:
                route_constants_gpsimd(pool)
            pool.wait_ge(ctx_loaded, 16)
            pool.tensor_tensor(sq[:, 0, :, 0:BM], ctxT[:], ctxT[:], ALU.mult).then_inc(c_sq, 1)
            pool.wait_ge(consts_made, 2)
            pool.tensor_copy(ident_bf[:], ident[:]).then_inc(consts_made, 1)
            pool.iota(pidx[:, 0:1], [[0, 1]], base=0, channel_multiplier=1).then_inc(masks_made, 1)
            pool.wait_ge(rows_loaded, 5 * 16)
            pool.wait_ge(gains_ready, 1)
            row = add_row[:, 0]
            pool.tensor_tensor(row, row, gain(1).broadcast_to([P, D]), ALU.mult).then_inc(rows_ready, 1)
            row = add_row[:, 3]
            pool.tensor_tensor(row, row, gain(6).broadcast_to([P, D]), ALU.mult).then_inc(rows_ready, 1)
            pool.wait_ge(c_ms, 1)
            slot_iterations_gpsimd(pool)
            if last_stage >= 2:
                mha_constants_gpsimd(pool)
            pool.wait_ge(rows_ready, 2)
            add_rows_gpsimd(pool, 1, 0)
            if last_stage >= 2:
                pool.wait_ge(*cvec_ready.at(0, 1))
                mha_gpsimd(pool, 0, 1)
            if last_stage >= 4:
                pool.wait_ge(*cvec_ready.at(1, 1))
                mha_gpsimd(pool, 1, 2)
            if last_stage >= 5:
                scatter_gpsimd(pool, 5, xs5)
                gather_gpsimd(pool)
            if last_stage >= 6:
                add_rows_gpsimd(pool, 6, 3)
            if last_stage >= 7:
                scatter_gpsimd(pool, 7, xs7)
                gather7_gpsimd(pool)

        @block.tensor
        def _(pe):
            pe.wait_ge(consts_made, 2)
            start_slots_tensor(pe)
            context_slots_tensor(pe)
            slot_iterations_tensor(pe)
            finish_slots_tensor(pe)
            if last_stage >= 1:
                ternary_tensor(pe)
            if last_stage >= 2:
                mha_context_tensor(pe, 0)
                mha_tensor(pe, 0)
            if last_stage >= 3:
                tri_fold_tensor(pe)
                tri_tensor(pe)
            if last_stage >= 4:
                mha_context_tensor(pe, 1)
                mha_tensor(pe, 1)
            if last_stage >= 5:
                route_tensor(pe, 5, wr5, (w5_loaded, 4 * 16), free=lambda: pe.wait_ge(*x_done.at(4, G)))
                expert_tiles_tensor(pe)
            if last_stage >= 6:
                single_context_tensor(pe)
                single_tensor(pe)
            if last_stage >= 7:
                route_tensor(pe, 7, wr7, (ws_loaded, 5 * 16), free=lambda: pe.wait_ge(*x_done.at(6, G)))
                shared_tensor(pe)
                quads_tensor(pe)

        @block.scalar
        def _(act):
            act.wait_ge(gains_loaded, 16)
            act.activation(tanh_g[:], tanh_g[:], ACT.Tanh).then_inc(gains_ready, 1)
            for g in range(G):
                copy_turned(act, 0, g, hT[:, :, g * GN:(g + 1) * GN])
            context_slots_scalar(act)
            slot_iterations_scalar(act)
            if last_stage >= 1:
                ternary_scalar(act)
            if last_stage >= 2:
                mha_scalar(act, 0)
            if last_stage >= 3:
                tri_scalar(act)
            if last_stage >= 4:
                mha_scalar(act, 1)
            if last_stage >= 5:
                route_scalar(act, 5)
                expert_tiles_scalar(act)
            if last_stage >= 6:
                single_context_scalar(act)
                single_scalar(act)
            if last_stage >= 7:
                route_scalar(act, 7)
                shared_scalar(act)
                quads_scalar(act)

        @block.vector
        def _(dve):
            ch = Chain(dve, dve_step)
            dve.wait_ge(x_loaded, 16)
            for g in range(G):
                layer_norm(dve, ch, 0, g)
            context_slots_vector(dve)
            slot_iterations_vector(dve)
            unpack_ternary_vector(dve)
            finish_slots_vector(dve, ch)
            ternary_vector(dve, ch)
            if last_stage >= 2:
                mha_context_vector(dve, ch, 0)
                mha_vector(dve, ch, 0)
            if last_stage >= 3:
                tri_vector(dve, ch)
            if last_stage >= 4:
                mha_context_vector(dve, ch, 1)
                mha_vector(dve, ch, 1)
            if last_stage >= 5:
                route_vector(dve, ch, 5, br5)
                expert_tiles_vector(dve)
            if last_stage >= 6:
                single_context_vector(dve, ch)
            if last_stage >= 5:
                combine_vector(dve, ch)
            if last_stage >= 6:
                single_vector(dve, ch)
            if last_stage >= 7:
                route_vector(dve, ch, 7, br7)
                shares_vector(dve, ch)
                shared_vector(dve, ch)
                quads_vector(dve)
                combine7_vector(dve, ch)


LAST = 7


def kernel(**inputs):
    import numpy as np
    import concourse.bacc as bacc
    from concourse.bass_utils import run_bass_kernel_spmd

    a = {k: np.ascontiguousarray(v) for k, v in inputs.items()}
    columns = lambda *v: np.ascontiguousarray(np.stack([w.reshape(-1, P).T for w in v], 1).reshape(P, -1))
    T_ = lambda w: np.ascontiguousarray(w.T)
    bih, bhh = a["L0_xattn_gru_bih"].reshape(3, D), a["L0_xattn_gru_bhh"].reshape(3, D)
    lay = {
        "x": a["x"].reshape(B * S, D),
        "ctxT": T_(a["ctx_1024"].reshape(BM, D)),
        "gains": np.concatenate([a["g_xattn"], a["g_ffn"]]),
        "wq0": a["L0_xattn_Wq"], "wk0": T_(a["L0_xattn_Wk"]), "wv0": T_(a["L0_xattn_Wv"]),
        "wih": T_(a["L0_xattn_gru_wih"]), "whh": T_(a["L0_xattn_gru_whh"]),
        "vec0": columns(*bih, *bhh, a["L0_xattn_slot_norm_w"], a["L0_xattn_input_norm_w"]),
    }
    lay |= {
        "packed": T_(a["L0_ffn_packed_weight"].reshape(D // 4, D)),
        "wscale": a["L0_ffn_weight_scale"], "row1": a["L0_ffn_bias"],
        "row2": a["L1_xattn_bo"], "row4": a["L2_xattn_bo"], "row6": a["L3_xattn_bv"], "row3": a["L1_ffn_bias"],
        "tri_wT": T_(a["L1_ffn_weight"]), "tri_a1T": T_(a["L1_ffn_aux_weight1"]), "tri_a2": a["L1_ffn_aux_weight2"],
        "wq1": a["L1_xattn_wq"], "wk1": a["L1_xattn_wk"], "wv1": a["L1_xattn_wv"], "wo1": a["L1_xattn_wo"],
        "wq2": T_(a["L2_xattn_Wq"]), "wk2": T_(a["L2_xattn_Wk"]), "wv2": T_(a["L2_xattn_Wv"]), "wo2": T_(a["L2_xattn_Wo"]),
        "vec1": columns(a["L1_xattn_bq"], a["L1_xattn_bk"], a["L1_xattn_bv"], a["L1_xattn_bv"]),
        "vec2": columns(a["L2_xattn_bq"], a["L2_xattn_bk"], a["L2_xattn_bv"], a["L2_xattn_bv"]),
    }
    lay |= {
        "W1": T_(a["L2_ffn_W1"].reshape(E2 * F2, D)).reshape(D, E2, F2).transpose(1, 0, 2).reshape(E2 * D, F2),
        "W2": a["L2_ffn_W2"].transpose(0, 2, 1).reshape(E2 * F2, D),
        "b1": T_(a["L2_ffn_b1"].reshape(-1, P)), "b2": a["L2_ffn_b2"].reshape(-1),
        "wr5": T_(a["L2_ffn_Wr"]), "br5": a["L2_ffn_br"],
    }
    lay |= {
        "wk6": a["L3_xattn_Wk"], "wv6": a["L3_xattn_Wv"], "wq6": T_(a["L3_xattn_Wq"]),
        "vec6": columns(a["L3_xattn_bq"], a["L3_xattn_bk"]),
    }
    lay |= {
        "gate_up": np.concatenate([a["L3_ffn_gate_w"].transpose(0, 2, 1), a["L3_ffn_up_w"].transpose(0, 2, 1)], 2).reshape(E4 * D, 2 * F4),
        "down": a["L3_ffn_down_w"].transpose(0, 2, 1).reshape(E4 * F4, D),
        "wr7": T_(a["L3_ffn_router_w"]), "br7": a["L3_ffn_router_bias"],
        "sgate": T_(a["L3_ffn_sgate_w"]), "sup": T_(a["L3_ffn_sup_w"]), "sdown": T_(a["L3_ffn_sdown_w"]),
    }
    lay = {k: np.ascontiguousarray(v) for k, v in lay.items()}
    nc = bacc.Bacc("TRN2", target_bir_lowering=False, num_devices=1)
    d = {k: nc.dram_tensor(f"in_{k}", v.shape, mybir.dt.from_np(v.dtype), kind="ExternalInput").ap() for k, v in lay.items()}
    out = nc.dram_tensor("out_x", (B * S, D), F32, kind="ExternalOutput").ap()
    build(nc, d, out, LAST)
    r = run_bass_kernel_spmd(nc, [{f"in_{k}": v for k, v in lay.items()}], core_ids=[0])
    return r.results[0]["out_x"].reshape(B, S, D)
```

```python
from contextlib import ExitStack

import concourse.bass as bass
from concourse import mybir

F32 = mybir.dt.float32
BF16 = mybir.dt.bfloat16
I32 = mybir.dt.int32
U32 = mybir.dt.uint32
ALU = mybir.AluOpType
ACT = mybir.ActivationFunctionType
AX = mybir.AxisListType

P = 128
B, S, D, M = 2, 1024, 256, 154
C = D // P
T = B * S // P
GT = 4
GN = GT * P
G = T // GT
GB = G // B
MR = M - P
BM = B * M
ITERS = 3
H, HD = 16, 16
E4, K4, F4 = 32, 4, 128
NT4 = K4 * T + E4
NQ = NT4 // 4
FS = K4 * F4
E2, F2 = 8, 1024
NT2 = T + E2
ROUND = 1.5 * 2 ** 23
LN_EPS, RMS_EPS = 1e-5, 1e-6
RSQRT_MAGIC = 0x5F3759DF
NEWTON = 3


class Chain:

    def __init__(self, eng, sem, per_turn=0, turn=0):
        self.eng, self.sem, self.n = eng, sem, 0
        self.base, self.per_turn = turn * per_turn, per_turn

    def step(self, ins):
        ins.then_inc(self.sem, 1)
        self.n += 1

    def settle(self, n=None):
        self.eng.wait_ge(self.sem, self.base + (self.n if n is None else n))

    def close(self):
        assert self.n == self.per_turn, (self.n, self.per_turn)


class Series:

    def __init__(self, sem, totals):
        self.sem, self.base, n = sem, {}, 0
        for stage, total in totals.items():
            self.base[stage] = n
            n += total

    def at(self, stage, n):
        return self.sem, self.base[stage] + n


class Alternate:

    def __init__(self, even, odd):
        self.series = even, odd

    def of(self, stage):
        return self.series[stage % 2].sem

    def at(self, stage, n):
        return self.series[stage % 2].at(stage, n)


def weight(ap):
    return ap.rearrange("(c p) n -> p c n", p=P)


def build(nc, d, out, last_stage):
    ctx = ExitStack()
    with ctx:
        def sb(name, shape, dt=F32):
            return ctx.enter_context(nc.sbuf_tensor(name, shape, dt))

        def sem(name):
            return ctx.enter_context(nc.semaphore(name))

        def series(name, totals):
            return Series(sem(name), totals)

        psum = ctx.enter_context(nc.psum_tensor("psum", [P, 8, 512], F32))
        bank = [psum[:, i] for i in range(8)]
        x_tok = sb("x_tok", [P, T, D])
        ident = sb("ident", [P, P])
        ones = sb("ones", [P, P])
        ctxT = sb("ctxT", [P, C, BM])
        tanh_g = sb("tanh_g", [P, 8])
        arena = sb("arena", [P, 32768])
        used = [0]

        def carve(cols, *shape, at=None):
            if at is None:
                at = used[0]
                used[0] += cols
            assert at + cols <= 32768
            return arena[:, at:at + cols]

        xn = sb("xn", [P, G, GT, D])
        xq = sb("xq", [P, 2, GT * D], BF16)
        xnT = sb("xnT", [P, 2, C, GN])
        stats = sb("stats", [P, 2, GT, 6])
        meanvar = sb("meanvar", [P, 2, GT, 2])
        add_row = sb("add_row", [P, 5, D])
        ident_bf = sb("ident_bf", [P, P], BF16)
        scrap = sb("scrap", [P, 64])
        scraps = iter(range(64))

        def take_wait(dve):
            k = next(scraps)
            dve.memset(scrap[:, k:k + 1], 0.0)

        nwt = sb("nwt", [P, 2, 3, T])

        hT = carve(C * T * P).rearrange("p (c n) -> p c n", c=C)
        wqkv0 = carve(3 * C * D).rearrange("p (w c n) -> p w c n", w=3, c=C)
        wih = carve(C * 3 * D).rearrange("p (c n) -> p c n", c=C)
        whh = carve(C * 3 * D).rearrange("p (c n) -> p c n", c=C)
        vec0 = carve(16 * C).rearrange("p (v c) -> p v c", c=C)
        sq = carve(2 * C * GN).rearrange("p (q c n) -> p q c n", q=2, c=C)
        PnT = carve(C * BM).rearrange("p (c n) -> p c n", c=C)
        kvT = carve(2 * C * BM).rearrange("p (w c n) -> p w c n", w=2, c=C)
        kqT = carve(C * BM).rearrange("p (c n) -> p c n", c=C)
        vW = carve(B * 3 * D).rearrange("p (b n) -> p b n", b=B)
        vWr = carve(B * 3 * D).rearrange("p (b n) -> p b n", b=B)
        vWs = carve(B * 3 * D).rearrange("p (b n) -> p b n", b=B)
        vWsr = carve(B * 3 * D).rearrange("p (b n) -> p b n", b=B)
        diag = carve(2 * GN).rearrange("p (q n) -> p q n", q=2)
        sinv_rep = diag[:, 0].rearrange("p (k b n) -> p k b n", k=2, b=B)
        spread = carve(G * GN).rearrange("p (q n) -> p q n", q=G)
        e_main = carve(B * S).rearrange("p (b n) -> p b n", b=B)
        e_rem = carve(B * S).rearrange("p (b n) -> p b n", b=B)
        gate_r = carve(2 * GN).rearrange("p (q n) -> p q n", q=2)
        gate_z = carve(2 * GN).rearrange("p (q n) -> p q n", q=2)
        gate_u = carve(2 * GN).rearrange("p (q n) -> p q n", q=2)
        cand = carve(2 * GN).rearrange("p (q n) -> p q n", q=2)
        small = carve(256)
        rms16 = small[:, 0:T]
        mx = small[:, 16:32].rearrange("p (k b q) -> p k b q", k=2, b=B)[:, :, :, 0:2]
        mneg = small[:, 32:36].rearrange("p (k b) -> p k b", k=2)
        ssum = small[:, 36:40].rearrange("p (k b) -> p k b", k=2)
        sinv = small[:, 40:44].rearrange("p (k b) -> p k b", k=2)
        bsum = small[:, 64:64 + 8 * C].rearrange("p (v c) -> p v c", c=C)
        BIH, BHH, SLOTW, INW = 0, 3, 6, 7

        packed = sb("packed", [P, C, D // 4], I32)
        unpacked = sb("unpacked", [P, C, D // 4], I32)
        tern = sb("tern", [P, C, D], BF16)
        qT = xnT[:].bitcast(BF16)
        wscale = sb("wscale", [P, 1])
        amax = sb("amax", [P, G, 3, GT])

        used[0] = 0
        wmha = carve(2 * 4 * C * D).rearrange("p (l w c n) -> p l w c n", l=2, w=4, c=C)
        vmha = carve(2 * 4 * C).rearrange("p (l v c) -> p l v c", l=2, v=4)
        qhT = carve(2 * C * GN).rearrange("p (u c n) -> p u c n", u=2, c=C)
        keys = carve(C * B * 2 * M).rearrange("p (c b h m) -> p c b h m", c=C, b=B, h=2)
        ctxR = carve(C * B * P).rearrange("p (c b n) -> p c b n", c=C, b=B)
        vals = carve(B * H * P + P)
        valsR = carve(B * 4 * P + P)
        probs = carve(2 * H * M).rearrange("p (u h m) -> p u h m", u=2, h=H)
        probsR = carve(2 * H * 32).rearrange("p (u h m) -> p u h m", u=2, h=H)
        probsT = carve(2 * 20 * P).rearrange("p (u h m) -> p u h m", u=2, h=20)
        headsT = carve(2 * C * GN).rearrange("p (u c n) -> p u c n", u=2, c=C)
        smax = carve(2 * H).rearrange("p (u h) -> p u h", u=2)
        nmax = carve(2 * H).rearrange("p (u h) -> p u h", u=2)
        hsum = carve(2 * H).rearrange("p (u h) -> p u h", u=2)
        rsum = carve(2 * H).rearrange("p (u h) -> p u h", u=2)
        bvrow = carve(C * P).rearrange("p (c n) -> p c n", c=C)
        mask16 = sb("mask16", [P, 2])
        mask32 = sb("mask32", [P, 4])
        pidx = sb("pidx", [P, 2], I32)

        side = sb("side", [P, 4608])
        wtri = side[:, 0:3 * C * D].rearrange("p (w c n) -> p w c n", w=3, c=C)
        wtri12 = side[:, 1536:2560].rearrange("p (w c n) -> p w c n", w=2, c=C)
        tri_out = side[:, 2560:4608].rearrange("p (u n) -> p u n", u=2)

        W1 = arena[:, 0:E2 * C * F2].rearrange("p (e n) -> p e n", e=E2)
        W2 = arena[:, E2 * C * F2:].rearrange("p (e n) -> p e n", e=E2)
        b2row = side[:, 0:E2 * D]
        xin = side[:, 2560:3072].rearrange("p (u n) -> p u n", u=2)
        xinT = side[:, 3072:3584].rearrange("p (u n) -> p u n", u=2)
        yout = side[:, 3584:4096].rearrange("p (u n) -> p u n", u=2)
        b1col = side[:, 4096:4096 + E2 * F2 // P]
        wr5 = side[:, 4160:4160 + C * E2].rearrange("p (c n) -> p c n", c=C)
        br5 = side[:, 4176:4176 + E2]
        hpre = xn[:].rearrange("p g t d -> p (g t d)")[:, 0:2048].rearrange("p (u n) -> p u n", u=2)
        hact = xn[:].rearrange("p g t d -> p (g t d)")[:, 2048:4096].rearrange("p (u n) -> p u n", u=2)
        gathered5 = side[:, 0:T * D].rearrange("p (k d) -> p k d", d=D)

        used[0] = 24576
        w6 = carve(3 * C * D).rearrange("p (w c n) -> p w c n", w=3, c=C)
        vec6 = carve(2 * C).rearrange("p (v c) -> p v c", c=C)
        max6 = carve(16)
        kpT6 = carve(C * BM).rearrange("p (c n) -> p c n", c=C)
        kq6 = carve(C * BM).rearrange("p (c n) -> p c n", c=C)
        bias6 = carve(BM)
        bq6 = carve(C * P).rearrange("p (c n) -> p c n", c=C)
        vals6 = carve(B * D).rearrange("p (b n) -> p b n", b=B)
        vals6R = carve(B * D).rearrange("p (b n) -> p b n", b=B)
        sc6 = carve(2 * GT * M).rearrange("p (u t m) -> p u t m", u=2, t=GT)
        probs6T = carve(2 * GN).rearrange("p (u n) -> p u n", u=2)
        probs6R = carve(2 * GN).rearrange("p (u n) -> p u n", u=2)
        col6 = carve(2 * 4 * GT).rearrange("p (u k t) -> p u k t", u=2, k=4)

        GU = arena[:, 0:E4 * C * 2 * F4].rearrange("p (e c n) -> p e c n", e=E4, c=C)
        DOWN0 = E4 * C * 2 * F4
        DW = arena[:, DOWN0:DOWN0 + E4 * D].rearrange("p (e n) -> p e n", e=E4)
        TAIL = DOWN0 + E4 * D
        sgate = side[:, 0:C * FS].rearrange("p (c n) -> p c n", c=C)
        sup = side[:, C * FS:2 * C * FS].rearrange("p (c n) -> p c n", c=C)
        sdown = side[:, 2 * C * FS:2 * C * FS + FS // P * D].rearrange("p (h n) -> p h n", n=D)
        wr7 = side[:, 3072:3072 + C * E4].rearrange("p (c n) -> p c n", c=C)
        br7 = side[:, 3136:3136 + E4]
        tanh_s = xq[:].rearrange("p u n -> p (u n)").bitcast(F32).rearrange("p (u n) -> p u n", u=2)
        xnT_more = arena[:, 28672:28672 + 1024].rearrange("p (c n) -> p c n", c=C)
        xnT_last = side[:, 3200:3200 + 1024].rearrange("p (c n) -> p c n", c=C)
        hshared = arena[:, 30720:30720 + 2048].rearrange("p (h n) -> p h n", n=GN)
        xn_flat = xn[:].rearrange("p g t d -> p (g t d)")
        qin = xn_flat[:, 0:2048].rearrange("p (u t d) -> p u t d", u=2, t=4)
        qinT = xn_flat[:, 2048:4096].rearrange("p (u c n) -> p u c n", u=2, c=C)
        qout = xnT[:].rearrange("p u c n -> p (u c n)").rearrange("p (u n) -> p u n", u=2)
        qtanh = arena[:, 28672:29696].rearrange("p (u t n) -> p u t n", u=2, t=4)
        qhid = arena[:, 29696:30720].rearrange("p (u t n) -> p u t n", u=2, t=4)
        qhidT = arena[:, 30720:31744].rearrange("p (u n) -> p u n", u=2)
        gathered7 = arena[:, 0:T * K4 * D].rearrange("p (t k d) -> p t k d", t=T, k=K4)

        before = sb("before", [P, P], BF16)
        upto = sb("upto", [P, 2, 32], BF16)
        ones_bf = sb("ones_bf", [P, P], BF16)
        iota_e = sb("iota_e", [P, 32])
        iota_n = sb("iota_n", [P, 96])
        zeros = sb("zeros", [P, D])
        route = {}
        for s_, E_, K_, NT_, region in ((5, E2, 1, NT2, xq[:].rearrange("p u n -> p (u n)").bitcast(F32)),
                                      (7, E4, K4, NT4, arena[:, TAIL:28672])):
            at = [0]

            def part(cols, dt=F32):
                r = region[:, at[0]:at[0] + cols]
                at[0] += cols
                return r if dt is F32 else r.bitcast(dt)

            route[s_] = dict(
                E=E_, K=K_, NT=NT_,
                logits=part(T * E_).rearrange("p (t e) -> p t e", t=T),
                top=part(T * 8).rearrange("p (t k) -> p t k", k=8),
                index=part(T * 8, U32).rearrange("p (t k) -> p t k", k=8),
                index_f=part(T * K_).rearrange("p (t k) -> p t k", k=K_),
                hot=part(T * K_ * E_ // 2, BF16).rearrange("p (t k e) -> p t k e", t=T, k=K_),
                any_hot=part(T * E_ // 2, BF16).rearrange("p (t e) -> p t e", t=T),
                earlier=part((T + 1) * E_ // 2, BF16).rearrange("p (t e) -> p t e", t=T + 1),
                place=part(T * E_).rearrange("p (t e) -> p t e", t=T),
                picked=part(T * E_).rearrange("p (t e) -> p t e", t=T),
                slot=part(T * K_).rearrange("p (t k) -> p t k", k=K_),
                slot_i=part(T * K_, I32).rearrange("p (t k) -> p t k", k=K_),
                start=part(2 * E_),
                share=part(T * K_).rearrange("p (t k) -> p t k", k=K_) if K_ > 1 else None,
                total=part(2 * T) if K_ > 1 else None,
                count=part(4),
                count_i=part(2, I32),
                tiles_b=part(P // 2, BF16),
                passed=part(NT_ // 2, BF16),
                expert=part(NT_, I32) if s_ == 7 else sb(f"expert{s_}", [1, NT_], I32)[:],
                expert_f=part(NT_) if s_ == 7 else sb(f"expert_f{s_}", [1, NT_])[:])
            assert at[0] <= region.shape[1], at[0]

        def head_steps():
            for n in range(-1, T + 1):
                g, t = n // GT, n % GT
                ops = []
                if n == -1:
                    ops += [("turn", 0), ("query", 0)]
                score = [("score", n + 1, k) for k in range(4)] if n + 1 < T else []
                turn = [("weights", n, k) for k in range(5)] if 0 <= n < T else []
                weigh = [("values", n - 1, c) for c in range(C)] if n >= 1 else []
                ops += score[0:2] + turn[0:2] + score[2:3] + weigh[0:1] + turn[2:3] + score[3:4] + weigh[1:2] + turn[3:5]
                if n >= 0 and t == 1 and g + 1 < G:
                    ops.append(("turn", g + 1))
                if n >= 0 and t == 2 and g + 1 < G:
                    ops.append(("query", g + 1))
                if n >= GT and t == 0:
                    ops.append(("project", g - 1))
                yield n, ops

        ring = {}
        for n, ops in head_steps():
            for op in ops:
                if op[0] == "weights":
                    ring[op] = len(ring)
                elif op[0] in ("turn", "query"):
                    for c in range(C):
                        ring[op + (c,)] = len(ring)
        RING = len(ring)
        assert RING % 2 == 0

        x_loaded = sem("x_loaded")
        ctx_loaded = sem("ctx_loaded")
        gains_loaded = sem("gains_loaded")
        w0_loaded = sem("w0_loaded")
        unpacked_ready = sem("unpacked_ready")
        out_stored = sem("out_stored")
        w1_loaded = sem("w1_loaded")
        rows_loaded = sem("rows_loaded")
        w3_loaded = sem("w3_loaded")
        wmha_loaded = [sem(f"wmha_loaded{l}") for l in range(2)]
        rows_ready = sem("rows_ready")
        row_added = series("row_added", {s: G for s in (1, 2, 4, 6)})
        tern_ready = sem("tern_ready")
        xq_ready = sem("xq_ready")
        masks_made = sem("masks_made")
        project_ready = series("project_ready", {1: G, 3: G})
        tri_folded = sem("tri_folded")
        tri_copied = sem("tri_copied")
        tri_summed = sem("tri_summed")
        tri_tanh = sem("tri_tanh")
        ctxR_made = sem("ctxR_made")
        bv_ready = series("bv_ready", {l: C for l in range(2)})
        context_done = series("context_done", {l: 7 for l in range(2)})
        keys_ready = series("keys_ready", {l: C for l in range(2)})
        vals_ready = series("vals_ready", {l: B for l in range(2)})
        cvec_ready = series("cvec_ready", {l: 1 for l in range(2)})
        q_ready, half_projected = (series(k, {s: 2 * G for s in (2, 4)}) for k in ("q_ready", "half_projected"))
        half_added = series("half_added", {s: G for s in (2, 4)})
        headsT_ready = [series(f"headsT_ready{c}", {s: G for s in (2, 4)}) for c in range(C)]
        pair_scored, pair_max, pair_exp = (series(k, {s: 4 * T for s in (2, 4)}) for k in ("pair_scored", "pair_max", "pair_exp"))
        half_sums, half_scaled = (series(k, {s: 2 * T for s in (2, 4)}) for k in ("half_sums", "half_scaled"))
        pv_done = series("pv_done", {s: 2 * T for s in (2, 4)})
        ring_filled = series("ring_filled", {s: RING for s in (2, 4)})
        ring_read = [series(f"ring_read{k}", {s: RING // 2 for s in (2, 4)}) for k in range(2)]
        route_consts = sem("route_consts")
        zeroed = sem("zeroed")
        w5_loaded = sem("w5_loaded")
        expert5_loaded = sem("expert5_loaded")
        logits_done, logits_read, hot_ready = (series(k, {s: G for s in (5, 7)}) for k in ("logits_done", "logits_read", "hot_ready"))
        earlier_ready = series("earlier_ready", {s: T for s in (5, 7)})
        ranks_done, count_done, tiles_ready, start_done, slots_ready, passed_ready, expert_done, expert_ready = (
            series(k, {s: 1 for s in (5, 7)}) for k in (
                "ranks_done", "count_done", "tiles_ready", "start_done", "slots_ready", "passed_ready", "expert_done", "expert_ready"))
        scattered = series("scattered", {5: 16 * T, 7: 16 * T * 4})
        in_loaded, stored = ([series(f"{k}{u}", {5: 8 * NT2, 7: 8 * NQ}) for u in range(2)] for k in ("in_loaded", "stored"))
        in_turned, inT_ready = (series(k, {5: NT2, 7: 2 * NQ}) for k in ("in_turned", "inT_ready"))
        hidden_done, out_done, out_ready = (series(k, {5: NT2, 7: NQ}) for k in ("hidden_done", "out_done", "out_ready"))
        hidden_turned = series("hidden_turned", {5: 2 * NT2, 7: NQ})
        hpre_copied, h_act = sem("hpre_copied"), sem("h_act")
        gathered5_in = [sem(f"gathered5_in{g}") for g in range(G)]
        (shares_shifted, shares_exp, shared_hid, shared_done, shared_added, shared_down, shared_tanh, qtanh_ready,
         qgate_ready, qhid_ready, qhidT_ready, w7_loaded) = (
            sem(k) for k in ("shares_shifted", "shares_exp", "shared_hid", "shared_done", "shared_added", "shared_down",
                             "shared_tanh", "qtanh_ready", "qgate_ready", "qhid_ready", "qhidT_ready", "w7_loaded"))
        ws_loaded = sem("ws_loaded")
        gathered7_in = [sem(f"gathered7_in{i}") for i in range(G + 1)]
        w6_loaded, max_found, max_turned, max_diag, max_spread, w6_rounded, kp_done, kp_ready, ctx6_done, ctx6_ready = (
            sem(k) for k in ("w6_loaded", "max_found", "max_turned", "max_diag", "max_spread", "w6_rounded", "kp_done",
                             "kp_ready", "ctx6_done", "ctx6_ready"))
        scored6, scores_read6, max_ready6, exp_ready6, turned6, main_copied6, rest_copied6, pv_done6 = (
            sem(k) for k in ("scored6", "scores_read6", "max_ready6", "exp_ready6", "turned6", "main_copied6",
                             "rest_copied6", "pv_done6"))
        consts_made = sem("consts_made")
        gains_ready = sem("gains_ready")
        dve_step = sem("dve_step")
        xn_ready = Alternate(series("xn_ready_even", {s: G for s in (0, 2, 4, 6)}), series("xn_ready_odd", {s: G for s in (1, 3, 5, 7)}))
        turned = series("turned", {s: G * C for s in (0, 1, 3, 5, 6, 7)})
        xnT_ready = series("xnT_ready", {s: G * C for s in (0, 1, 3, 5, 6, 7)})
        h_ready = sem("h_ready")
        c_sq = sem("c_sq")
        c_ms = sem("c_ms")
        c_rms = sem("c_rms")
        c_pn = sem("c_pn")
        c_kv = sem("c_kv")
        c_kv_copied = sem("c_kv_copied")
        c_kq = sem("c_kq")
        c_kq_copied = sem("c_kq_copied")
        c_vw = sem("c_vw")
        c_vw_copied = sem("c_vw_copied")
        sq_ready = sem("sq_ready")
        ms_ready = sem("ms_ready")
        diag_ready = sem("diag_ready")
        spread_ready = sem("spread_ready")
        spread_copied = sem("spread_copied")
        scores_ready = sem("scores_ready")
        scores_scaled = sem("scores_scaled")
        max_ready = sem("max_ready")
        sinv_spread = sem("sinv_spread")
        exp_ready = sem("exp_ready")
        sinv_ready = sem("sinv_ready")
        vws_ready = sem("vws_ready")
        attn_ready = sem("attn_ready")
        gate_done = {k: sem(f"gate_{k}_done") for k in ("hn", "r", "z", "xn")}
        gate_read = {k: sem(f"gate_{k}_read") for k in ("hn", "r", "z", "xn")}
        cand_ready = sem("cand_ready")
        slotsT_ready = sem("slotsT_ready")
        x_done = Alternate(series("x_done_even", {s: G for s in (0, 2, 4, 6)}), series("x_done_odd", {s: G for s in (1, 3, 5, 7)}))

        xs5 = nc.dram_tensor("xs5", (NT2 * P, D), F32, kind="Internal").ap()
        ys5 = nc.dram_tensor("ys5", (NT2 * P, D), F32, kind="Internal").ap()
        xs7 = nc.dram_tensor("xs7", (NT4 * P, D), F32, kind="Internal").ap()
        ys7 = nc.dram_tensor("ys7", (NT4 * P, D), F32, kind="Internal").ap()
        block = ctx.enter_context(nc.Block())


        def route_constants_gpsimd(pool):
            pool.memset(zeros[:], 0.0).then_inc(route_consts, 1)
            pool.memset(ones_bf[:], 1.0).then_inc(route_consts, 1)
            pool.iota(iota_e[:], [[1, 32]], base=0, channel_multiplier=0,
                      allow_small_or_imprecise_dtypes=True).then_inc(route_consts, 1)
            pool.iota(iota_n[:], [[1, 96]], base=0, channel_multiplier=0,
                      allow_small_or_imprecise_dtypes=True).then_inc(route_consts, 1)
            pool.wait_ge(route_consts, 2)
            pool.affine_select(before[:], ones_bf[:], [[1, P]], ALU.is_gt, 0.0, base=0,
                               channel_multiplier=-1).then_inc(route_consts, 1)
            pool.affine_select(upto[:, 0], ones_bf[:, 0:32], [[1, 32]], ALU.is_gt, 0.0, base=0,
                               channel_multiplier=-1).then_inc(route_consts, 1)
            pool.affine_select(upto[:, 1], ones_bf[:, 0:32], [[1, 32]], ALU.is_ge, 0.0, base=0,
                               channel_multiplier=-1).then_inc(route_consts, 1)

        def place(s, g):
            if s == 7 and g == 2:
                return xnT_more
            return xnT_last if s == 7 and g == 3 else xnT[:, g % 2]

        def route_tensor(pe, s, wr, wr_loaded, free):
            r = route[s]
            E = r["E"]
            pe.wait_ge(*wr_loaded)
            pe.wait_ge(route_consts, 7)
            free()
            for g in range(G):
                turn_group(pe, s, g)
                pe.wait_ge(*xnT_ready.at(s, (g + 1) * C))
                if g >= 2:
                    pe.wait_ge(*logits_read.at(s, g - 1))
                for t in range(GT):
                    for c in range(C):
                        ins = pe.matmul(bank[2 + g % 2][:, t * E:(t + 1) * E], place(s, g)[:, c, t * P:(t + 1) * P], wr[:, c],
                                        start=(c == 0), stop=(c == C - 1))
                ins.then_inc(logits_done.sem, 1)
            pe.wait_ge(*earlier_ready.at(s, T))
            pe.wait_ge(*hot_ready.at(s, G))
            for n in range(T):
                dst = bank[4][:, n * E:(n + 1) * E]
                ins = pe.matmul(dst, before[:], r["any_hot"][:, n], start=True, stop=(n == 0))
                if n:
                    ins = pe.matmul(dst, ones_bf[:], r["earlier"][:, n], start=False, stop=True)
            ins.then_inc(ranks_done.sem, 1)
            pe.matmul(bank[5][0:E, 0:1], r["earlier"][:, T], ones_bf[:, 0:1], start=True, stop=True).then_inc(count_done.sem, 1)
            pe.wait_ge(*tiles_ready.at(s, 1))
            pe.matmul(bank[6][:, 0:E], r["tiles_b"][0:E], upto[0:E, 0, 0:E], start=True, stop=True)
            pe.matmul(bank[6][0:E, E:E + 1], upto[0:E, 1, 0:E], r["tiles_b"][0:E, 0:1], start=True,
                      stop=True).then_inc(start_done.sem, 1)
            pe.wait_ge(*passed_ready.at(s, 1))
            pe.matmul(bank[7][0:1, 0:r["NT"]], ones_bf[0:E, 0:1], r["passed"][0:E], start=True,
                      stop=True).then_inc(expert_done.sem, 1)

        def route_scalar(act, s):
            for g in range(G):
                if g >= 2 and s == 5:
                    act.wait_ge(*logits_done.at(s, g - 1))
                elif g >= 2:
                    act.wait_ge(*x_done.at(6, G))
                copy_turned(act, s, g, place(s, g))

        def route_vector(dve, ch, s, br):
            r = route[s]
            E, K, NT = r["E"], r["K"], r["NT"]
            dve.wait_ge(route_consts, 7)
            for g in range(G):
                ts_ = slice(g * GT, (g + 1) * GT)
                dve.wait_ge(*logits_done.at(s, g + 1))
                dve.tensor_tensor(r["logits"][:, ts_], bank[2 + g % 2][:, 0:GT * E].rearrange("p (t e) -> p t e", t=GT),
                                  br.unsqueeze(1).broadcast_to([P, GT, E]), ALU.add).then_inc(logits_read.sem, 1)
                dve.wait_ge(*logits_read.at(s, g + 1))
                for n in range(g * GT, (g + 1) * GT):
                    ch.step(dve.max(r["top"][:, n], r["logits"][:, n]))
                ch.settle()
                for n in range(g * GT, (g + 1) * GT):
                    ch.step(dve.max_index(r["index"][:, n], r["top"][:, n], r["logits"][:, n]))
                ch.settle()
                ch.step(dve.tensor_copy(r["index_f"][:, ts_], r["index"][:, ts_, 0:K]))
                ch.settle()
                ins = dve.tensor_tensor(r["hot"][:, ts_].rearrange("p t k e -> p (t k) e"),
                                        iota_e[:, 0:E].unsqueeze(1).broadcast_to([P, GT * K, E]),
                                        r["index_f"][:, ts_].rearrange("p t k -> p (t k)").unsqueeze(2).broadcast_to([P, GT * K, E]),
                                        ALU.is_equal)
                ch.step(ins)
                ch.settle()
                with nc.allow_low_precision(reason="sums of zeros and ones"):
                    dve.tensor_reduce(r["any_hot"][:, ts_], r["hot"][:, ts_].rearrange("p t k e -> p t e k"), AX.X,
                                      ALU.add).then_inc(hot_ready.sem, 1)
                for n in range(g * GT, (g + 1) * GT):
                    dve.wait_ge(*hot_ready.at(s, g + 1))
                    if n:
                        dve.wait_ge(*earlier_ready.at(s, n))
                        ins = dve.tensor_tensor(r["earlier"][:, n + 1], r["earlier"][:, n], r["any_hot"][:, n], ALU.add)
                    else:
                        ins = dve.tensor_copy(r["earlier"][:, 1], r["any_hot"][:, 0])
                    ins.then_inc(earlier_ready.sem, 1)
            dve.wait_ge(*count_done.at(s, 1))
            ch.step(dve.tensor_scalar(r["count_i"][0:E, 0:1], bank[5][0:E, 0:1], P - 1.0, None, ALU.add))
            ch.settle()
            ch.step(dve.tensor_scalar(r["count_i"][0:E, 1:2], r["count_i"][0:E, 0:1], 7, None, ALU.arith_shift_right))
            ch.settle()
            ch.step(dve.tensor_copy(r["count"][0:E, 0:1], r["count_i"][0:E, 1:2]))
            ch.settle()
            dve.tensor_scalar(r["tiles_b"][0:E], ones[0:E], r["count"][0:E, 0:1], None, ALU.mult).then_inc(tiles_ready.sem, 1)
            dve.wait_ge(*start_done.at(s, 1))
            ch.step(dve.tensor_copy(r["start"][:, 0:E], bank[6][:, 0:E]))
            ch.step(dve.tensor_copy(r["count"][0:E, 1:2], bank[6][0:E, E:E + 1]))
            ch.settle()
            dve.tensor_scalar(r["passed"][0:E], iota_n[0:E, 0:NT], r["count"][0:E, 1:2], None,
                              ALU.is_ge).then_inc(passed_ready.sem, 1)
            dve.wait_ge(*ranks_done.at(s, 1))
            ch.step(dve.scalar_tensor_tensor(r["place"], r["start"][:, 0:E].unsqueeze(1).broadcast_to([P, T, E]), float(P),
                                             bank[4][:, 0:T * E].rearrange("p (t e) -> p t e", t=T), ALU.mult, ALU.add))
            ch.settle()
            for k in range(K):
                ch.step(dve.tensor_tensor(r["picked"], r["hot"][:, :, k], r["place"], ALU.mult))
                ch.settle()
                ch.step(dve.tensor_reduce(r["slot"][:, :, k], r["picked"], AX.X, ALU.add))
                ch.settle()
            dve.tensor_copy(r["slot_i"], r["slot"]).then_inc(slots_ready.sem, 1)
            dve.wait_ge(*expert_done.at(s, 1))
            ch.step(dve.tensor_scalar(r["expert_f"][0:1], bank[7][0:1, 0:NT], float(E - 1), None, ALU.min))
            ch.settle()
            names = r["expert_f"][0:1]
            if s == 7:
                quad = names.rearrange("p (q t) -> p q t", t=4)
                for t in range(2, -1, -1):
                    ch.step(dve.scalar_tensor_tensor(quad[:, :, t], quad[:, :, t + 1], float(E4), quad[:, :, t], ALU.mult, ALU.add))
                    ch.settle()
                names = quad[:, :, 0]
            dve.tensor_copy(r["expert"][0:1, 0:names.shape[1]], names).then_inc(expert_ready.sem, 1)

        def scatter_gpsimd(pool, s, xs):
            r = route[s]
            pool.wait_ge(*slots_ready.at(s, 1))
            pool.wait_ge(zeroed, 2 * 16)
            for n in range(T):
                for k in range(r["K"]):
                    pool.indirect_dma_start(xs, bass.IndirectOffsetOnAxis(r["slot_i"][:, n, k:k + 1].bitcast(U32), 0),
                                            xn[:, n // GT, n % GT], None).then_inc(scattered.sem, 16)

        def shares_vector(dve, ch):
            r = route[7]
            top, share, total = r["top"][:, :, 0:K4], r["share"], r["total"]
            ch.step(dve.tensor_tensor(share, top, top[:, :, 0:1].broadcast_to([P, T, K4]), ALU.subtract))
            ch.settle()
            dve.tensor_copy(total[:, T:T + 1], gain(7)).then_inc(shares_shifted, 1)
            dve.wait_ge(shares_exp, 1)
            ch.step(dve.tensor_reduce(total[:, 0:T], share, AX.X, ALU.add))
            ch.settle()
            ch.step(dve.reciprocal(total[:, 0:T], total[:, 0:T]))
            ch.settle()
            ch.step(dve.tensor_scalar(total[:, 0:T], total[:, 0:T], gain(7), None, ALU.mult))
            ch.settle()
            ch.step(dve.tensor_tensor(share, share, total[:, 0:T].unsqueeze(2).broadcast_to([P, T, K4]), ALU.mult))

        def shared_tensor(pe, groups):
            def hidden(k):
                g, h = k // 4, k % 4
                if k >= 2:
                    pe.wait_ge(shared_hid, k - 1)
                for j, w in enumerate((sgate, sup)):
                    for c in range(C):
                        ins = pe.matmul(bank[2 * (k % 2) + j], w[:, c, h * P:(h + 1) * P], place(7, g)[:, c],
                                        start=(c == 0), stop=(c == C - 1))
                ins.then_inc(shared_done, 1)

            def down(g):
                pe.wait_ge(shared_hid, 4 * (g + 1))
                for t in range(GT):
                    if g and t % 2 == 0:
                        pe.wait_ge(shared_added, 2 * (g - 1) + t // 2 + 1)
                    for h in range(4):
                        ins = pe.matmul(bank[6 + t // 2][:, (t % 2) * D:(t % 2 + 1) * D], hshared[:, h, t * P:(t + 1) * P],
                                        sdown[:, h], start=(h == 0), stop=(h == 3))
                    if t % 2:
                        ins.then_inc(shared_down, 1)

            pe.wait_ge(*slots_ready.at(7, 1))
            pe.wait_ge(*expert_ready.at(7, 1))
            pe.wait_ge(*logits_read.at(7, G))
            for k in range(4 * groups[0], 4 * groups[-1] + 4):
                hidden(k)
                if k % 4 == 0 and k // 4 - 1 in groups:
                    down(k // 4 - 1)
            down(groups[-1])

        def shared_scalar(act, groups):
            if groups[0] == 0:
                act.wait_ge(shares_shifted, 1)
                act.activation(route[7]["share"], route[7]["share"], ACT.Exp).then_inc(shares_exp, 1)
            for k in range(4 * groups[0], 4 * groups[-1] + 4):
                act.wait_ge(shared_done, k + 1)
                act.activation(tanh_s[:, k % 2], bank[2 * (k % 2)], ACT.Tanh, scale=0.5).then_inc(shared_tanh, 1)

        def shared_vector(dve, ch, groups):
            def add(g):
                for half in range(2):
                    dve.wait_ge(shared_down, 2 * g + half + 1)
                    t0 = g * GT + 2 * half
                    xs = x_tok[:, t0:t0 + 2].rearrange("p t d -> p (t d)")
                    dve.scalar_tensor_tensor(xs, bank[6 + half], gain(7), xs, ALU.mult, ALU.add).then_inc(shared_added, 1)

            for k in range(4 * groups[0], 4 * groups[-1] + 4):
                g, h = k // 4, k % 4
                dve.wait_ge(shared_tanh, k + 1)
                ch.step(dve.scalar_tensor_tensor(tanh_s[:, k % 2], tanh_s[:, k % 2], 1.0, bank[2 * (k % 2)], ALU.add, ALU.mult))
                if h == 0 and g:
                    dve.wait_ge(shared_down, 2 * g)
                ch.settle()
                dve.scalar_tensor_tensor(hshared[:, h], tanh_s[:, k % 2], 0.5, bank[2 * (k % 2) + 1], ALU.mult,
                                         ALU.mult).then_inc(shared_hid, 1)
                if h == 0 and g - 1 in groups:
                    add(g - 1)
            add(groups[-1])

        def quads_sync(sp):
            def load(q, u):
                sp.dma_start(qin[:, u], xs7[bass.ds(q * 4 * P, 4 * P), :].rearrange("(t p) d -> p t d", p=P)
                             ).then_inc(in_loaded[u].sem, 16)

            def store(q, u):
                sp.dma_start(ys7[bass.ds(q * 4 * P, 4 * P), :].rearrange("(t p) d -> p t d", p=P),
                             qout[:, u].rearrange("p (t d) -> p t d", d=D)).then_inc(stored[u].sem, 16)

            sp.wait_ge(*scattered.at(7, T * K4 * 16))
            load(0, 0)
            load(1, 1)

            def step(q, u, first=False):
                sp.wait_ge(*in_turned.at(7, 2 * (q + 1)))
                load(q + 2, u)
                if not first:
                    sp.wait_ge(*out_ready.at(7, q))
                    store(q - 1, 1 - u)

            step(0, 0, first=True)
            step(1, 1)
            with sp.Fori(1, NQ // 2 - 1) as j:
                step(2 * j, 0)
                step(2 * j + 1, 1)
            for q in range(NQ - 3, NQ):
                sp.wait_ge(*out_ready.at(7, q + 1))
                store(q, q % 2)

        def quads_tensor(pe):
            ex = route[7]["expert"]

            def experts_of(q):
                word = pe.value_load(ex[0:1, bass.ds(q, 1)], min_val=0, max_val=E4 ** 4 - 1)
                return [(word >> (5 * t)) & (E4 - 1) for t in range(4)]

            def turn_in(u, turn):
                pe.wait_ge(*in_loaded[u].at(7, 16 * turn + 16))
                for c in range(C):
                    for t in range(4):
                        ins = pe.transpose(bank[c][:, t * P:(t + 1) * P], qin[:, u, t, c * P:(c + 1) * P], ident[:])
                    ins.then_inc(in_turned.sem, 1)

            def hidden(q, u, experts):
                pe.wait_ge(*inT_ready.at(7, 2 * q + 2))
                for t, e in enumerate(experts):
                    for c in range(C):
                        ins = pe.matmul(bank[2 + t // 2][:, (t % 2) * 2 * F4:(t % 2 + 1) * 2 * F4],
                                        qinT[:, u, c, t * P:(t + 1) * P],
                                        arena[:, bass.ds(e * (C * 2 * F4) + c * 2 * F4, 2 * F4)],
                                        start=(c == 0), stop=(c == C - 1))
                ins.then_inc(hidden_done.sem, 1)

            def turn_hidden(q, u):
                pe.wait_ge(qhid_ready, q + 1)
                for t in range(4):
                    ins = pe.transpose(bank[4][:, t * P:(t + 1) * P], qhid[:, u, t], ident[:])
                ins.then_inc(hidden_turned.sem, 1)

            def output(q, u, experts, first=False):
                if not first:
                    pe.wait_ge(*out_ready.at(7, q))
                pe.wait_ge(qhidT_ready, q + 1)
                for t, e in enumerate(experts):
                    ins = pe.matmul(bank[6 + t // 2][:, (t % 2) * D:(t % 2 + 1) * D], qhidT[:, u, t * P:(t + 1) * P],
                                    arena[:, bass.ds(e * D + DOWN0, D)], start=True, stop=True)
                ins.then_inc(out_done.sem, 1)

            def step(q, u, turn, first=False):
                now, ahead = experts_of(q), experts_of(q + 1)
                hidden(q + 1, 1 - u, ahead)
                turn_in(u, turn)
                output(q, u, now, first)
                turn_hidden(q + 1, 1 - u)

            pe.wait_ge(w7_loaded, 8 * 16)
            turn_in(0, 0)
            pe.wait_ge(shared_hid, 4 * (G - 1))
            hidden(0, 0, experts_of(0))
            turn_in(1, 0)
            turn_hidden(0, 0)
            pe.wait_ge(shared_added, 2 * (G - 1))
            step(0, 0, 1, first=True)
            with pe.Fori(0, NQ // 2 - 2) as j:
                step(2 * j + 1, 1, j + 1)
                step(2 * j + 2, 0, j + 2)
            step(NQ - 3, 1, NQ // 2 - 1)
            hidden(NQ - 1, 1, experts_of(NQ - 1))
            output(NQ - 2, 0, experts_of(NQ - 2))
            turn_hidden(NQ - 1, 1)
            output(NQ - 1, 1, experts_of(NQ - 1))

        def quads_scalar(act):
            def copy_in(q, u):
                for c in range(C):
                    act.wait_ge(*in_turned.at(7, 2 * q + c + 1))
                    act.activation(qinT[:, u, c], bank[c], ACT.Copy).then_inc(inT_ready.sem, 1)

            def tanh_gate(q, u):
                act.wait_ge(*hidden_done.at(7, q + 1))
                gate = psum[:, 2:4].rearrange("p b (t w n) -> p (b t) w n", t=2, w=2)[:, :, 0]
                act.activation(qtanh[:, u], gate, ACT.Tanh, scale=0.5).then_inc(qtanh_ready, 1)

            def copy_hidden(q, u):
                act.wait_ge(*hidden_turned.at(7, q + 1))
                act.activation(qhidT[:, u], bank[4], ACT.Copy).then_inc(qhidT_ready, 1)

            copy_in(0, 0)
            tanh_gate(0, 0)
            copy_in(1, 1)
            copy_hidden(0, 0)
            with act.Fori(0, NQ // 2 - 1) as j:
                for u in range(2):
                    tanh_gate(2 * j + u + 1, 1 - u)
                    copy_in(2 * j + u + 2, u)
                    copy_hidden(2 * j + u + 1, 1 - u)
            tanh_gate(NQ - 1, 1)
            copy_hidden(NQ - 1, 1)

        def quads_vector(dve):
            up = psum[:, 2:4].rearrange("p b (t w n) -> p (b t) w n", t=2, w=2)[:, :, 1]
            gate = psum[:, 2:4].rearrange("p b (t w n) -> p (b t) w n", t=2, w=2)[:, :, 0]

            def hidden(q, u):
                dve.wait_ge(qtanh_ready, q + 1)
                dve.scalar_tensor_tensor(qtanh[:, u], qtanh[:, u], 1.0, gate, ALU.add, ALU.mult).then_inc(qgate_ready, 1)
                dve.wait_ge(qgate_ready, q + 1)
                dve.scalar_tensor_tensor(qhid[:, u], qtanh[:, u], 0.5, up, ALU.mult, ALU.mult).then_inc(qhid_ready, 1)

            def copy_out(q, u):
                dve.wait_ge(*out_done.at(7, q + 1))
                dve.tensor_copy(qout[:, u], psum[:, 6:8].rearrange("p b n -> p (b n)")).then_inc(out_ready.sem, 1)

            hidden(0, 0)
            hidden(1, 1)
            copy_out(0, 0)
            hidden(2, 0)
            copy_out(1, 1)
            with dve.Fori(1, NQ // 2 - 1) as j:
                hidden(2 * j + 1, 1)
                dve.wait_ge(*stored[0].at(7, 16 * j))
                copy_out(2 * j, 0)
                hidden(2 * j + 2, 0)
                dve.wait_ge(*stored[1].at(7, 16 * j))
                copy_out(2 * j + 1, 1)
            hidden(NQ - 1, 1)
            for u in range(2):
                dve.wait_ge(*stored[u].at(7, 16 * (NQ // 2 - 1)))
                copy_out(NQ - 2 + u, u)

        combined7 = [range(g * GT, (g + 1) * GT) for g in range(G - 1)]
        combined7 += [range(T - GT, T - GT // 2), range(T - GT // 2, T)]

        def gather7_gpsimd(pool):
            for u in range(2):
                pool.wait_ge(*stored[u].at(7, NQ // 2 * 16))
            for i, tiles in enumerate(combined7):
                for n in tiles:
                    for k in range(K4):
                        pool.indirect_dma_start(gathered7[:, n, k], None, ys7, bass.IndirectOffsetOnAxis(
                            route[7]["slot_i"][:, n, k:k + 1].bitcast(U32), 0)).then_inc(gathered7_in[i], 16)

        def combine7_vector(dve, ch):
            dve.wait_ge(shared_added, 2 * G)
            ch.settle()
            for i, tiles in enumerate(combined7):
                dve.wait_ge(gathered7_in[i], 16 * len(tiles) * K4)
                for k in range(K4):
                    for n in tiles:
                        ins = dve.scalar_tensor_tensor(x_tok[:, n], gathered7[:, n, k], route[7]["share"][:, n, k:k + 1],
                                                       x_tok[:, n], ALU.mult, ALU.add)
                        if k < K4 - 1:
                            ch.step(ins)
                    ch.settle()
                if tiles[-1] % GT == GT - 1:
                    ins.then_inc(x_done.of(7), 1)

        def expert_tiles_sync(sp):
            def load(i, u):
                sp.dma_start(xin[:, u], xs5[bass.ds(i * P, P), :]).then_inc(in_loaded[u].sem, 16)

            def store(i, u):
                sp.dma_start(ys5[bass.ds(i * P, P), :], yout[:, u]).then_inc(stored[u].sem, 16)

            sp.wait_ge(*scattered.at(5, T * 16))
            load(0, 0)
            load(1, 1)

            def step(q, u, first=False):
                sp.wait_ge(*in_turned.at(5, q + 1))
                load(q + 2, u)
                if not first:
                    sp.wait_ge(*out_ready.at(5, q))
                    store(q - 1, 1 - u)

            step(0, 0, first=True)
            step(1, 1)
            with sp.Fori(1, NT2 // 2 - 1) as j:
                step(2 * j, 0)
                step(2 * j + 1, 1)
            for q in range(NT2 - 3, NT2):
                sp.wait_ge(*out_ready.at(5, q + 1))
                store(q, q % 2)

        def expert_tiles_tensor(pe):
            ex = route[5]["expert"]

            def turn_in(u, turn):
                pe.wait_ge(*in_loaded[u].at(5, 16 * turn + 16))
                for c in range(C):
                    ins = pe.transpose(bank[0][:, c * P:(c + 1) * P], xin[:, u, c * P:(c + 1) * P], ident[:])
                ins.then_inc(in_turned.sem, 1)

            def hidden(i, u, e):
                pe.wait_ge(*inT_ready.at(5, i + 1))
                for h in range(2):
                    for c in range(C):
                        ins = pe.matmul(bank[2 + h], xinT[:, u, c * P:(c + 1) * P],
                                        W1[:, e, c * F2 + h * 512:c * F2 + h * 512 + 512] if isinstance(e, int) else
                                        arena[:, bass.ds(e * (C * F2) + (c * F2 + h * 512), 512)],
                                        start=(c == 0), stop=(c == C - 1))
                ins.then_inc(hidden_done.sem, 1)

            def turn_hidden(i, u):
                pe.wait_ge(hpre_copied, i + 1)
                for k in range(8):
                    ins = pe.transpose(bank[4 + k // 4][:, k % 4 * P:(k % 4 + 1) * P], hpre[:, u, k * P:(k + 1) * P], ident[:])
                    if k % 4 == 3:
                        ins.then_inc(hidden_turned.sem, 1)

            def output(i, u, e):
                pe.wait_ge(h_act, (i + 1) * 2)
                for k in range(8):
                    ins = pe.matmul(bank[6 + u][:, 0:D], hact[:, u, k * P:(k + 1) * P],
                                    arena[:, bass.ds(e * (8 * D) + (E2 * C * F2 + k * D), D)], start=(k == 0), stop=(k == 7))
                ins.then_inc(out_done.sem, 1)

            def expert_of(i):
                return pe.value_load(ex[0:1, bass.ds(i, 1)], min_val=0, max_val=E2 - 1)

            pe.wait_ge(*expert_ready.at(5, 1))
            pe.wait_ge(*logits_read.at(5, G))
            pe.wait_ge(*slots_ready.at(5, 1))
            pe.wait_ge(expert5_loaded, 2 * E2 * 16)
            def step(i, u, turn):
                now, ahead = expert_of(i), expert_of(i + 1)
                hidden(i + 1, 1 - u, ahead)
                turn_in(u, turn)
                output(i, u, now)
                turn_hidden(i + 1, 1 - u)

            turn_in(0, 0)
            hidden(0, 0, expert_of(0))
            turn_in(1, 0)
            turn_hidden(0, 0)
            step(0, 0, 1)
            with pe.Fori(0, NT2 // 2 - 2) as j:
                step(2 * j + 1, 1, j + 1)
                step(2 * j + 2, 0, j + 2)
            step(NT2 - 3, 1, NT2 // 2 - 1)
            hidden(NT2 - 1, 1, expert_of(NT2 - 1))
            output(NT2 - 2, 0, expert_of(NT2 - 2))
            turn_hidden(NT2 - 1, 1)
            output(NT2 - 1, 1, expert_of(NT2 - 1))

        def expert_tiles_scalar(act):
            ex = route[5]["expert"]
            act.wait_ge(*expert_ready.at(5, 1))

            def copy_in(i, u):
                act.wait_ge(*in_turned.at(5, i + 1))
                act.activation(xinT[:, u], bank[0][:, 0:C * P], ACT.Copy).then_inc(inT_ready.sem, 1)

            def rectify(i, u):
                e = act.value_load(ex[0:1, bass.ds(i, 1)], min_val=0, max_val=E2 - 1)
                for k in range(8):
                    if k % 4 == 0:
                        act.wait_ge(*hidden_turned.at(5, 2 * i + k // 4 + 1))
                    ins = act.activation(hact[:, u, k * P:(k + 1) * P], bank[4 + k // 4][:, k % 4 * P:(k % 4 + 1) * P],
                                         ACT.Relu, bias=b1col[:, bass.ds(e * 8 + k, 1)])
                    if k % 4 == 3:
                        ins.then_inc(h_act, 1)

            copy_in(0, 0)
            copy_in(1, 1)
            rectify(0, 0)
            with act.Fori(0, NT2 // 2 - 1) as j:
                for u in range(2):
                    copy_in(2 * j + u + 2, u)
                    rectify(2 * j + u + 1, 1 - u)
            rectify(NT2 - 1, 1)

        def expert_tiles_vector(dve):
            ex = route[5]["expert"]

            def copy_hidden(i, u):
                dve.wait_ge(*hidden_done.at(5, i + 1))
                dve.tensor_copy(hpre[:, u], psum[:, 2:4].rearrange("p b n -> p (b n)")).then_inc(hpre_copied, 1)

            def copy_out(i, u):
                e = dve.value_load(ex[0:1, bass.ds(i, 1)], min_val=0, max_val=E2 - 1)
                dve.wait_ge(*out_done.at(5, i + 1))
                dve.tensor_tensor(yout[:, u], bank[6 + u][:, 0:D], b2row[:, bass.ds(e * D, D)], ALU.add).then_inc(out_ready.sem, 1)

            dve.wait_ge(w5_loaded, 4 * 16)
            dve.wait_ge(*expert_ready.at(5, 1))
            dve.wait_ge(*scattered.at(5, T * 16))
            def steps(j):
                copy_hidden(2 * j + 1, 1)
                dve.wait_ge(*stored[0].at(5, 16 * j))
                copy_out(2 * j, 0)
                copy_hidden(2 * j + 2, 0)
                dve.wait_ge(*stored[1].at(5, 16 * j))
                copy_out(2 * j + 1, 1)

            copy_hidden(0, 0)
            copy_hidden(1, 1)
            copy_out(0, 0)
            copy_hidden(2, 0)
            copy_out(1, 1)
            with dve.Fori(1, NT2 // 2 - 1) as j:
                steps(j)
            copy_hidden(NT2 - 1, 1)
            for u in range(2):
                dve.wait_ge(*stored[u].at(5, 16 * (NT2 // 2 - 1)))
                copy_out(NT2 - 2 + u, u)

        def gather_gpsimd(pool):
            for u in range(2):
                pool.wait_ge(*stored[u].at(5, NT2 // 2 * 16))
            for n in range(T):
                pool.indirect_dma_start(gathered5[:, n], None, ys5,
                                        bass.IndirectOffsetOnAxis(route[5]["slot_i"][:, n, 0:1].bitcast(U32), 0)
                                        ).then_inc(gathered5_in[n // GT], 16)

        def combine_parts(dve, ch, g):
            dve.wait_ge(gathered5_in[g], 16 * GT)
            for n in range(g * GT, (g + 1) * GT):
                ins = dve.scalar_tensor_tensor(x_tok[:, n], gathered5[:, n], gain(5), x_tok[:, n], ALU.mult, ALU.add)
                if n % GT == GT - 1:
                    ins.then_inc(x_done.of(5), 1)
                yield
            yield from next_norm_parts(dve, ch, 5, g)

        def single_context_tensor(pe):
            pe.wait_ge(max_found, 3)
            pe.wait_ge(*inT_ready.at(5, NT2))
            pe.wait_ge(*out_ready.at(5, NT2))
            pe.transpose(bank[0][0:3, 0:P], max6[:, 0:3], ident[:]).then_inc(max_turned, 1)
            pe.wait_ge(max_diag, 1)
            pe.matmul(bank[1][:, 0:3], ones[0:3], max6[0:3, 4:7], start=True, stop=True).then_inc(max_spread, 1)
            pe.wait_ge(w6_rounded, 1)
            for o in range(C):
                for c in range(C):
                    ins = pe.matmul(bank[2 + o][:, 0:BM], w6[:, 0, c, o * P:(o + 1) * P], ctxT[:, c],
                                    start=(c == 0), stop=(c == C - 1))
                ins.then_inc(kp_done, 1)
            pe.wait_ge(w6_rounded, 2)
            for b in range(B):
                for c in range(C):
                    ins = pe.matmul(bank[7][:, b * D:(b + 1) * D], ctxT[:, c, b * M:b * M + P], w6[:, 1, c],
                                    start=(c == 0), stop=(c == C - 1))
            ins.then_inc(ctx6_done, 1)
            for b in range(B):
                for c in range(C):
                    ins = pe.matmul(bank[0][0:MR, b * D:(b + 1) * D], ctxT[:, c, b * M + P:(b + 1) * M], w6[:, 1, c],
                                    start=(c == 0), stop=(c == C - 1))
            ins.then_inc(ctx6_done, 1)
            pe.wait_ge(w6_rounded, 3)
            pe.wait_ge(kp_ready, C)
            for o in range(C):
                for c in range(C):
                    ins = pe.matmul(bank[4 + o][:, 0:BM], w6[:, 2, c, o * P:(o + 1) * P], kpT6[:, c],
                                    start=(c == 0), stop=(c == C - 1))
                ins.then_inc(ctx6_done, 1)
            for c in range(C):
                ins = pe.matmul(bank[6][:, 0:BM], bq6[:, c], kpT6[:, c], start=(c == 0), stop=(c == C - 1))
            ins.then_inc(ctx6_done, 1)

        def single_context_scalar(act):
            act.wait_ge(w6_loaded, 4 * 16)
            for o in range(C):
                act.wait_ge(kp_done, o + 1)
                act.activation(kpT6[:, o], bank[2 + o][:, 0:BM], ACT.Identity, bias=vec6[:, 1, o:o + 1]).then_inc(kp_ready, 1)

        def single_context_vector(dve, ch):
            dve.wait_ge(w6_loaded, 4 * 16)
            for k in range(3):
                dve.tensor_reduce(max6[:, k:k + 1], w6[:, k].rearrange("p c n -> p (c n)"), AX.X, ALU.max,
                                  apply_absolute_value=True).then_inc(max_found, 1)
            for c in range(C):
                ch.step(dve.tensor_scalar(bq6[:, c], ones[:], vec6[:, 0, c:c + 1], None, ALU.mult))
            dve.wait_ge(max_turned, 1)
            ch.step(dve.tensor_reduce(max6[0:3, 3:4], bank[0][0:3, 0:P], AX.X, ALU.max))
            ch.settle()
            dve.tensor_scalar(max6[0:3, 4:7], ident[0:3, 0:3], max6[0:3, 3:4], None, ALU.mult).then_inc(max_diag, 1)
            dve.wait_ge(max_spread, 1)
            ch.step(dve.tensor_scalar(max6[:, 8:11], bank[1][:, 0:3], 1.0 / 128, None, ALU.mult))
            ch.settle()
            ch.step(dve.reciprocal(max6[:, 12:15], max6[:, 8:11]))
            ch.settle()
            for k in range(3):
                w = w6[:, k].rearrange("p c n -> p (c n)")
                ch.step(dve.tensor_scalar(w, w, max6[:, 12 + k:13 + k], ROUND, ALU.mult, ALU.add))
                ch.settle()
                dve.tensor_scalar(w, w, -ROUND, max6[:, 8 + k:9 + k], ALU.add, ALU.mult).then_inc(w6_rounded, 1)
            dve.wait_ge(ctx6_done, 1)
            dve.tensor_copy(vals6.rearrange("p b n -> p (b n)"), bank[7]).then_inc(ctx6_ready, 1)
            dve.wait_ge(ctx6_done, 2)
            dve.tensor_copy(vals6R[0:MR].rearrange("p b n -> p (b n)"), bank[0][0:MR]).then_inc(ctx6_ready, 1)
            for o in range(C):
                dve.wait_ge(ctx6_done, 3 + o)
                dve.tensor_copy(kq6[:, o], bank[4 + o][:, 0:BM]).then_inc(ctx6_ready, 1)
            dve.wait_ge(ctx6_done, 5)
            dve.tensor_copy(bias6, bank[6][:, 0:BM]).then_inc(ctx6_ready, 1)

        def single_tensor(pe):
            def scores(g):
                b = g // GB
                turn_group(pe, 6, g)
                pe.wait_ge(*xnT_ready.at(6, (g + 1) * C))
                if g == 0:
                    pe.wait_ge(ctx6_ready, 5)
                else:
                    pe.wait_ge(scores_read6, 2 * g)
                for t in range(GT):
                    for c in range(C):
                        ins = pe.matmul(bank[2 + t // 2][:, (t % 2) * M:(t % 2 + 1) * M], xnT[:, g % 2, c, t * P:(t + 1) * P],
                                        kq6[:, c, b * M:(b + 1) * M], start=(c == 0), stop=(c == C - 1))
                    if t % 2:
                        ins.then_inc(scored6, 1)

            pe.wait_ge(ctx6_ready, 2)
            scores(0)
            for g in range(G):
                if g + 1 < G:
                    scores(g + 1)
                u, b = g % 2, g // GB
                pe.wait_ge(exp_ready6, g + 1)
                if g:
                    pe.wait_ge(main_copied6, g)
                for t in range(GT):
                    ins = pe.transpose(bank[4][:, t * P:(t + 1) * P], sc6[:, u, t, 0:P], ident[:])
                ins.then_inc(turned6, 1)
                if g:
                    pe.wait_ge(rest_copied6, g)
                for t in range(GT):
                    ins = pe.transpose(bank[5][0:MR, t * P:(t + 1) * P], sc6[:, u, t, P:M], ident[:])
                ins.then_inc(turned6, 1)
                pe.wait_ge(main_copied6, g + 1)
                pe.wait_ge(rest_copied6, g + 1)
                if g:
                    pe.wait_ge(*x_done.at(6, g))
                for t in range(GT):
                    dst = bank[6 + t // 2][:, (t % 2) * D:(t % 2 + 1) * D]
                    pe.matmul(dst, probs6T[:, u, t * P:(t + 1) * P], vals6[:, b], start=True, stop=False)
                    ins = pe.matmul(dst, probs6R[0:MR, u, t * P:(t + 1) * P], vals6R[0:MR, b], start=False, stop=True)
                    if t % 2:
                        ins.then_inc(pv_done6, 1)

        def single_scalar(act):
            def copy_group(g):
                if g >= 2:
                    act.wait_ge(scored6, 2 * (g - 1))
                copy_turned(act, 6, g, xnT[:, g % 2])

            copy_group(0)
            for g in range(G):
                if g + 1 < G:
                    copy_group(g + 1)
                u = g % 2
                act.wait_ge(max_ready6, g + 1)
                for t in range(GT):
                    ins = act.activation(sc6[:, u, t], sc6[:, u, t], ACT.Exp, bias=col6[:, u, 1, t:t + 1], scale=D ** -0.5,
                                         accum_out=col6[:, u, 2, t:t + 1])
                ins.then_inc(exp_ready6, 1)
                act.wait_ge(turned6, 2 * g + 1)
                if g >= 2:
                    act.wait_ge(pv_done6, 2 * (g - 1))
                act.activation(probs6T[:, u], bank[4], ACT.Copy).then_inc(main_copied6, 1)

        def single_vector(dve, ch):
            def scores(g):
                u, b = g % 2, g // GB
                if g >= 2:
                    dve.wait_ge(turned6, 2 * (g - 1))
                for half in range(2):
                    dve.wait_ge(scored6, 2 * g + half + 1)
                    dve.tensor_tensor(sc6[:, u, 2 * half:2 * half + 2],
                                      bank[2 + half][:, 0:2 * M].rearrange("p (t m) -> p t m", t=2),
                                      bias6[:, b * M:(b + 1) * M].unsqueeze(1).broadcast_to([P, 2, M]),
                                      ALU.add).then_inc(scores_read6, 1)
                dve.wait_ge(scores_read6, 2 * (g + 1))
                ch.step(dve.tensor_reduce(col6[:, u, 0], sc6[:, u], AX.X, ALU.max))
                ch.settle()
                dve.tensor_scalar(col6[:, u, 1], col6[:, u, 0], -D ** -0.5, None, ALU.mult).then_inc(max_ready6, 1)

            def finish(g):
                u = g % 2
                dve.wait_ge(exp_ready6, g + 1)
                ch.step(dve.reciprocal(col6[:, u, 3], col6[:, u, 2]))
                yield
                ch.settle()
                ch.step(dve.tensor_scalar(col6[:, u, 3], col6[:, u, 3], gain(6), None, ALU.mult))
                yield
                dve.wait_ge(turned6, 2 * g + 2)
                if g >= 2:
                    dve.wait_ge(pv_done6, 2 * (g - 1))
                dve.tensor_copy(probs6R[0:MR, u], bank[5][0:MR]).then_inc(rest_copied6, 1)
                yield
                dve.wait_ge(*row_added.at(6, g + 1))
                ch.settle()
                for t in range(GT):
                    dve.wait_ge(pv_done6, 2 * g + t // 2 + 1)
                    xs = x_tok[:, g * GT + t]
                    ins = dve.scalar_tensor_tensor(xs, bank[6 + t // 2][:, (t % 2) * D:(t % 2 + 1) * D], col6[:, u, 3, t:t + 1],
                                                   xs, ALU.mult, ALU.add)
                    if t == GT - 1:
                        ins.then_inc(x_done.of(6), 1)
                    yield

            combined = [combine_parts(dve, ch, g) for g in range(G)]
            run(combined[0])
            run(combined[1])
            scores(0)
            norm = iter(())
            for g in range(G):
                if g + 2 < G:
                    run(combined[g + 2], norm)
                if g + 1 < G:
                    scores(g + 1)
                run(finish(g), norm)
                run(norm)
                norm = next_norm_parts(dve, ch, 6, g)
            run(norm)

        def rsqrt_newton(ch, v, y, t):
            dve = nc.vector
            ch.step(dve.tensor_scalar(y.bitcast(I32), v.bitcast(I32), -0.5, float(RSQRT_MAGIC), ALU.mult, ALU.add))
            k = ch.n
            for _ in range(NEWTON):
                ch.settle(k)
                ch.step(dve.tensor_tensor(t, y, y, ALU.mult))
                k = ch.n
                yield
                ch.settle(k)
                ch.step(dve.scalar_tensor_tensor(t, t, -0.5, v, ALU.mult, ALU.mult))
                k = ch.n
                yield
                ch.settle(k)
                ch.step(dve.scalar_tensor_tensor(y, t, 1.5, y, ALU.add, ALU.mult))
                k = ch.n
                yield
            ch.settle(k)

        def layer_norm_parts(dve, ch, s, g):
            u = g % 2
            for t in range(GT):
                ch.step(dve.bn_stats(stats[:, u, t], x_tok[:, g * GT + t]))
                k = ch.n
                yield
            ch.settle(k)
            for t in range(GT):
                ch.step(dve.bn_aggr(meanvar[:, u, t], stats[:, u, t]))
            k = ch.n
            yield
            ch.settle(k)
            v, y, t_ = (nwt[:, u, k, 0:GT] for k in range(3))
            ch.step(dve.tensor_scalar(v, meanvar[:, u, :, 1], LN_EPS, None, ALU.add))
            k = ch.n
            yield
            ch.settle(k)
            yield from rsqrt_newton(ch, v, y, t_)
            for t in range(GT):
                ins = dve.tensor_scalar(xn[:, g, t], x_tok[:, g * GT + t], meanvar[:, u, t, 0:1],
                                        nwt[:, u, 1, t:t + 1], ALU.subtract, ALU.mult)
                if t == GT - 1:
                    ins.then_inc(xn_ready.of(s), 1)
                k = ch.n
                yield

        def together(*works):
            works = list(works)
            while works:
                works = [w for w in works if next(w, works) is not works]

        def run(parts, between=()):
            between = iter(between)
            for _ in parts:
                next(between, None)
                next(between, None)

        def turn_group(pe, s, g):
            pe.wait_ge(*xn_ready.at(s, g + 1))
            for c in range(C):
                if g >= 1:
                    pe.wait_ge(*xnT_ready.at(s, (g - 1) * C + c + 1))
                for t in range(GT):
                    ins = pe.transpose(bank[c][:, t * P:(t + 1) * P], xn[:, g, t, c * P:(c + 1) * P], ident[:])
                ins.then_inc(turned.sem, 1)

        def copy_turned(act, s, g, dst):
            for c in range(C):
                act.wait_ge(*turned.at(s, g * C + c + 1))
                act.activation(dst[:, c], bank[c][:], ACT.Copy).then_inc(xnT_ready.sem, 1)

        def gain(s):
            k = (4 if s % 2 else 0) + s // 2
            return tanh_g[:, k:k + 1]


        def slot_iterations_gpsimd(pool):
            pool.wait_ge(*xnT_ready.at(0, G * C))
            pool.sem_inc(h_ready, 8)

            def squares(turn, q, first=False):
                pool.wait_ge(h_ready, turn * 8 + 2 * q + 2)
                if not first:
                    pool.wait_ge(ms_ready, turn * G + q - 1)
                pool.tensor_tensor(sq[:, q % 2], hT[:, :, q * GN:(q + 1) * GN], hT[:, :, q * GN:(q + 1) * GN],
                                   ALU.mult).then_inc(sq_ready, 1)

            for q in range(G - 1):
                squares(0, q, first=(q < 2))
            with pool.Fori(0, ITERS) as it:
                squares(it, G - 1)
                for b in range(B):
                    pool.wait_ge(sinv_ready, it * B + b + 1)
                    if b == 0:
                        pool.wait_ge(h_ready, it * 8 + 8)
                    pool.tensor_tensor(vWs[:, b], vW[:, b], sinv[:, 0, b:b + 1].broadcast_to([P, 3 * D]), ALU.mult)
                    pool.tensor_tensor(vWsr[0:MR, b], vWr[0:MR, b], sinv[0:MR, 1, b:b + 1].broadcast_to([MR, 3 * D]),
                                       ALU.mult).then_inc(vws_ready, 1)
                for q in range(G - 1):
                    squares(it + 1, q)

        def mha_constants_gpsimd(pool):
            pool.wait_ge(*x_done.at(0, G))
            pool.memset(ctxR, 0.0).then_inc(ctxR_made, 1)
            pool.memset(vals, 0.0).then_inc(ctxR_made, 1)
            pool.memset(valsR, 0.0).then_inc(ctxR_made, 1)
            pool.memset(probsR, 0.0).then_inc(ctxR_made, 1)
            pool.wait_ge(ctxR_made, 1)
            for c in range(C):
                for b in range(B):
                    pool.tensor_copy(ctxR[:, c, b].rearrange("p (q m) -> p q m", q=4)[:, :, 0:MR],
                                     ctxT[:, c, b * M + P:(b + 1) * M].unsqueeze(1).broadcast_to([P, 4, MR])
                                     ).then_inc(ctxR_made, 1)

        def mha_gpsimd(pool, l, k):
            s = 2 + 2 * l
            for n in range(T):
                u = n % 2
                if n % GT == 0:
                    add_row_gpsimd(pool, s, k, n // GT)
                for half in range(2):
                    hs = slice(8 * half, 8 * half + 8)
                    pool.wait_ge(*half_sums.at(s, 2 * n + half + 1))
                    pool.tensor_tensor(probs[:, u, hs, 0:P], probs[:, u, hs, 0:P],
                                       rsum[:, u, hs].unsqueeze(2).broadcast_to([P, 8, P]), ALU.mult)
                    if half == 0 and n >= 2:
                        pool.wait_ge(*ring_filled.at(s, ring["weights", n - 2, 4] + 1))
                    pool.tensor_tensor(probsR[:, u, hs, 0:MR], probs[:, u, hs, P:M],
                                       rsum[:, u, hs].unsqueeze(2).broadcast_to([P, 8, MR]), ALU.mult).then_inc(half_scaled.sem, 1)

        def add_rows_gpsimd(pool, s, k):
            for g in range(G):
                add_row_gpsimd(pool, s, k, g)

        def add_row_gpsimd(pool, s, k, g):
            pool.wait_ge(*xn_ready.at(s, g + 1))
            xs = x_tok[:, g * GT:(g + 1) * GT]
            pool.tensor_tensor(xs, xs, add_row[:, k].unsqueeze(1).broadcast_to([P, GT, D]), ALU.add).then_inc(row_added.sem, 1)


        def start_slots_tensor(pe):
            for g in range(G):
                turn_group(pe, 0, g)

        def context_slots_tensor(pe):
            pe.wait_ge(*xnT_ready.at(0, G * C))
            pe.wait_ge(c_sq, 1)
            for c in range(C):
                ins = pe.matmul(bank[0][:, 0:BM], ones[:], sq[:, 0, c, 0:BM], start=(c == 0), stop=(c == C - 1))
            ins.then_inc(c_ms, 1)
            pe.wait_ge(w0_loaded, 6 * 16)
            pe.wait_ge(c_pn, C)
            for w in range(2):
                for o in range(C):
                    for c in range(C):
                        ins = pe.matmul(bank[1 + 2 * w + o][:, 0:BM], wqkv0[:, 1 + w, c, o * P:(o + 1) * P],
                                        PnT[:, c], start=(c == 0), stop=(c == C - 1))
                    ins.then_inc(c_kv, 1)
            pe.wait_ge(c_kv_copied, 4)
            for o in range(C):
                for c in range(C):
                    ins = pe.matmul(bank[1 + o][:, 0:BM], wqkv0[:, 0, c, o * P:(o + 1) * P], kvT[:, 0, c],
                                    start=(c == 0), stop=(c == C - 1))
                ins.then_inc(c_kq, 1)
            half = 3 * D // 2
            for b in range(B):
                for k, (lo, n) in enumerate(((0, P), (P, MR))):
                    j = b * 2 + k
                    if j >= 1:
                        pe.wait_ge(c_vw_copied, j)
                    for h in range(2):
                        for c in range(C):
                            ins = pe.matmul(bank[6 + h][0:n, 0:half], kvT[:, 1, c, b * M + lo:b * M + lo + n],
                                            wih[:, c, h * half:(h + 1) * half], start=(c == 0), stop=(c == C - 1))
                    ins.then_inc(c_vw, 1)

        def slot_iterations_tensor(pe):
            pe.wait_ge(c_kq_copied, C)
            pe.wait_ge(c_vw_copied, 4)

            def square_sums(turn, q):
                pe.wait_ge(sq_ready, turn * G + q + 1)
                for t in range(GT):
                    for c in range(C):
                        ins = pe.matmul(bank[0][:, q * GT + t:q * GT + t + 1], sq[:, q % 2, c, t * P:(t + 1) * P],
                                        ones[:, 0:1], start=(c == 0), stop=(c == C - 1))
                    if t == GT - 1:
                        ins.then_inc(ms_ready, 1)
                    yield

            for q in range(G - 1):
                for _ in square_sums(0, q):
                    pass
            with pe.Fori(0, ITERS) as it:
                def spread_group(q, j):
                    pe.wait_ge(diag_ready, it * G + j + 1)
                    if j >= 1:
                        pe.wait_ge(spread_copied, it * 8 + j)
                    pe.matmul(bank[1][:], ones[:], diag[:, q % 2], start=True, stop=True).then_inc(spread_ready, 1)

                for q in range(G):
                    if q == 0:
                        pe.wait_ge(h_ready, it * 8 + 2)
                    elif q == 1:
                        pe.wait_ge(h_ready, it * 8 + 8)
                    elif q == 2:
                        for _ in square_sums(it, G - 1):
                            pass
                    if q == 3:
                        for k in range(G):
                            spread_group(k, k)
                    main, rem = (bank[2 + 2 * (q % 3)], bank[3 + 2 * (q % 3)])
                    if q == 3:
                        pe.wait_ge(scores_scaled, it * 8 + 2)
                    b = q // GB
                    for dst, lo, n in ((main, 0, P), (rem, P, MR)):
                        for c in range(C):
                            ins = pe.matmul(dst[0:n, :], kqT[:, c, b * M + lo:b * M + lo + n],
                                            hT[:, c, q * GN:(q + 1) * GN], start=(c == 0), stop=(c == C - 1))
                    ins.then_inc(scores_ready, 1)

                def gate_block(k, cols, w, rhs, start, stop, between):
                    ins = None
                    for n, (lhs, r) in enumerate(zip(w, rhs)):
                        next(between, None)
                        ins = pe.matmul(bank[dict(hn=4, r=5, z=6, xn=7)[k]][:], lhs[:, cols], r,
                                        start=(start and n == 0), stop=(stop and n == len(w) - 1))
                    return ins

                def recurrent_part(q, o, between=iter(()), blocks=("hn", "r", "z")):
                    j = 2 * q + o
                    h = [hT[:, c, q * GN:(q + 1) * GN] for c in range(C)]
                    if j == 0:
                        pe.wait_ge(scores_scaled, it * 8 + 6)
                    for k in blocks:
                        gate = dict(hn=2, r=0, z=1)[k]
                        if j >= 1:
                            pe.wait_ge(gate_read[k], it * 8 + j)
                        cols = slice(gate * D + o * P, gate * D + (o + 1) * P)
                        ins = gate_block(k, cols, [whh[:, c] for c in range(C)], h, True, k == "hn", between)
                        if k == "hn":
                            ins.then_inc(gate_done["hn"], 1)

                def input_part(q, o, between=iter(())):
                    j, b = 2 * q + o, q // GB
                    n0 = (q % GB) * GN
                    e = [e_main[:, b, n0:n0 + GN], e_rem[0:MR, b, n0:n0 + GN]]
                    pe.wait_ge(attn_ready, it * G + q + 1)
                    if o == 0 and q % GB == 0:
                        pe.wait_ge(vws_ready, it * B + b + 1)
                    for k, gate in (("r", 0), ("z", 1), ("xn", 2)):
                        if k == "xn" and j >= 1:
                            pe.wait_ge(gate_read["xn"], it * 8 + j)
                        cols = slice(gate * D + o * P, gate * D + (o + 1) * P)
                        gate_block(k, cols, [vWs[:, b], vWsr[0:MR, b]], e, k == "xn", True, between).then_inc(gate_done[k], 1)

                def row_sums(q):
                    j, b = 4 + q, q // GB
                    n0 = (q % GB) * GN
                    pe.wait_ge(sinv_spread, it * B + b + 1)
                    pe.wait_ge(spread_copied, it * 8 + max(4, j - 1))
                    dst = bank[(q + 1) % 2][:]
                    pe.matmul(dst, sinv_rep[:, 0, b], e_main[:, b, n0:n0 + GN], start=True, stop=False)
                    pe.matmul(dst, sinv_rep[0:MR, 1, b], e_rem[0:MR, b, n0:n0 + GN], start=False,
                              stop=True).then_inc(spread_ready, 1)

                recurrent_part(0, 0)
                row_sums(0)
                row_sums(1)
                row_sums(2)
                recurrent_part(0, 1, blocks=("hn",))
                input_part(0, 0)
                recurrent_part(0, 1, blocks=("r", "z"))
                row_sums(3)
                input_part(0, 1)
                for q in range(1, G):
                    recurrent_part(q, 0)
                    input_part(q, 0)
                    sums = square_sums(it + 1, q - 1)
                    recurrent_part(q, 1, sums)
                    input_part(q, 1, sums)

        def finish_slots_tensor(pe):
            for q in range(G):
                pe.wait_ge(h_ready, 8 * ITERS + (2 * q + 2 if q < 2 else 8))
                for half in range(2):
                    k = 2 * q + half
                    for t in range(2):
                        for c in range(C):
                            n0 = q * GN + (half * 2 + t) * P
                            ins = pe.transpose(bank[k][:, t * D + c * P:t * D + (c + 1) * P],
                                               hT[:, c, n0:n0 + P], ident[:])
                    ins.then_inc(slotsT_ready, 1)

        def ternary_tensor(pe):
            pe.wait_ge(consts_made, 3)
            pe.wait_ge(tern_ready, 4)
            for g in range(G):
                u = g % 2
                pe.wait_ge(xq_ready, g + 1)
                if g == 0:
                    pe.wait_ge(*x_done.at(0, 1))
                for c in range(C):
                    if g >= 1:
                        pe.wait_ge(*xnT_ready.at(1, (g - 1) * C + c + 1))
                    for t in range(GT):
                        ins = pe.transpose(bank[c].bitcast(BF16)[:, t * P:(t + 1) * P],
                                           xq[:, u, t * D + c * P:t * D + (c + 1) * P], ident_bf[:])
                    ins.then_inc(turned.sem, 1)
                pe.wait_ge(*xnT_ready.at(1, (g + 1) * C))
                if g < 2:
                    pe.wait_ge(*x_done.at(0, G))
                else:
                    pe.wait_ge(*x_done.at(1, g - 1))
                for t in range(GT):
                    for c in range(C):
                        ins = pe.matmul(bank[4 + 2 * u + t // 2][:, (t % 2) * D:(t % 2 + 1) * D],
                                        qT[:, u, c, t * P:(t + 1) * P], tern[:, c], start=(c == 0), stop=(c == C - 1))
                ins.then_inc(project_ready.sem, 1)

        def mha_context_tensor(pe, l):
            s = 2 + 2 * l
            pe.wait_ge(wmha_loaded[l], 5 * 16)
            pe.wait_ge(*x_done.at(1 + l, G))
            for o in range(C):
                for c in range(C):
                    ins = pe.matmul(bank[2 + o][:, 0:BM], wmha[:, l, 1, c, o * P:(o + 1) * P], ctxT[:, c],
                                    start=(c == 0), stop=(c == C - 1))
                ins.then_inc(context_done.sem, 1)
            pe.wait_ge(ctxR_made, 4 + C * B)
            for b in range(B):
                for c in range(C):
                    ins = pe.matmul(bank[4 + b][:, 0:D], ctxT[:, c, b * M:b * M + P], wmha[:, l, 2, c],
                                    start=(c == 0), stop=(c == C - 1))
                ins.then_inc(context_done.sem, 1)
            for b in range(B):
                for c in range(C):
                    ins = pe.matmul(bank[6 + b][:, 0:D], ctxR[:, c, b], wmha[:, l, 2, c],
                                    start=(c == 0), stop=(c == C - 1))
                ins.then_inc(context_done.sem, 1)
            pe.wait_ge(*keys_ready.at(l, 1))
            pe.wait_ge(*bv_ready.at(l, C))
            for c in range(C):
                ins = pe.matmul(bank[2][:, 0:D], bvrow[:, c], wmha[:, l, 3, c], start=(c == 0), stop=(c == C - 1))
            ins.then_inc(context_done.sem, 1)

        def fill_ring(pe, s, op):
            r = ring[op]
            if r >= 2:
                pe.wait_ge(*ring_read[r % 2].at(s, r // 2))
            return bank[2 + r % 2]

        def mha_tensor(pe, l):
            s = 2 + 2 * l

            def turn(g):
                pe.wait_ge(*xn_ready.at(s, g + 1))
                for c in range(C):
                    dst = fill_ring(pe, s, ("turn", g, c))
                    for t in range(GT):
                        ins = pe.transpose(dst[:, t * P:(t + 1) * P], xn[:, g, t, c * P:(c + 1) * P], ident[:])
                    ins.then_inc(ring_filled.sem, 1)

            def query(g):
                for c in range(C):
                    r = ring["turn", g, c]
                    pe.wait_ge(*ring_read[r % 2].at(s, r // 2 + 1))
                for o in range(C):
                    dst = fill_ring(pe, s, ("query", g, o))
                    for c in range(C):
                        ins = pe.matmul(dst, wmha[:, l, 0, c, o * P:(o + 1) * P], xnT[:, g % 2, c],
                                        start=(c == 0), stop=(c == C - 1))
                    ins.then_inc(ring_filled.sem, 1)

            def score(n, k):
                g, t, b = n // GT, n % GT, n // (GT * GB)
                if t == 0 and k == 0:
                    for o in range(C):
                        r = ring["query", g, o]
                        pe.wait_ge(*ring_read[r % 2].at(s, r // 2 + 1))
                K = 4 * n + k
                if K >= 2:
                    pe.wait_ge(*pair_exp.at(s, K - 1))
                for j in range(2 * (k % 2), 2 * (k % 2) + 2):
                    rows = slice(32 * j, 32 * j + 32)
                    ins = pe.matmul(bank[4 + j][:, 0:2 * M], qhT[rows, g % 2, k // 2, t * P:(t + 1) * P],
                                    keys[rows, k // 2, b].rearrange("p h m -> p (h m)"), start=True, stop=True,
                                    tile_position=(32 * j, 0))
                ins.then_inc(pair_scored.sem, 1)

            def weights(n, k):
                u = n % 2
                if k in (0, 2, 4):
                    pe.wait_ge(*half_scaled.at(s, 2 * n + (1 if k == 0 else 2)))
                dst = fill_ring(pe, s, ("weights", n, k))
                for j in range(4):
                    src = probs[:, u, 4 * k + j, 0:P] if k < 4 else probsR[:, u, 4 * j:4 * j + 4].rearrange("p h m -> p (h m)")
                    ins = pe.transpose(dst[:, j * P:(j + 1) * P], src, ident[:])
                ins.then_inc(ring_filled.sem, 1)

            def values(n, c):
                g, t, b, u = n // GT, n % GT, n // (GT * GB), n % 2
                if t == 0 and g >= 1:
                    pe.wait_ge(*(x_done if c else half_added).at(s, g))
                if c == 0:
                    for k in (3, 4):
                        r = ring["weights", n, k]
                        pe.wait_ge(*ring_read[r % 2].at(s, r // 2 + 1))
                for h in range(8 * c, 8 * c + 8):
                    pe.matmul(bank[c][:, t * P:(t + 1) * P], vals[:, (b * H + h) * P:(b * H + h + 1) * P], probsT[:, u, h],
                              start=(h == 8 * c), stop=False)
                for q in range(2 * c, 2 * c + 2):
                    ins = pe.matmul(bank[c][:, t * P:(t + 1) * P], valsR[:, (b * 4 + q) * P:(b * 4 + q + 1) * P],
                                    probsT[:, u, 16 + q], start=False, stop=(q == 2 * c + 1))
                ins.then_inc(pv_done.sem, 1)

            def project(g):
                for c in range(C):
                    pe.wait_ge(*headsT_ready[c].at(s, g + 1))
                for t in range(GT):
                    for c in range(C):
                        ins = pe.matmul(bank[t // 2][:, (t % 2) * D:(t % 2 + 1) * D],
                                        headsT[:, g % 2, c, t * P:(t + 1) * P], wmha[:, l, 3, c],
                                        start=(c == 0), stop=(c == C - 1))
                    if t % 2:
                        ins.then_inc(half_projected.sem, 1)

            pe.wait_ge(*vals_ready.at(l, B))
            pe.wait_ge(*cvec_ready.at(l, 1))
            for n, ops in head_steps():
                for op in ops:
                    dict(turn=turn, query=query, score=score, weights=weights, values=values, project=project)[op[0]](*op[1:])

        def tri_fold_tensor(pe):
            pe.wait_ge(w3_loaded, 3 * 16)
            pe.wait_ge(*x_done.at(2, G))
            if last_stage >= 4:
                pe.wait_ge(*cvec_ready.at(1, 1))
            for k in range(2):
                if k:
                    pe.wait_ge(tri_copied, C)
                for o in range(C):
                    for c in range(C):
                        ins = pe.matmul(bank[2 + o][:, 0:D], wtri[:, 1 - k, c, o * P:(o + 1) * P],
                                        wtri[:, 2, c] if k == 0 else wtri12[:, 0, c], start=(c == 0), stop=(c == C - 1))
                    ins.then_inc(tri_folded, 1)
            pe.wait_ge(tri_copied, 2 * C)

        def tri_tensor(pe):
            for g in range(G):
                u = g % 2
                turn_group(pe, 3, g)
                pe.wait_ge(*xnT_ready.at(3, (g + 1) * C))
                if g >= 2:
                    pe.wait_ge(tri_summed, g - 1)
                for t in range(GT):
                    for c in range(C):
                        ins = pe.matmul(bank[4 + 2 * u + t // 2][:, (t % 2) * D:(t % 2 + 1) * D],
                                        xnT[:, u, c, t * P:(t + 1) * P], wtri12[:, 1, c], start=(c == 0), stop=(c == C - 1))
                ins.then_inc(project_ready.sem, 1)


        def context_slots_scalar(act):
            for k in range(4):
                act.wait_ge(c_kv, k + 1)
                act.activation(kvT[:, k // 2, k % 2], bank[1 + k][:, 0:BM], ACT.Copy).then_inc(c_kv_copied, 1)
            for o in range(C):
                act.wait_ge(c_kq, o + 1)
                act.activation(kqT[:, o], bank[1 + o][:, 0:BM], ACT.Copy, scale=vec0[:, SLOTW, o:o + 1]).then_inc(c_kq_copied, 1)
            half = 3 * D // 2
            for b in range(B):
                for k, (dst, n) in enumerate(((vW, P), (vWr, MR))):
                    act.wait_ge(c_vw, b * 2 + k + 1)
                    act.activation(dst[0:n, b, 0:half], bank[6][0:n, 0:half], ACT.Copy)
                    act.activation(dst[0:n, b, half:], bank[7][0:n, 0:half], ACT.Copy).then_inc(c_vw_copied, 1)

        def slot_iterations_scalar(act):
            act.wait_ge(c_rms, 2)
            with act.Fori(0, ITERS) as it:
                def copy_spread(q):
                    act.wait_ge(spread_ready, it * 8 + q + 1)
                    act.activation(spread[:, q], bank[1][:], ACT.Copy).then_inc(spread_copied, 1)

                def exponentials(b):
                    act.wait_ge(max_ready, it * B + b + 1)
                    act.activation(e_main[:, b], e_main[:, b], ACT.Exp, bias=mneg[:, 0, b:b + 1], scale=D ** -0.5,
                                   accum_out=ssum[:, 0, b:b + 1]).then_inc(exp_ready, 1)
                    act.activation(e_rem[0:MR, b], e_rem[0:MR, b], ACT.Exp, bias=mneg[0:MR, 1, b:b + 1], scale=D ** -0.5,
                                   accum_out=ssum[0:MR, 1, b:b + 1]).then_inc(exp_ready, 1)

                def gates(q, o):
                    j = 2 * q + o
                    for k, dst, bias, fn in (("hn", gate_u, 5, ACT.Identity), ("r", gate_r, 0, ACT.Tanh),
                                             ("z", gate_z, 1, ACT.Tanh)):
                        act.wait_ge(gate_done[k], it * 8 + j + 1)
                        if k == "hn" and j >= 2:
                            act.wait_ge(h_ready, 8 + it * 8 + j - 1)
                        act.activation(dst[:, o], bank[dict(hn=4, r=5, z=6)[k]][:], fn, bias=bsum[:, bias, o:o + 1],
                                       scale=0.5).then_inc(gate_read[k], 1)

                def candidate(q, o):
                    j = 2 * q + o
                    act.wait_ge(gate_read["xn"], it * 8 + j + 1)
                    act.activation(cand[:, o], cand[:, o], ACT.Tanh, bias=vec0[:, BIH + 2, o:o + 1]).then_inc(cand_ready, 1)

                for q in range(G):
                    copy_spread(q)
                exponentials(0)
                exponentials(1)
                gates(0, 0)
                gates(0, 1)
                candidate(0, 0)
                candidate(0, 1)
                for q in range(1, G):
                    gates(q, 0)
                    gates(q, 1)
                    candidate(q, 0)
                    candidate(q, 1)

        def ternary_scalar(act):
            for g in range(G):
                if g >= 2:
                    act.wait_ge(*project_ready.at(1, g - 1))
                for c in range(C):
                    act.wait_ge(*turned.at(1, g * C + c + 1))
                    act.activation(qT[:, g % 2, c, 0:GN], bank[c].bitcast(BF16)[:, 0:GN], ACT.Copy).then_inc(xnT_ready.sem, 1)

        def empty_ring(eng, l, op, copy):
            s = 2 + 2 * l
            r = ring[op]
            if (eng is nc.scalar) != (r % 2 == 0):
                return
            src = bank[2 + r % 2]
            eng.wait_ge(*ring_filled.at(s, r + 1))
            if op[0] == "turn":
                g, c = op[1:]
                copy(xnT[:, g % 2, c], src, None).then_inc(ring_read[r % 2].sem, 1)
            elif op[0] == "query":
                g, o = op[1:]
                copy(qhT[:, g % 2, o], src, vmha[:, l, 0, o:o + 1]).then_inc(ring_read[r % 2].sem, 1)
            else:
                n, k = op[1:]
                if k < 2 and n >= 2:
                    eng.wait_ge(*pv_done.at(s, 2 * (n - 1)))
                copy(probsT[:, n % 2, 4 * k:4 * k + 4].rearrange("p h m -> p (h m)"), src, None).then_inc(ring_read[r % 2].sem, 1)

        def mha_scalar(act, l):
            s = 2 + 2 * l

            def copy(dst, src, bias):
                if bias is None:
                    return act.activation(dst, src, ACT.Copy)
                return act.activation(dst, src, ACT.Identity, bias=bias)

            def score(n, k):
                u = n % 2
                act.wait_ge(*pair_max.at(s, 4 * n + k + 1))
                if k == 0 and n >= 2:
                    r = ring["weights", n - 2, 4]
                    act.wait_ge(*ring_filled.at(s, r + 1))
                for j in range(4):
                    h = 4 * k + j
                    ins = act.activation(probs[:, u, h, 0:M], bank[4 + 2 * (k % 2) + j // 2][:, (j % 2) * M:(j % 2 + 1) * M],
                                         ACT.Exp, bias=nmax[:, u, h:h + 1], scale=HD ** -0.5, accum_out=hsum[:, u, h:h + 1])
                ins.then_inc(pair_exp.sem, 1)

            act.wait_ge(wmha_loaded[l], 5 * 16)
            act.wait_ge(ctxR_made, 4)
            if l:
                act.wait_ge(*x_done.at(s - 1, G))
            for n, ops in head_steps():
                for op in ops:
                    if op[0] == "score":
                        score(*op[1:])
                    elif op[0] == "weights":
                        empty_ring(act, l, op, copy)
                    elif op[0] in ("turn", "query"):
                        for c in range(C):
                            empty_ring(act, l, op + (c,), copy)
                    elif op[0] == "project":
                        act.wait_ge(*pv_done.at(s, 2 * GT * (op[1] + 1)))
                        act.activation(headsT[:, op[1] % 2, 0], bank[0], ACT.Copy).then_inc(headsT_ready[0].sem, 1)

        def tri_scalar(act):
            for k in range(2):
                for o in range(C):
                    act.wait_ge(tri_folded, k * C + o + 1)
                    act.activation(wtri12[:, k, o], bank[2 + o][:, 0:D], ACT.Copy).then_inc(tri_copied, 1)
            for g in range(G + 1):
                if g < G:
                    if g >= 2:
                        act.wait_ge(*project_ready.at(3, g - 1))
                    copy_turned(act, 3, g, xnT[:, g % 2])
                if g >= 1:
                    act.wait_ge(tri_summed, g)
                    r = tri_out[:, (g - 1) % 2]
                    act.activation(r, r, ACT.Tanh).then_inc(tri_tanh, 1)


        def context_slots_vector(dve):
            dve.wait_ge(w0_loaded, 6 * 16)
            ch = Chain(dve, sem("ctx_steps"))
            ch.step(dve.tensor_tensor(bsum[:, 0:2], vec0[:, BIH:BIH + 2], vec0[:, BHH:BHH + 2], ALU.add))
            ch.settle()
            dve.tensor_scalar(bsum[:, 0:2], bsum[:, 0:2], 0.5, None, ALU.mult).then_inc(c_rms, 1)
            dve.tensor_scalar(bsum[:, 5], vec0[:, BHH + 2], 0.5, None, ALU.mult).then_inc(c_rms, 1)
            dve.wait_ge(c_ms, 1)
            v, y, t_ = (spread[:, k, 0:BM] for k in range(3))
            ch.step(dve.tensor_scalar(v, bank[0][:, 0:BM], 1.0 / D, RMS_EPS, ALU.mult, ALU.add))
            ch.settle()
            for _ in rsqrt_newton(ch, v, y, t_):
                pass
            for c in range(C):
                dve.scalar_tensor_tensor(PnT[:, c], ctxT[:, c], vec0[:, INW, c:c + 1], y, ALU.mult,
                                         ALU.mult).then_inc(c_pn, 1)

        SLOT_STEPS = 2 + 3 * NEWTON + 2 * 2 + 2 * 1 + 4 * 1 + 8 * 3
        def slot_iterations_vector(dve):
            steps = sem("slot_steps")
            with dve.Fori(0, ITERS) as it:
                ch = Chain(dve, steps, SLOT_STEPS, it)

                def diagonal(q, col, j):
                    if j >= 2:
                        dve.wait_ge(spread_ready, it * 8 + j - 1)
                    dve.tensor_tensor(diag[:, q % 2].rearrange("p (t n) -> p t n", t=GT),
                                      ident[:].unsqueeze(1).broadcast_to([P, GT, P]),
                                      col.unsqueeze(2).broadcast_to([P, GT, P]), ALU.mult).then_inc(diag_ready, 1)

                dve.wait_ge(ms_ready, it * G + G)
                v, t_ = nwt[:, 0, 0], nwt[:, 0, 2]
                ch.step(dve.tensor_scalar(v, bank[0][:, 0:T], 1.0 / D, RMS_EPS, ALU.mult, ALU.add))
                ch.settle()
                for _ in rsqrt_newton(ch, v, rms16, t_):
                    pass
                for q in range(G):
                    diagonal(q, rms16[:, q * GT:(q + 1) * GT], q)

                def scale_scores(q):
                    b, n0 = q // GB, (q % GB) * GN
                    main, rem = (bank[2 + 2 * (q % 3)], bank[3 + 2 * (q % 3)])
                    dve.wait_ge(scores_ready, it * G + q + 1)
                    dve.wait_ge(spread_copied, it * 8 + q + 1)
                    take_wait(dve)
                    for k, (src, dst, n) in enumerate(((main, e_main, P), (rem, e_rem, MR))):
                        dve.tensor_tensor_reduce(dst[0:n, b, n0:n0 + GN], src[0:n, :], spread[0:n, q], 1.0, -3.0e38,
                                                 ALU.mult, ALU.max, mx[0:n, k, b, q % GB:q % GB + 1]).then_inc(scores_scaled, 1)

                def negated_max(b):
                    dve.wait_ge(scores_scaled, it * 8 + 4 * b + 4)
                    for k, n in enumerate((P, MR)):
                        ch.step(dve.tensor_reduce(mneg[0:n, k, b:b + 1], mx[0:n, k, b], AX.X, ALU.max, negate=True))
                    ch.settle()
                    dve.tensor_scalar(mneg[:, 0, b:b + 1], mneg[:, 0, b:b + 1], D ** -0.5, None, ALU.mult)
                    dve.tensor_scalar(mneg[0:MR, 1, b:b + 1], mneg[0:MR, 1, b:b + 1], D ** -0.5, None,
                                      ALU.mult).then_inc(max_ready, 1)

                def inverse_sums(b):
                    dve.wait_ge(exp_ready, it * 4 + 2 * b + 2)
                    ch.step(dve.reciprocal(sinv[:, 0, b:b + 1], ssum[:, 0, b:b + 1]))
                    dve.reciprocal(sinv[0:MR, 1, b:b + 1], ssum[0:MR, 1, b:b + 1]).then_inc(sinv_ready, 1)
                    ch.settle()
                    dve.wait_ge(sinv_ready, it * B + b + 1)
                    dve.tensor_scalar(sinv_rep[:, 0, b], ones[:], sinv[:, 0, b:b + 1], None, ALU.mult)
                    dve.tensor_scalar(sinv_rep[0:MR, 1, b], ones[0:MR], sinv[0:MR, 1, b:b + 1], None,
                                      ALU.mult).then_inc(sinv_spread, 1)

                def attention(q):
                    b, n0 = q // GB, (q % GB) * GN
                    dve.wait_ge(spread_ready, it * 8 + 4 + q + 1)
                    dve.tensor_scalar(spread[:, q], bank[(q + 1) % 2], RMS_EPS, None, ALU.add).then_inc(spread_copied, 1)
                    dve.wait_ge(spread_copied, it * 8 + 4 + q + 1)
                    ch.step(dve.reciprocal(spread[:, q], spread[:, q]))
                    ch.settle()
                    dve.tensor_tensor(e_main[:, b, n0:n0 + GN], e_main[:, b, n0:n0 + GN], spread[:, q], ALU.mult)
                    dve.tensor_tensor(e_rem[0:MR, b, n0:n0 + GN], e_rem[0:MR, b, n0:n0 + GN], spread[0:MR, q],
                                      ALU.mult).then_inc(attn_ready, 1)

                def argument(q, o):
                    j = 2 * q + o
                    dve.wait_ge(gate_read["r"], it * 8 + j + 1)
                    ch.step(dve.scalar_tensor_tensor(gate_u[:, o], gate_r[:, o], 1.0, gate_u[:, o], ALU.add, ALU.mult))
                    ch.settle()
                    dve.wait_ge(gate_done["xn"], it * 8 + j + 1)
                    dve.tensor_tensor(cand[:, o], bank[7][:], gate_u[:, o], ALU.add).then_inc(gate_read["xn"], 1)

                def new_slots(q, o):
                    j = 2 * q + o
                    h = hT[:, o, q * GN:(q + 1) * GN]
                    dve.wait_ge(cand_ready, it * 8 + j + 1)
                    dve.wait_ge(gate_read["z"], it * 8 + j + 1)
                    dve.wait_ge(gate_done["xn"], it * 8 + 2 * q + 2)
                    ch.step(dve.tensor_tensor(gate_r[:, o], h, cand[:, o], ALU.subtract))
                    ch.settle()
                    ch.step(dve.scalar_tensor_tensor(gate_r[:, o], gate_z[:, o], 1.0, gate_r[:, o], ALU.add, ALU.mult))
                    ch.settle()
                    dve.scalar_tensor_tensor(h, gate_r[:, o], 0.5, cand[:, o], ALU.mult, ALU.add).then_inc(h_ready, 1)

                scale_scores(0)
                scale_scores(1)
                negated_max(0)
                scale_scores(2)
                scale_scores(3)
                negated_max(1)
                inverse_sums(0)
                inverse_sums(1)
                attention(0)
                attention(1)
                attention(2)
                argument(0, 0)
                attention(3)
                argument(0, 1)
                new_slots(0, 0)
                new_slots(0, 1)
                for q in range(1, G):
                    argument(q, 0)
                    argument(q, 1)
                    new_slots(q, 0)
                    new_slots(q, 1)
                ch.close()

        def unpack_ternary_vector(dve):
            dve.wait_ge(w1_loaded, 2 * 16)
            for k in range(4):
                if k:
                    dve.wait_ge(tern_ready, k)
                dve.tensor_scalar(unpacked[:], packed[:], 2 * k, 3, ALU.arith_shift_right,
                                  ALU.bitwise_and).then_inc(unpacked_ready, 1)
                dve.wait_ge(unpacked_ready, k + 1)
                dve.tensor_scalar(tern[:, :, k * 64:(k + 1) * 64], unpacked[:], -1.0, None, ALU.add).then_inc(tern_ready, 1)

        def quantise(dve, ch, g):
            top, scale, back = (amax[:, g, k] for k in range(3))
            dve.wait_ge(*xn_ready.at(1, g + 1))
            ch.step(dve.tensor_reduce(top, xn[:, g], AX.X, ALU.max, apply_absolute_value=True))
            k = ch.n
            yield
            ch.settle(k)
            ch.step(dve.tensor_scalar(top, top, 1e-5, None, ALU.max))
            k = ch.n
            yield
            ch.settle(k)
            ch.step(dve.reciprocal(scale, top))
            k = ch.n
            yield
            ch.settle(k)
            ch.step(dve.tensor_scalar(scale, scale, 127.0, None, ALU.mult))
            ch.step(dve.tensor_scalar(back, top, wscale[:], 1.0 / 127.0, ALU.mult, ALU.mult))
            k = ch.n
            yield
            ch.settle(k)
            ch.step(dve.tensor_scalar(back, back, gain(1), None, ALU.mult))
            for t in range(GT):
                ch.step(dve.tensor_scalar(xn[:, g, t], xn[:, g, t], scale[:, t:t + 1], ROUND, ALU.mult, ALU.add))
            k = ch.n
            yield
            ch.settle(k)
            flat = xn[:, g].rearrange("p t d -> p (t d)")
            ch.step(dve.tensor_scalar(flat, flat, -ROUND, 127.0, ALU.add, ALU.min))
            k = ch.n
            yield
            ch.settle(k)
            if g >= 2:
                dve.wait_ge(*turned.at(1, (g - 1) * C))
            dve.tensor_scalar(xq[:, g % 2], flat, -128.0, None, ALU.max).then_inc(xq_ready, 1)

        def finish_slots_vector(dve, ch):
            dve.wait_ge(gains_ready, 1)

            def finish(g):
                for k in (2 * g, 2 * g + 1):
                    dve.wait_ge(slotsT_ready, k + 1)
                    xs = x_tok[:, 2 * k:2 * k + 2].rearrange("p t d -> p (t d)")
                    ins = dve.scalar_tensor_tensor(xs, bank[k], gain(0), xs, ALU.mult, ALU.add)
                    if k % 2:
                        ins.then_inc(x_done.of(0), 1)
                    else:
                        ch.step(ins)
                    yield
                yield from next_norm_parts(dve, ch, 0, g)
                if last_stage >= 1:
                    yield from quantise(dve, ch, g)

            for g in range(0, G, 2):
                together(finish(g), finish(g + 1))

        def next_norm_parts(dve, ch, s, g):
            if s < last_stage:
                dve.wait_ge(*x_done.at(s, g + 1))
                yield from layer_norm_parts(dve, ch, s + 1, g)

        def ternary_vector(dve, ch):
            def finish(g):
                dve.wait_ge(*project_ready.at(1, g + 1))
                dve.wait_ge(*row_added.at(1, g + 1))
                for t in range(GT):
                    xs = x_tok[:, g * GT + t]
                    ins = dve.scalar_tensor_tensor(xs, bank[4 + 2 * (g % 2) + t // 2][:, (t % 2) * D:(t % 2 + 1) * D],
                                                   amax[:, g, 2, t:t + 1], xs, ALU.mult, ALU.add)
                    if t == GT - 1:
                        ins.then_inc(x_done.of(1), 1)
                    yield
                yield from next_norm_parts(dve, ch, 1, g)

            for g in range(0, G, 2):
                together(finish(g), finish(g + 1))

        def mha_context_vector(dve, ch, l):
            s = 2 + 2 * l
            if l == 0:
                dve.wait_ge(masks_made, 1)
                ch.step(dve.tensor_scalar(pidx[:, 1:2], pidx[:, 0:1], 16, None, ALU.bitwise_and))
                ch.settle()
                for k in range(2):
                    ch.step(dve.tensor_scalar(mask16[:, k:k + 1], pidx[:, 1:2], 16.0 * k, None, ALU.is_equal))
                ch.settle()
                ch.step(dve.tensor_scalar(pidx[:, 1:2], pidx[:, 0:1], 5, None, ALU.arith_shift_right))
                ch.settle()
                for k in range(4):
                    ch.step(dve.tensor_scalar(mask32[:, k:k + 1], pidx[:, 1:2], 1.0 * k, None, ALU.is_equal))
                ch.settle()
            dve.wait_ge(wmha_loaded[l], 5 * 16)
            if l:
                dve.wait_ge(*context_done.at(0, 7))
            for c in range(C):
                dve.tensor_scalar(bvrow[:, c], ones[:], vmha[:, l, 2, c:c + 1], None, ALU.mult).then_inc(bv_ready.sem, 1)
            for o in range(C):
                dve.wait_ge(*context_done.at(l, o + 1))
                for b in range(B):
                    for h in range(2):
                        ins = dve.tensor_scalar(keys[:, o, b, h], bank[2 + o][:, b * M:(b + 1) * M], vmha[:, l, 1, o:o + 1],
                                                mask16[:, h:h + 1], ALU.add, ALU.mult)
                ins.then_inc(keys_ready.sem, 1)
            dve.wait_ge(ctxR_made, 4)
            for b in range(B):
                dve.wait_ge(*context_done.at(l, 3 + b))
                for c in range(C):
                    at = (b * C + c) * 8 * P
                    ch.step(dve.tensor_copy(vals[:, at:at + 8 * (P + HD)].rearrange("p (j n) -> p j n", j=8)[:, :, 0:HD],
                                            bank[4 + b][:, c * P:(c + 1) * P].rearrange("p (j n) -> p j n", j=8)))
                dve.wait_ge(*context_done.at(l, 5 + b))
                for h in range(4):
                    for c in range(C):
                        at = (b * C + c) * 2 * P
                        ins = dve.tensor_scalar(
                            valsR[:, at:at + 2 * (P + 64)].rearrange("p (q n) -> p q n", q=2)[:, :, h * HD:(h + 1) * HD],
                            bank[6 + b][:, c * P:(c + 1) * P].rearrange("p (q n) -> p q n", q=2)[:, :, h * HD:(h + 1) * HD],
                            mask32[:, h:h + 1], None, ALU.mult)
                        if h < 3 or c == 0:
                            ch.step(ins)
                ins.then_inc(vals_ready.sem, 1)
            dve.wait_ge(*context_done.at(l, 7))
            dve.wait_ge(rows_loaded, 5 * 16)
            row = add_row[:, 1 + l]
            ch.step(dve.tensor_tensor(row, bank[2][:, 0:D], row, ALU.add))
            ch.settle()
            dve.tensor_scalar(row, row, gain(s), None, ALU.mult).then_inc(cvec_ready.sem, 1)

        def mha_vector(dve, ch, l):
            s = 2 + 2 * l

            def copy(dst, src, bias):
                if bias is None:
                    return dve.tensor_copy(dst, src)
                return dve.tensor_scalar(dst, src, bias, None, ALU.add)

            def score(n, k):
                u = n % 2
                dve.wait_ge(*pair_scored.at(s, 4 * n + k + 1))
                m = smax[:, u, 4 * k:4 * k + 4]
                ch.step(dve.tensor_reduce(m.rearrange("p (b h) -> p b h", b=2),
                                          psum[:, 4 + 2 * (k % 2):6 + 2 * (k % 2), 0:2 * M].rearrange("p b (h m) -> p b h m", h=2),
                                          AX.X, ALU.max))
                ch.settle()
                dve.tensor_scalar(nmax[:, u, 4 * k:4 * k + 4], m, -HD ** -0.5, None, ALU.mult).then_inc(pair_max.sem, 1)

            def inverse_sums(n, half):
                dve.wait_ge(*pair_exp.at(s, 4 * n + 2 * half + 2))
                dve.reciprocal(rsum[:, n % 2, 8 * half:8 * half + 8], hsum[:, n % 2, 8 * half:8 * half + 8]).then_inc(half_sums.sem, 1)

            def finish(g):
                dve.wait_ge(*row_added.at(s, g + 1))
                for half in range(2):
                    dve.wait_ge(*half_projected.at(s, 2 * g + half + 1))
                    t0 = g * GT + 2 * half
                    xs = x_tok[:, t0:t0 + 2].rearrange("p t d -> p (t d)")
                    dve.scalar_tensor_tensor(xs, bank[half], gain(s), xs, ALU.mult,
                                             ALU.add).then_inc(x_done.of(s) if half else half_added.sem, 1)

            norm = iter(())
            for n, ops in head_steps():
                for op in ops:
                    next(norm, None)
                    next(norm, None)
                    if op[0] == "score":
                        score(*op[1:])
                        if op[2] == 2:
                            inverse_sums(op[1], 0)
                    elif op[0] == "weights":
                        empty_ring(dve, l, op, copy)
                    elif op[0] in ("turn", "query"):
                        for c in range(C):
                            empty_ring(dve, l, op + (c,), copy)
                    elif op[0] == "project":
                        g = op[1]
                        dve.wait_ge(*pv_done.at(s, 2 * GT * (g + 1)))
                        dve.tensor_copy(headsT[:, g % 2, 1], bank[1]).then_inc(headsT_ready[1].sem, 1)
                if n + 1 < T:
                    inverse_sums(n + 1, 1)
                for op in ops:
                    if op[0] == "project":
                        for _ in norm:
                            pass
                        finish(op[1])
                        norm = next_norm_parts(dve, ch, s, op[1])
            for _ in norm:
                pass

        def tri_vector(dve, ch):
            def finish(g):
                dve.wait_ge(tri_tanh, g + 1)
                xs = x_tok[:, g * GT:(g + 1) * GT].rearrange("p t d -> p (t d)")
                dve.scalar_tensor_tensor(xs, tri_out[:, g % 2], gain(3), xs, ALU.mult, ALU.add).then_inc(x_done.of(3), 1)
                yield
                yield from next_norm_parts(dve, ch, 3, g)

            for g in range(G):
                u = g % 2
                dve.wait_ge(*project_ready.at(3, g + 1))
                dve.tensor_tensor(tri_out[:, u].rearrange("p (t d) -> p t d", d=D),
                                  psum[:, 4 + 2 * u:6 + 2 * u].rearrange("p b (t d) -> p (b t) d", d=D),
                                  add_row[:, 4].unsqueeze(1).broadcast_to([P, GT, D]), ALU.add).then_inc(tri_summed, 1)
                if u:
                    together(finish(g - 1), finish(g))

        @block.sync
        def _(sp):
            sp.dma_start(x_tok[:], d["x"].rearrange("(t p) d -> p t d", p=P)).then_inc(x_loaded, 16)
            sp.dma_start(ctxT[:], d["ctxT"].rearrange("(c p) n -> p c n", p=P)).then_inc(ctx_loaded, 16)
            sp.dma_start(tanh_g[:], d["gains"].partition_broadcast(P)).then_inc(gains_loaded, 16)
            for k, name in enumerate(("wq0", "wk0", "wv0")):
                sp.dma_start(wqkv0[:, k], weight(d[name])).then_inc(w0_loaded, 16)
            sp.dma_start(wih, weight(d["wih"])).then_inc(w0_loaded, 16)
            sp.dma_start(whh, weight(d["whh"])).then_inc(w0_loaded, 16)
            sp.dma_start(vec0[:, 0:8], d["vec0"].rearrange("p (v c) -> p v c", c=C)).then_inc(w0_loaded, 16)
            sp.dma_start(packed[:], weight(d["packed"])).then_inc(w1_loaded, 16)
            sp.dma_start(wscale[:], d["wscale"].partition_broadcast(P)).then_inc(w1_loaded, 16)
            for k, name in enumerate(("row1", "row2", "row4", "row6", "row3")):
                sp.dma_start(add_row[:, k], d[name].partition_broadcast(P)).then_inc(rows_loaded, 16)
            for k, name in enumerate(("tri_wT", "tri_a1T", "tri_a2")):
                sp.dma_start(wtri[:, k], weight(d[name])).then_inc(w3_loaded, 16)
            if last_stage >= 5:
                sp.wait_ge(route_consts, 1)
                sp.dma_start(xs5.rearrange("(t p) d -> p t d", p=P),
                             zeros[:].unsqueeze(1).broadcast_to([P, NT2, D])).then_inc(zeroed, 16)
                sp.dma_start(xs7.rearrange("(t p) d -> p t d", p=P),
                             zeros[:].unsqueeze(1).broadcast_to([P, NT4, D])).then_inc(zeroed, 16)
            if last_stage >= 2:
                sp.wait_ge(*x_done.at(0, G))
                for l in range(2):
                    for k, name in enumerate(("wq", "wk", "wv", "wo")):
                        sp.dma_start(wmha[:, l, k], weight(d[f"{name}{l + 1}"])).then_inc(wmha_loaded[l], 16)
                    sp.dma_start(vmha[:, l], d[f"vec{l + 1}"].rearrange("p (v c) -> p v c", c=C)).then_inc(wmha_loaded[l], 16)
            if last_stage >= 5:
                sp.wait_ge(*x_done.at(3, G))
                sp.dma_start(b2row, d["b2"].partition_broadcast(P)).then_inc(w5_loaded, 16)
                sp.dma_start(br5, d["br5"].partition_broadcast(P)).then_inc(w5_loaded, 16)
                sp.dma_start(b1col, d["b1"]).then_inc(w5_loaded, 16)
                sp.dma_start(wr5, weight(d["wr5"])).then_inc(w5_loaded, 16)
                sp.wait_ge(*x_done.at(4, G))
                for e in range(E2):
                    sp.dma_start(W1[:, e].rearrange("p (c n) -> p c n", c=C), weight(d["W1"][e * D:(e + 1) * D])).then_inc(expert5_loaded, 16)
                    sp.dma_start(W2[:, e].rearrange("p (k n) -> p k n", n=D), weight(d["W2"][e * F2:(e + 1) * F2])).then_inc(expert5_loaded, 16)
                expert_tiles_sync(sp)
            if last_stage >= 6:
                sp.wait_ge(*out_done.at(5, NT2))
                for k, name in enumerate(("wk6", "wv6", "wq6")):
                    sp.dma_start(w6[:, k], weight(d[name])).then_inc(w6_loaded, 16)
                sp.dma_start(vec6, d["vec6"].rearrange("p (v c) -> p v c", c=C)).then_inc(w6_loaded, 16)
            if last_stage >= 7:
                sp.wait_ge(*x_done.at(5, G))
                sp.dma_start(wr7, weight(d["wr7"])).then_inc(ws_loaded, 16)
                sp.dma_start(br7, d["br7"].partition_broadcast(P)).then_inc(ws_loaded, 16)
                sp.dma_start(sgate, weight(d["sgate"])).then_inc(ws_loaded, 16)
                sp.dma_start(sup, weight(d["sup"])).then_inc(ws_loaded, 16)
                sp.dma_start(sdown, weight(d["sdown"])).then_inc(ws_loaded, 16)
                for k in range(4):
                    sp.dma_start(GU[:, 8 * k:8 * k + 8].rearrange("p e c n -> p (e c) n"),
                                 d["gate_up"][8 * k * D:8 * (k + 1) * D].rearrange("(e p) n -> p e n", p=P)).then_inc(w7_loaded, 16)
                    sp.dma_start(DW[:, 8 * k:8 * k + 8],
                                 d["down"][8 * k * F4:8 * (k + 1) * F4].rearrange("(e p) n -> p e n", p=P)).then_inc(w7_loaded, 16)
                quads_sync(sp)
            for g in range(G):
                sp.wait_ge(*x_done.at(last_stage, g + 1))
                sp.dma_start(out.rearrange("(t p) d -> p t d", p=P)[:, g * GT:(g + 1) * GT],
                             x_tok[:, g * GT:(g + 1) * GT]).then_inc(out_stored, 16)
            sp.wait_ge(out_stored, G * 16)

        @block.gpsimd
        def _(pool):
            pool.memset(ones[:], 1.0).then_inc(consts_made, 1)
            pool.wait_ge(consts_made, 1)
            pool.affine_select(ident[:], ones[:], [[-1, P]], ALU.is_equal, 0.0, base=0,
                               channel_multiplier=1).then_inc(consts_made, 1)
            if last_stage >= 5:
                route_constants_gpsimd(pool)
            pool.wait_ge(ctx_loaded, 16)
            pool.tensor_tensor(sq[:, 0, :, 0:BM], ctxT[:], ctxT[:], ALU.mult).then_inc(c_sq, 1)
            pool.wait_ge(consts_made, 2)
            pool.tensor_copy(ident_bf[:], ident[:]).then_inc(consts_made, 1)
            pool.iota(pidx[:, 0:1], [[0, 1]], base=0, channel_multiplier=1).then_inc(masks_made, 1)
            pool.wait_ge(rows_loaded, 5 * 16)
            pool.wait_ge(gains_ready, 1)
            row = add_row[:, 0]
            pool.tensor_tensor(row, row, gain(1).broadcast_to([P, D]), ALU.mult).then_inc(rows_ready, 1)
            row = add_row[:, 3]
            pool.tensor_tensor(row, row, gain(6).broadcast_to([P, D]), ALU.mult).then_inc(rows_ready, 1)
            pool.wait_ge(c_ms, 1)
            slot_iterations_gpsimd(pool)
            if last_stage >= 2:
                pool.wait_ge(rows_ready, 2)
            add_rows_gpsimd(pool, 1, 0)
            if last_stage >= 2:
                mha_constants_gpsimd(pool)
            if last_stage >= 2:
                pool.wait_ge(*cvec_ready.at(0, 1))
                mha_gpsimd(pool, 0, 1)
            if last_stage >= 4:
                pool.wait_ge(*cvec_ready.at(1, 1))
                mha_gpsimd(pool, 1, 2)
            if last_stage >= 5:
                scatter_gpsimd(pool, 5, xs5)
                gather_gpsimd(pool)
            if last_stage >= 6:
                add_rows_gpsimd(pool, 6, 3)
            if last_stage >= 7:
                scatter_gpsimd(pool, 7, xs7)
                gather7_gpsimd(pool)

        @block.tensor
        def _(pe):
            pe.wait_ge(consts_made, 2)
            start_slots_tensor(pe)
            context_slots_tensor(pe)
            slot_iterations_tensor(pe)
            finish_slots_tensor(pe)
            if last_stage >= 1:
                ternary_tensor(pe)
            if last_stage >= 2:
                mha_context_tensor(pe, 0)
                mha_tensor(pe, 0)
            if last_stage >= 4:
                mha_context_tensor(pe, 1)
            if last_stage >= 3:
                tri_fold_tensor(pe)
                tri_tensor(pe)
            if last_stage >= 4:
                mha_tensor(pe, 1)
            if last_stage >= 5:
                route_tensor(pe, 5, wr5, (w5_loaded, 4 * 16), free=lambda: pe.wait_ge(*x_done.at(4, G)))
                expert_tiles_tensor(pe)
            if last_stage >= 6:
                single_context_tensor(pe)
                single_tensor(pe)
            if last_stage >= 7:
                route_tensor(pe, 7, wr7, (ws_loaded, 5 * 16), free=lambda: pe.wait_ge(*x_done.at(6, G)))
                shared_tensor(pe, range(G - 1))
                quads_tensor(pe)
                pe.wait_ge(*out_ready.at(7, NQ))
                shared_tensor(pe, range(G - 1, G))

        @block.scalar
        def _(act):
            act.wait_ge(gains_loaded, 16)
            act.activation(tanh_g[:], tanh_g[:], ACT.Tanh).then_inc(gains_ready, 1)
            for g in range(G):
                copy_turned(act, 0, g, hT[:, :, g * GN:(g + 1) * GN])
            context_slots_scalar(act)
            slot_iterations_scalar(act)
            if last_stage >= 1:
                ternary_scalar(act)
            if last_stage >= 2:
                mha_scalar(act, 0)
            if last_stage >= 3:
                tri_scalar(act)
            if last_stage >= 4:
                mha_scalar(act, 1)
            if last_stage >= 5:
                route_scalar(act, 5)
                expert_tiles_scalar(act)
            if last_stage >= 6:
                single_context_scalar(act)
                single_scalar(act)
            if last_stage >= 7:
                route_scalar(act, 7)
                shared_scalar(act, range(G - 1))
                quads_scalar(act)
                shared_scalar(act, range(G - 1, G))

        @block.vector
        def _(dve):
            ch = Chain(dve, dve_step)
            dve.wait_ge(x_loaded, 16)
            for g in range(0, G, 2):
                together(*(layer_norm_parts(dve, ch, 0, g + k) for k in range(2)))
            context_slots_vector(dve)
            slot_iterations_vector(dve)
            unpack_ternary_vector(dve)
            finish_slots_vector(dve, ch)
            ternary_vector(dve, ch)
            if last_stage >= 2:
                mha_context_vector(dve, ch, 0)
                mha_vector(dve, ch, 0)
            if last_stage >= 4:
                mha_context_vector(dve, ch, 1)
            if last_stage >= 3:
                tri_vector(dve, ch)
            if last_stage >= 4:
                mha_vector(dve, ch, 1)
            if last_stage >= 5:
                route_vector(dve, ch, 5, br5)
                expert_tiles_vector(dve)
            if last_stage >= 6:
                single_context_vector(dve, ch)
                single_vector(dve, ch)
            if last_stage >= 7:
                route_vector(dve, ch, 7, br7)
                shares_vector(dve, ch)
                shared_vector(dve, ch, range(G - 1))
                quads_vector(dve)
                shared_vector(dve, ch, range(G - 1, G))
                combine7_vector(dve, ch)


LAST = 7


def kernel(**inputs):
    import numpy as np
    import concourse.bacc as bacc
    from concourse.bass_utils import run_bass_kernel_spmd

    a = {k: np.ascontiguousarray(v) for k, v in inputs.items()}
    columns = lambda *v: np.ascontiguousarray(np.stack([w.reshape(-1, P).T for w in v], 1).reshape(P, -1))
    T_ = lambda w: np.ascontiguousarray(w.T)
    bih, bhh = a["L0_xattn_gru_bih"].reshape(3, D), a["L0_xattn_gru_bhh"].reshape(3, D)
    lay = {
        "x": a["x"].reshape(B * S, D),
        "ctxT": T_(a["ctx_1024"].reshape(BM, D)),
        "gains": np.concatenate([a["g_xattn"], a["g_ffn"]]),
        "wq0": a["L0_xattn_Wq"], "wk0": T_(a["L0_xattn_Wk"]), "wv0": T_(a["L0_xattn_Wv"]),
        "wih": T_(a["L0_xattn_gru_wih"]), "whh": T_(a["L0_xattn_gru_whh"]),
        "vec0": columns(*bih, *bhh, a["L0_xattn_slot_norm_w"], a["L0_xattn_input_norm_w"]),
    }
    lay |= {
        "packed": T_(a["L0_ffn_packed_weight"].reshape(D // 4, D)),
        "wscale": a["L0_ffn_weight_scale"], "row1": a["L0_ffn_bias"],
        "row2": a["L1_xattn_bo"], "row4": a["L2_xattn_bo"], "row6": a["L3_xattn_bv"], "row3": a["L1_ffn_bias"],
        "tri_wT": T_(a["L1_ffn_weight"]), "tri_a1T": T_(a["L1_ffn_aux_weight1"]), "tri_a2": a["L1_ffn_aux_weight2"],
        "wq1": a["L1_xattn_wq"], "wk1": a["L1_xattn_wk"], "wv1": a["L1_xattn_wv"], "wo1": a["L1_xattn_wo"],
        "wq2": T_(a["L2_xattn_Wq"]), "wk2": T_(a["L2_xattn_Wk"]), "wv2": T_(a["L2_xattn_Wv"]), "wo2": T_(a["L2_xattn_Wo"]),
        "vec1": columns(a["L1_xattn_bq"], a["L1_xattn_bk"], a["L1_xattn_bv"], a["L1_xattn_bv"]),
        "vec2": columns(a["L2_xattn_bq"], a["L2_xattn_bk"], a["L2_xattn_bv"], a["L2_xattn_bv"]),
    }
    lay |= {
        "W1": T_(a["L2_ffn_W1"].reshape(E2 * F2, D)).reshape(D, E2, F2).transpose(1, 0, 2).reshape(E2 * D, F2),
        "W2": a["L2_ffn_W2"].transpose(0, 2, 1).reshape(E2 * F2, D),
        "b1": T_(a["L2_ffn_b1"].reshape(-1, P)), "b2": a["L2_ffn_b2"].reshape(-1),
        "wr5": T_(a["L2_ffn_Wr"]), "br5": a["L2_ffn_br"],
    }
    lay |= {
        "wk6": a["L3_xattn_Wk"], "wv6": a["L3_xattn_Wv"], "wq6": T_(a["L3_xattn_Wq"]),
        "vec6": columns(a["L3_xattn_bq"], a["L3_xattn_bk"]),
    }
    lay |= {
        "gate_up": np.concatenate([a["L3_ffn_gate_w"].transpose(0, 2, 1), a["L3_ffn_up_w"].transpose(0, 2, 1)], 2).reshape(E4 * D, 2 * F4),
        "down": a["L3_ffn_down_w"].transpose(0, 2, 1).reshape(E4 * F4, D),
        "wr7": T_(a["L3_ffn_router_w"]), "br7": a["L3_ffn_router_bias"],
        "sgate": T_(a["L3_ffn_sgate_w"]), "sup": T_(a["L3_ffn_sup_w"]), "sdown": T_(a["L3_ffn_sdown_w"]),
    }
    lay = {k: np.ascontiguousarray(v) for k, v in lay.items()}
    nc = bacc.Bacc("TRN2", target_bir_lowering=False, num_devices=1)
    d = {k: nc.dram_tensor(f"in_{k}", v.shape, mybir.dt.from_np(v.dtype), kind="ExternalInput").ap() for k, v in lay.items()}
    out = nc.dram_tensor("out_x", (B * S, D), F32, kind="ExternalOutput").ap()
    build(nc, d, out, LAST)
    r = run_bass_kernel_spmd(nc, [{f"in_{k}": v for k, v in lay.items()}], core_ids=[0])
    return r.results[0]["out_x"].reshape(B, S, D)
```
